# Optimizing a Trainium2 kernel written in Bass

```python
import numpy as np
import jax
import jax.numpy as jnp

def _softmax(x, axis=-1):
    return jax.nn.softmax(x, axis=axis)

def _gelu(x):
    return jax.nn.gelu(x, approximate=True)

def _silu(x):
    return jax.nn.silu(x)

def _sigmoid(x):
    return jax.nn.sigmoid(x)

def _layernorm(x, axis=-1, eps=1e-05):
    m = jnp.mean(x, axis=axis, keepdims=True)
    v = jnp.var(x, axis=axis, keepdims=True)
    return (x - m) / jnp.sqrt(v + eps)

def _scatter_add(tgt, idx, src, axis=0):
    return tgt.at[idx].add(src)

def _segment_sum(src, seg, n):
    return jax.ops.segment_sum(src, seg, n)
kernel_name = 'mk_adj_ffn_d2_adj_r2_804e43'

def setup_inputs(seed: int=0):
    np.random.seed(seed)
    _w = jnp.asarray

    def _rec_inputs():
        import jax
        import jax.numpy as jnp
        _gk = jax.random.key(seed)
        x = -0.0005207 + 1.001 * jax.random.normal(jax.random.fold_in(_gk, 1), (16, 512, 128), jnp.float32)
        _w = (1.0 + jnp.arange(512, dtype=jnp.float32)) ** (-0.5)
        _w = _w / _w.mean()
        _pij = jnp.clip(0.015625 * _w[:, None] * _w[None, :], 0.0, 1.0)
        _a = jax.random.uniform(jax.random.fold_in(_gk, 2), (16, 512, 512)) < _pij
        _af = _a.astype(jnp.float32)
        adj = _af
        return (x, adj)
    x, adj = _rec_inputs()

    def _L0_gnn_setup():
        import jax, jax.numpy as jnp
        import numpy as np
        B, N, IN_F, OUT_F = (2, 2048, 128, 128)
        ALPHA = 0.2
        MASK_NEG = -9000000000000000.0
        SINK_NEG = -1000000000.0
        key = jax.random.key(seed)
        kx, kadj, kw, kbw, kai, kbi, kaj, kbj = jax.random.split(key, 8)
        x = jax.random.normal(kx, (B, N, IN_F), dtype=jnp.float32)
        adjs = (jax.random.uniform(kadj, (B, N, N)) < 0.01).astype(jnp.float32)

        def xavier(k, shape, gain=1.414):
            fan_out, fan_in = shape
            bound = gain * np.sqrt(6.0 / (fan_in + fan_out))
            return jax.random.uniform(k, shape, minval=-bound, maxval=bound, dtype=jnp.float32)
        W = xavier(kw, (OUT_F, IN_F))
        bW = jax.random.uniform(kbw, (OUT_F,), minval=-1 / np.sqrt(IN_F), maxval=1 / np.sqrt(IN_F), dtype=jnp.float32)
        wai = xavier(kai, (1, OUT_F))
        bai = jax.random.uniform(kbi, (1,), minval=-1 / np.sqrt(OUT_F), maxval=1 / np.sqrt(OUT_F), dtype=jnp.float32)
        waj = xavier(kaj, (1, OUT_F))
        baj = jax.random.uniform(kbj, (1,), minval=-1 / np.sqrt(OUT_F), maxval=1 / np.sqrt(OUT_F), dtype=jnp.float32)
        return {'x': x, 'adjs': adjs, 'W': W, 'bW': bW, 'wai': wai, 'bai': bai, 'waj': waj, 'baj': baj}
    _L0_gnn_all = _L0_gnn_setup()
    _L0_gnn_in = {k: v for k, v in _L0_gnn_all.items() if k in ('W', 'bW', 'wai', 'bai', 'waj', 'baj')}
    del _L0_gnn_all

    def _L0_ffn_setup():
        import jax, jax.numpy as jnp
        import numpy as np
        E, D, H, TOP_K = (6, 128, 128, 2)
        ROUTER_H = D // 2
        key = jax.random.key(seed)
        ks = jax.random.split(key, 12)
        s = 1.0 / np.sqrt(D)
        sh = 1.0 / np.sqrt(H)
        sr = 1.0 / np.sqrt(ROUTER_H)
        return {'features': jax.random.normal(ks[0], (8, 2048, D), dtype=jnp.float32), 'router_w1': jax.random.uniform(ks[1], (D, ROUTER_H), jnp.float32, -s, s), 'router_b1': jnp.zeros((ROUTER_H,), jnp.float32), 'router_w2': jax.random.uniform(ks[2], (ROUTER_H, E), jnp.float32, -sr, sr), 'router_b2': jnp.zeros((E,), jnp.float32), 'expert_w1': jax.random.uniform(ks[3], (E, D, H), jnp.float32, -s, s), 'expert_b1': jnp.zeros((E, H), jnp.float32), 'expert_w2': jax.random.uniform(ks[4], (E, H, H), jnp.float32, -sh, sh), 'expert_b2': jnp.zeros((E, H), jnp.float32), 'expert_w3': jax.random.uniform(ks[5], (E, H, D), jnp.float32, -sh, sh), 'expert_b3': jnp.zeros((E, D), jnp.float32)}
    _L0_ffn_all = _L0_ffn_setup()
    _L0_ffn_in = {k: v for k, v in _L0_ffn_all.items() if k in ('router_w1', 'router_b1', 'router_w2', 'router_b2', 'expert_w1', 'expert_b1', 'expert_w2', 'expert_b2', 'expert_w3', 'expert_b3')}
    del _L0_ffn_all

    def _L1_gnn_setup():
        import jax, jax.numpy as jnp
        import numpy as np
        D_IN = 128
        D_HID = 256
        key = jax.random.key(seed)
        k1, k2, k3, k4, k5, k6 = jax.random.split(key, 6)
        x = jax.random.normal(k1, (8, 2048, D_IN), dtype=jnp.float32)
        adj = jax.random.uniform(k2, (8, 2048, 2048), dtype=jnp.float32)
        s1 = 1.0 / np.sqrt(D_IN)
        s2 = 1.0 / np.sqrt(D_HID)
        W1 = jax.random.uniform(k3, (D_IN, D_HID), dtype=jnp.float32, minval=-s1, maxval=s1)
        b1 = jax.random.uniform(k4, (D_HID,), dtype=jnp.float32, minval=-s1, maxval=s1)
        W2 = jax.random.uniform(k5, (D_HID, D_IN), dtype=jnp.float32, minval=-s2, maxval=s2)
        b2 = jax.random.uniform(k6, (D_IN,), dtype=jnp.float32, minval=-s2, maxval=s2)
        eps = jnp.zeros((1,), dtype=jnp.float32)
        return {'x': x, 'adj': adj, 'eps': eps, 'W1': W1, 'b1': b1, 'W2': W2, 'b2': b2}
    _L1_gnn_all = _L1_gnn_setup()
    _L1_gnn_in = {k: v for k, v in _L1_gnn_all.items() if k in ('eps', 'W1', 'b1', 'W2', 'b2')}
    del _L1_gnn_all

    def _L1_ffn_setup():
        import jax, jax.numpy as jnp
        import numpy as np
        E = 8
        K = 2
        D = 128
        H = 256
        DOUT = 128
        EPS = 1e-05
        key = jax.random.key(seed)
        ks = jax.random.split(key, 9)
        s = 0.02
        return {'x': jax.random.normal(ks[0], (4, 4096, D), jnp.float32), 'gamma': 1.0 + 0.05 * jax.random.normal(ks[1], (D,), jnp.float32), 'beta': 0.05 * jax.random.normal(ks[2], (D,), jnp.float32), 'Wr': 0.01 * jax.random.normal(ks[3], (D, E), jnp.float32), 'br': jnp.zeros((E,), jnp.float32), 'W1': s * jax.random.normal(ks[4], (E, D, H), jnp.float32), 'b1': s * jax.random.normal(ks[5], (E, H), jnp.float32), 'W2': s * jax.random.normal(ks[6], (E, H, DOUT), jnp.float32), 'b2': s * jax.random.normal(ks[7], (E, DOUT), jnp.float32)}
    _L1_ffn_all = _L1_ffn_setup()
    _L1_ffn_in = {k: v for k, v in _L1_ffn_all.items() if k in ('gamma', 'beta', 'Wr', 'br', 'W1', 'b1', 'W2', 'b2')}
    del _L1_ffn_all
    return {'x': x, 'adj': adj, 'L0_gnn_W': _L0_gnn_in['W'], 'L0_gnn_bW': _L0_gnn_in['bW'], 'L0_gnn_wai': _L0_gnn_in['wai'], 'L0_gnn_bai': _L0_gnn_in['bai'], 'L0_gnn_waj': _L0_gnn_in['waj'], 'L0_gnn_baj': _L0_gnn_in['baj'], 'L0_ffn_router_w1': _L0_ffn_in['router_w1'], 'L0_ffn_router_b1': _L0_ffn_in['router_b1'], 'L0_ffn_router_w2': _L0_ffn_in['router_w2'], 'L0_ffn_router_b2': _L0_ffn_in['router_b2'], 'L0_ffn_expert_w1': _L0_ffn_in['expert_w1'], 'L0_ffn_expert_b1': _L0_ffn_in['expert_b1'], 'L0_ffn_expert_w2': _L0_ffn_in['expert_w2'], 'L0_ffn_expert_b2': _L0_ffn_in['expert_b2'], 'L0_ffn_expert_w3': _L0_ffn_in['expert_w3'], 'L0_ffn_expert_b3': _L0_ffn_in['expert_b3'], 'L1_gnn_eps': _L1_gnn_in['eps'], 'L1_gnn_W1': _L1_gnn_in['W1'], 'L1_gnn_b1': _L1_gnn_in['b1'], 'L1_gnn_W2': _L1_gnn_in['W2'], 'L1_gnn_b2': _L1_gnn_in['b2'], 'L1_ffn_gamma': _L1_ffn_in['gamma'], 'L1_ffn_beta': _L1_ffn_in['beta'], 'L1_ffn_Wr': _L1_ffn_in['Wr'], 'L1_ffn_br': _L1_ffn_in['br'], 'L1_ffn_W1': _L1_ffn_in['W1'], 'L1_ffn_b1': _L1_ffn_in['b1'], 'L1_ffn_W2': _L1_ffn_in['W2'], 'L1_ffn_b2': _L1_ffn_in['b2']}

def reference(x, adj, L0_gnn_W, L0_gnn_bW, L0_gnn_wai, L0_gnn_bai, L0_gnn_waj, L0_gnn_baj, L0_ffn_router_w1, L0_ffn_router_b1, L0_ffn_router_w2, L0_ffn_router_b2, L0_ffn_expert_w1, L0_ffn_expert_b1, L0_ffn_expert_w2, L0_ffn_expert_b2, L0_ffn_expert_w3, L0_ffn_expert_b3, L1_gnn_eps, L1_gnn_W1, L1_gnn_b1, L1_gnn_W2, L1_gnn_b2, L1_ffn_gamma, L1_ffn_beta, L1_ffn_Wr, L1_ffn_br, L1_ffn_W1, L1_ffn_b1, L1_ffn_W2, L1_ffn_b2):
    import jax
    import jax.numpy as jnp

    def _L0_gnn_ref(x, adjs, W, bW, wai, bai, waj, baj):
        import jax, jax.numpy as jnp
        import numpy as np
        B, N, IN_F, OUT_F = (2, 2048, 128, 128)
        ALPHA = 0.2
        MASK_NEG = -9000000000000000.0
        SINK_NEG = -1000000000.0
        b, n, _ = adjs.shape
        z = jnp.einsum('bni,oi->bno', x, W) + bW
        ai = jnp.einsum('bno,ko->bnk', z, wai) + bai
        aj = jnp.einsum('bno,ko->bnk', z, waj) + baj
        e = ai + jnp.swapaxes(aj, 1, 2)
        e = jnp.where(e >= 0, e, ALPHA * e)
        att = jnp.where(adjs > 0, e, MASK_NEG)
        sink = jnp.full((b, n, 1), SINK_NEG, dtype=att.dtype)
        att = jax.nn.softmax(jnp.concatenate([att, sink], axis=-1), axis=-1)[:, :, :n]
        return jnp.einsum('bnm,bmo->bno', att, z)

    def _L0_ffn_ref(features, router_w1, router_b1, router_w2, router_b2, expert_w1, expert_b1, expert_w2, expert_b2, expert_w3, expert_b3):
        import jax, jax.numpy as jnp
        import numpy as np
        E, D, H, TOP_K = (6, 128, 128, 2)
        ROUTER_H = D // 2
        rh = jax.nn.relu(features @ router_w1 + router_b1)
        expert_logits = jax.nn.softmax(rh @ router_w2 + router_b2, axis=-1)
        top_w, top_i = jax.lax.top_k(expert_logits, TOP_K)
        routing_weights = jax.nn.softmax(top_w, axis=-1)
        h1 = jax.nn.relu(jnp.einsum('bsd,edh->bseh', features, expert_w1) + expert_b1)
        h2 = jax.nn.relu(jnp.einsum('bseh,ehf->bsef', h1, expert_w2) + expert_b2)
        expert_out = jnp.einsum('bsef,efo->bseo', h2, expert_w3) + expert_b3
        sel = jnp.take_along_axis(expert_out, top_i[:, :, :, None], axis=2)
        combined = jnp.sum(sel * routing_weights[..., None], axis=2)
        return combined

    def _L1_gnn_ref(x, adj, eps, W1, b1, W2, b2):
        import jax, jax.numpy as jnp
        import numpy as np
        D_IN = 128
        D_HID = 256
        aggregated = jnp.einsum('bnm,bmd->bnd', adj, x)
        h = (1.0 + eps) * x + aggregated
        h = jax.nn.relu(h @ W1 + b1)
        return h @ W2 + b2

    def _L1_ffn_ref(x, gamma, beta, Wr, br, W1, b1, W2, b2):
        import jax, jax.numpy as jnp
        import numpy as np
        E = 8
        K = 2
        D = 128
        H = 256
        DOUT = 128
        EPS = 1e-05
        mu = jnp.mean(x, axis=-1, keepdims=True)
        var = jnp.mean(jnp.square(x - mu), axis=-1, keepdims=True)
        xn = (x - mu) * jax.lax.rsqrt(var + EPS) * gamma + beta
        logits = jnp.einsum('bsd,de->bse', xn, Wr) + br
        top_vals, top_idx = jax.lax.top_k(logits, K)
        w = jax.nn.softmax(top_vals, axis=-1)
        w_full = jnp.einsum('bsk,bske->bse', w, jax.nn.one_hot(top_idx, E, dtype=w.dtype))
        y = jnp.zeros(x.shape[:-1] + (DOUT,), x.dtype)
        for e in range(E):
            h = jax.nn.gelu(jnp.einsum('bsd,dh->bsh', xn, W1[e]) + b1[e], approximate=False)
            y_e = jnp.einsum('bsh,hd->bsd', h, W2[e]) + b2[e]
            y = y + y_e * w_full[..., e, None]
        return y
    x = x + _L0_gnn_ref(_layernorm(x, axis=-1), adj, L0_gnn_W, L0_gnn_bW, L0_gnn_wai, L0_gnn_bai, L0_gnn_waj, L0_gnn_baj)
    x = x + _L0_ffn_ref(_layernorm(x, axis=-1), L0_ffn_router_w1, L0_ffn_router_b1, L0_ffn_router_w2, L0_ffn_router_b2, L0_ffn_expert_w1, L0_ffn_expert_b1, L0_ffn_expert_w2, L0_ffn_expert_b2, L0_ffn_expert_w3, L0_ffn_expert_b3)
    x = x + _L1_gnn_ref(_layernorm(x, axis=-1), adj, L1_gnn_eps, L1_gnn_W1, L1_gnn_b1, L1_gnn_W2, L1_gnn_b2)
    x = x + _L1_ffn_ref(_layernorm(x, axis=-1), L1_ffn_gamma, L1_ffn_beta, L1_ffn_Wr, L1_ffn_br, L1_ffn_W1, L1_ffn_b1, L1_ffn_W2, L1_ffn_b2)
    return x

_drawn_inputs = setup_inputs


def setup_inputs(seed=0):
    import zlib

    import numpy as np

    out = dict(_drawn_inputs(seed))
    spreads = {'L0_ffn_router_b1': (0.0, 0.1),
     'L0_ffn_router_b2': (0.0, 0.1),
     'L0_ffn_expert_b1': (0.0, 0.8),
     'L0_ffn_expert_b2': (0.0, 0.28),
     'L0_ffn_expert_b3': (0.0, 0.1),
     'L1_ffn_br': (0.0, 0.543)}
    factors = {'L1_gnn_b1': 4.572,
     'L1_ffn_gamma': 8.0,
     'L1_ffn_beta': 8.0,
     'L1_ffn_Wr': 4.028,
     'L1_ffn_W1': 3.593,
     'L1_ffn_b1': 8.0,
     'L1_ffn_W2': 3.598,
     'L1_ffn_b2': 6.866}
    for name, (base, spread) in spreads.items():
        noise = np.random.default_rng([zlib.crc32(name.encode()), seed]).standard_normal(out[name].shape)
        drawn = base * np.exp(spread * noise) if base else spread * noise
        out[name] = jnp.asarray(drawn.astype(out[name].dtype))
    for name, factor in factors.items():
        out[name] = (out[name] * factor).astype(out[name].dtype)
    return out
```

```python
from contextlib import ExitStack

import concourse.bass as bass
from concourse import mybir

F32 = mybir.dt.float32
U32 = mybir.dt.uint32
I32 = mybir.dt.int32
BF16 = mybir.dt.bfloat16
ALU = mybir.AluOpType
ACT = mybir.ActivationFunctionType
AX = mybir.AxisListType

P = 128
G, N, D = 16, 512, 128
NT = N // P
E0 = 6
RH = 64
DH = 256
E1 = 8
SLOPE = 0.2
MASKED = -9.0e15
SINK = -1.0e9
LN_EPS = 1e-5
HE = 256
NODES = G * N
CAP = NODES + P
SPARE = E1 * CAP
ROW = D + 2
PLACE, WEIGHT = D, D + 1
LAG = 5
TILES = 2 * NODES // P + E1
IDLE = E1
UNROLL = 8
PADW = 96


class Bank:

    def __init__(self, tensor, filled, drained, uses):
        self.tensor, self.filled, self.drained, self.uses = tensor, filled, drained, uses

    def wait_free(self, eng, t, use):
        k = self.uses.index(use)
        n = t * len(self.uses) + k
        if isinstance(n, int) and n == 0:
            return
        eng.wait_ge(self.drained, n)

    def wait_read(self, eng, t, use):
        eng.wait_ge(self.drained, t * len(self.uses) + self.uses.index(use) + 1)

    def wait_full(self, eng, t, use):
        eng.wait_ge(self.filled, t * len(self.uses) + self.uses.index(use) + 1)


def build(nc, a, out):
    with ExitStack() as ctx:
        def sb(name, shape, dt=F32):
            return ctx.enter_context(nc.sbuf_tensor(name, shape, dt))

        def sem(name):
            return ctx.enter_context(nc.semaphore(name))

        def bank(name, uses):
            t = ctx.enter_context(nc.psum_tensor(name + "_bank", [P, 512], F32))
            return Bank(t, sem(name + "_filled"), sem(name + "_drained"), uses)

        TA = [bank("ta0", ["xT", "pT0", "pT2", "oT"]), bank("ta1", ["ai", "pT1", "pT3"])]
        AJ = bank("aj", ["aj"])
        ZB = bank("zb", ["z", "o"])
        HB = [bank("hb0", ["adjT0", "adjT2", "route_h"] + [f"h1_{e}" for e in range(E0)]),
              bank("hb1", ["adjT1", "adjT3", "x1T", "logits"] + [f"h2_{e}" for e in range(E0)])]
        OB = bank("ob", ["e0", "e1", "gateT", "e2", "b3", "e3", "e4", "e5"])
        HC = bank("hc", ["agg", "m0", "m1", "out", "x3T", "logits1", "ranks"])

        XT = [TA[0].tensor, TA[1].tensor]
        HX = [AJ.tensor, ZB.tensor]
        HTX = [HB[0].tensor, HB[1].tensor]
        YX = [OB.tensor, HC.tensor]

        tri = sb("tri", [P, P], BF16)
        ones_b = sb("ones_b", [P, P], BF16)
        iota_node = sb("iota_node", [P, NT])
        iota_part = sb("iota_part", [P, 1])
        iota_region = sb("iota_region", [P, E1])
        iota_tile = sb("iota_tile", [1, TILES])
        gamma = sb("gamma", [P, 1])
        beta = sb("beta", [P, 1])
        wr = sb("wr", [P, PADW])
        br_bc = sb("br_bc", [P, E1])
        fw1 = sb("fw1", [P, E1 * HE])
        fw2 = sb("fw2", [P, E1 * HE])
        fb1_bc = sb("fb1_bc", [P, E1 * HE])
        fb2_bc = sb("fb2_bc", [P, E1 * D])
        ident = sb("ident", [P, P])
        eps_ident = sb("eps_ident", [P, P])
        eps_tile = sb("eps_tile", [P, NT])
        minus_half = sb("minus_half", [P, NT])
        iota8 = sb("iota8", [P, 8])
        gW = sb("gW", [P, D])
        gWT = sb("gWT", [P, D])
        bW_bc = sb("bW_bc", [P, D])
        bW_col = sb("bW_col", [P, 1])
        wa_col = sb("wa_col", [P, 2])
        ba_bc = sb("ba_bc", [P, 2])
        u_col = sb("u_col", [P, 2])
        uj_bc = sb("uj_bc", [P, P])
        bwa = sb("bwa", [P, 2])
        c_pair = sb("c_pair", [P, 2])
        c_sum = sb("c_sum", [P, 1])
        c_relu = sb("c_relu", [P, 1])
        c_sink = sb("c_sink", [P, 1])
        ones = sb("ones", [P, P])
        rw1 = sb("rw1", [P, RH])
        rb1 = sb("rb1", [RH, 1])
        rw2 = sb("rw2", [RH, PADW])
        rb2_bc = sb("rb2_bc", [P, E0])
        ew = [sb(f"ew{i}", [P, E0, D]) for i in (1, 2, 3)]
        eb1 = sb("eb1", [P, E0])
        eb2 = sb("eb2", [P, E0])
        eb3 = sb("eb3", [E0, D])
        eps_bc = sb("eps_bc", [P, 1])
        mw1 = sb("mw1", [P, DH])
        mb1 = sb("mb1", [P, 2])
        mw2 = sb("mw2", [P, 2, D])
        mb2_bc = sb("mb2_bc", [P, D])

        adj = [sb(f"adj{i}", [P, NT, N]) for i in range(2)]
        x0 = [sb(f"x0_{i}", [P, NT, D]) for i in range(2)]
        bn = {s: sb(f"bn_{s}", [P, NT, 6]) for s in "ABCDE"}
        mv = {s: sb(f"mv_{s}", [P, NT, 2]) for s in "ABCDE"}
        var_eps = {s: sb(f"ve_{s}", [P, NT]) for s in "ABCDE"}
        rstd = {s: sb(f"rstd_{s}", [P, NT]) for s in "ABCDE"}
        xn = sb("xn", [P, NT, D])
        xnT = sb("xnT", [P, N])
        z = sb("z", [P, NT, D])
        relu_bias = sb("relu_bias", [P, NT])
        sink = sb("sink", [P, NT])
        aj02 = sb("aj02", [P, N])
        pen = sb("pen", [P, NT, N])
        att = sb("att", [P, NT, N])
        row_max = sb("row_max", [P, NT])
        top = sb("top", [P, NT])
        neg_max = sb("neg_max", [P, NT])
        sink_arg = sb("sink_arg", [P, NT])
        sink_exp = sb("sink_exp", [P, NT])
        row_sum = sb("row_sum", [P, NT])
        den = sb("den", [P, NT])
        rden = sb("rden", [P, NT])
        pT = sb("pT", [P, NT, N])
        oT = sb("oT", [P, N])
        x1 = [sb(f"x1_{i}", [P, NT, D]) for i in range(2)]
        x1n = sb("x1n", [P, NT, D])
        x1nT = sb("x1nT", [P, N])
        adjT = [sb(f"adjT{i}", [P, NT, N]) for i in range(2)]
        rh = sb("rh", [RH, N])
        lg = sb("lg", [P, NT, E0])
        lg_max = sb("lg_max", [P, NT])
        lg_sum = sb("lg_sum", [P, NT])
        lg_rsum = sb("lg_rsum", [P, NT])
        prob = sb("prob", [P, NT, 8])
        best, best_i, best_f, wgap, wexp, wden, w01, hot = ({} for _ in range(8))
        for r in "BD":
            best[r] = sb(f"best_{r}", [P, NT, 8])
            best_i[r] = sb(f"best_i_{r}", [P, NT, 8], U32)
            best_f[r] = sb(f"best_f_{r}", [P, 2, NT])
            wgap[r] = sb(f"wgap_{r}", [P, NT])
            wexp[r] = sb(f"wexp_{r}", [P, NT])
            wden[r] = sb(f"wden_{r}", [P, NT])
            w01[r] = sb(f"w01_{r}", [P, 2, NT])
            hot[r] = sb(f"hot_{r}", [P, 2, NT, 8])
        hotw = sb("hotw", [P, 2, NT, 8])
        gate = sb("gate", [P, NT, 8])
        gateT = sb("gateT", [8, N])
        h1 = [sb(f"h1_{i}", [P, N]) for i in range(2)]
        h2 = [sb(f"h2_{i}", [P, N]) for i in range(2)]
        x2 = [sb(f"x2_{i}", [P, NT, D]) for i in range(2)]
        x2n = [sb(f"x2n_{i}", [P, NT, D]) for i in range(2)]
        x2b = sb("x2b", [P, NT, D])
        hT = sb("hT", [P, N])
        m1 = sb("m1", [P, 2, N])
        x3 = sb("x3", [P, G, NT, D])
        x3n = sb("x3n", [P, NT, D])
        rows = [sb(f"rows{k}", [P, NT, ROW]) for k in range(2)]
        x3T = sb("x3T", [P, N])
        logits1 = sb("logits1", [P, NT, 8])
        chosen = sb("chosen", [P, NT, 8])
        earlier = sb("earlier", [P, NT + 1, 8], BF16)
        chosen_b = sb("chosen_b", [P, NT, 8], BF16)
        earlier_f = sb("earlier_f", [P, NT + 1, 8])
        base = sb("base", [P, E1])
        slot_of = sb("slot_of", [P, NT, 8])
        slot_hot = sb("slot_hot", [P, 2, NT, 8])
        slot_f = sb("slot_f", [P, 2, NT])
        slot = sb("slot", [P, 2, NT], U32)
        place = sb("place", [P, 2, NT])
        spare_rows, idle_rows = (
            b[:].rearrange("p j m -> p (j m)")[:, 0:E1 * ROW].rearrange("p (e r) -> p e r", r=ROW)
            for b in adj)
        spare_f = sb("spare_f", [P, E1])
        spare = sb("spare", [P, E1], U32)
        count = sb("count", [1, E1])
        count_i = sb("count_i", [1, E1], I32)
        tiles_i = sb("tiles_i", [1, E1], I32)
        tiles = sb("tiles", [1, E1])
        ends = [sb(f"ends{i}", [1, E1]) for i in range(4)]
        passed, behind = (b[0:1, :, :].rearrange("p j m -> p (j m)")[:, 0:TILES * E1].rearrange(
            "p (t e) -> p t e", e=E1) for b in (pen, att))
        expert_f = sb("expert_f", [1, TILES])
        first = sb("first", [1, TILES])
        inside = sb("inside", [1, TILES])
        row0_f = sb("row0_f", [1, TILES])
        expert_m = sb("expert_m", [1, TILES])
        expert_of = sb("expert_of", [1, TILES], I32)
        row0_of = sb("row0_of", [1, TILES], I32)
        tile_rows = [sb(f"tile_rows{i}", [P, ROW]) for i in range(UNROLL)]
        hb, hg, hgT = ([pT[:, k, i * HE:(i + 1) * HE] for i in range(2)] for k in range(3))
        xg, yb = ([pT[:, 3, (k + i) * P:(k + i + 1) * P] for i in range(2)] for k in (0, 2))
        yw = [att[:, i // NT, i % NT * D:(i % NT + 1) * D] for i in range(UNROLL)]
        pair = [b[:, 0:2, :].rearrange("p a (b d) -> p (a b) d", d=2 * D) for b in adj]
        fin = [b[:, 0, :].rearrange("p (j d) -> p j d", d=D) for b in adjT]
        sent = nc.dram_tensor("sent", (E1 * CAP + IDLE * P, ROW), F32, kind="Internal").ap()
        result2 = nc.dram_tensor("result2", (2 * NODES + (E1 + IDLE) * P, D), F32, kind="Internal").ap()

        S = {}

        def ready(name):
            if name not in S:
                S[name] = sem(name)
            return S[name]

        adj_loaded = [sem(f"adj_loaded{i}") for i in range(2)]
        x0_loaded = [sem(f"x0_loaded{i}") for i in range(2)]
        weights_loaded = sem("weights_loaded")
        rows_sent = sem("rows_sent")
        spare_sent = sem("spare_sent")
        tile_loaded = [sem(f"tile_loaded{i}") for i in range(UNROLL)]
        result_sent = [sem(f"result_sent{i}") for i in range(UNROLL)]
        pair_loaded = [sem(f"pair_loaded{i}") for i in range(2)]
        out_stored = [sem(f"out_stored{i}") for i in range(2)]

        x_d = a["x"].rearrange("g (j p) d -> g p j d", p=P)
        adj_d = a["adj"].rearrange("g (j p) m -> g p j m", p=P)
        out_d = out.rearrange("g (j p) d -> g p j d", p=P)

        def col(ap):
            return ap.rearrange("(p a) -> p a", a=1)

        loads = [
            (gW[:], a["L0_gnn_W"]),
            (bW_bc[:], a["L0_gnn_bW"].partition_broadcast(P)),
            (bW_col[:], col(a["L0_gnn_bW"])),
            (wa_col[:, 0:1], a["L0_gnn_wai"].rearrange("a p -> p a")),
            (wa_col[:, 1:2], a["L0_gnn_waj"].rearrange("a p -> p a")),
            (ba_bc[:, 0:1], a["L0_gnn_bai"].partition_broadcast(P)),
            (ba_bc[:, 1:2], a["L0_gnn_baj"].partition_broadcast(P)),
            (rw1[:], a["L0_ffn_router_w1"]),
            (rb1[:], col(a["L0_ffn_router_b1"])),
            (rw2[:, 0:E0], a["L0_ffn_router_w2"]),
            (rb2_bc[:], a["L0_ffn_router_b2"].partition_broadcast(P)),
            (ew[0][:], a["L0_ffn_expert_w1"].rearrange("e d h -> d e h")),
            (ew[1][:], a["L0_ffn_expert_w2"].rearrange("e d h -> d e h")),
            (ew[2][:], a["L0_ffn_expert_w3"].rearrange("e d h -> d e h")),
            (eb1[:], a["L0_ffn_expert_b1"].rearrange("e h -> h e")),
            (eb2[:], a["L0_ffn_expert_b2"].rearrange("e h -> h e")),
            (eb3[:], a["L0_ffn_expert_b3"]),
            (eps_bc[:], a["L1_gnn_eps"].partition_broadcast(P)),
            (mw1[:], a["L1_gnn_W1"]),
            (mb1[:], a["L1_gnn_b1"].rearrange("(c p) -> p c", p=P)),
            (mw2[:], a["L1_gnn_W2"].rearrange("(c p) d -> p c d", p=P)),
            (mb2_bc[:], a["L1_gnn_b2"].partition_broadcast(P)),
            (gamma[:], col(a["L1_ffn_gamma"])),
            (beta[:], col(a["L1_ffn_beta"])),
            (wr[:, 0:E1], a["L1_ffn_Wr"]),
            (br_bc[:], a["L1_ffn_br"].partition_broadcast(P)),
            (fw1[:].rearrange("p (e h) -> p e h", e=E1), a["L1_ffn_W1"].rearrange("e d h -> d e h")),
            (fw2[:].rearrange("p (e c d) -> p e c d", e=E1, c=2),
             a["L1_ffn_W2"].rearrange("e (c p) d -> p e c d", p=P)),
            (fb1_bc[:], a["L1_ffn_b1"].rearrange("e h -> (e h)").partition_broadcast(P)),
            (fb2_bc[:], a["L1_ffn_b2"].rearrange("e h -> (e h)").partition_broadcast(P)),
        ]
        WEIGHTS = 16 * len(loads)
        POOL_CONSTANTS = 16

        def iterations(eng, step):
            step(0, None, None, 0)
            step(1, 0, None, 1)
            step(2, 1, 0, 0)
            step(3, 2, 1, 1)
            with eng.Fori(1, (G - 2) // 2) as i:
                step(2 * i + 2, 2 * i + 1, 2 * i, 0)
                step(2 * i + 3, 2 * i + 2, 2 * i + 1, 1)
            step(None, G - 1, G - 2, 0)
            step(None, None, G - 1, 1)

        def wait(eng, name, t, per=1, k=0):
            eng.wait_ge(ready(name), t * per + k + 1)

        def wait_before(eng, name, t, per=1):
            if not (isinstance(t, int) and t == 0):
                eng.wait_ge(ready(name), t * per)

        def bc(ap, axis, n):
            shape = list(ap.shape)
            shape.insert(axis, n)
            return ap.unsqueeze(axis).broadcast_to(shape)

        def apart(eng):
            eng.nop(nofuse=True)

        def slots(eng, slot):
            for s in range(2 * UNROLL):
                slot(s, s % UNROLL)
            with eng.Fori(2, TILES // UNROLL) as r:
                for u in range(UNROLL):
                    slot(UNROLL * r + u, u)
            for s in range(TILES, TILES + LAG):
                slot(s, s % UNROLL)

        def tile_at(s, back):
            if isinstance(s, int) and not 0 <= s - back < TILES:
                return None
            return s - back

        block = ctx.enter_context(nc.Block())

        @block.sync
        def _(sp):
            def load(t, par):
                sp.dma_start(x0[par][:], x_d[t]).then_inc(x0_loaded[par], 16)
                sp.dma_start(adj[par][:], adj_d[t]).then_inc(adj_loaded[par], 16)

            load(0, 0)
            for dst, src in loads:
                sp.dma_start(dst, src, allow_slow_non_contiguous=True).then_inc(weights_loaded, 16)
            load(1, 1)
            with sp.Fori(0, (G - 2) // 2) as i:
                for par in range(2):
                    t = 2 * i + 2 + par
                    TA[0].wait_read(sp, t - 2, "oT")
                    HB[1].wait_full(sp, t - 2, "adjT3")
                    load(t, par)

            sp.wait_ge(ready("table"), 1)
            sp.wait_ge(rows_sent, 16 * 2 * NT * G)
            sp.wait_ge(spare_sent, 16 * (E1 + 1))

            def tile(i, q):
                row0 = sp.value_load(row0_of[0:1, bass.ds(i, 1)], min_val=0,
                                     max_val=SPARE + (IDLE - 1) * P)
                if not (isinstance(i, int) and i < UNROLL):
                    sp.wait_ge(result_sent[q], 16 * (i // UNROLL) if isinstance(i, int)
                               else 16 // UNROLL * (i - q))
                sp.dma_start(tile_rows[q][:], sent[bass.ds(row0, P), :]).then_inc(tile_loaded[q], 16)

            for i in range(UNROLL):
                tile(i, i)
            with sp.Fori(1, TILES // UNROLL) as r:
                for q in range(UNROLL):
                    tile(UNROLL * r + q, q)

            for q in range(UNROLL):
                sp.wait_ge(result_sent[q], 16 * (TILES // UNROLL))
            pairs = result2[0:2 * NODES, :].rearrange("(g j p k) d -> g p j (k d)", j=NT, p=P, k=2)

            def load_pair(g, par):
                sp.dma_start(pair[par], pairs[g]).then_inc(pair_loaded[par], 16)

            def store(g, par):
                wait(sp, "fin", g)
                sp.dma_start(out_d[g], fin[par]).then_inc(out_stored[par], 16)

            load_pair(0, 0)
            load_pair(1, 1)
            with sp.Fori(0, G // 2 - 1) as i:
                for par in range(2):
                    store(2 * i + par, par)
                    load_pair(2 * i + par + 2, par)
            for par in range(2):
                store(G - 2 + par, par)
            for par in range(2):
                sp.wait_ge(out_stored[par], 16 * G // 2)

        @block.gpsimd
        def _(pool):
            g = nc.gpsimd
            g.memset(ident[:], 0.0).then_inc(ready("ident0"), 1)
            g.memset(minus_half[:], -0.5).then_inc(ready("pool_const"), 1)
            g.memset(ones[:], 1.0).then_inc(ready("pool_const"), 1)
            g.memset(prob[:], -1.0).then_inc(ready("pool_const"), 1)
            g.iota(iota8[:], pattern=[[1, 8]], base=0, channel_multiplier=0,
                   allow_small_or_imprecise_dtypes=True).then_inc(ready("pool_const"), 1)
            g.memset(tri[:], 1.0).then_inc(ready("ident0"), 1)
            g.memset(ones_b[:], 1.0).then_inc(ready("pool_const"), 1)
            g.memset(eps_tile[:], LN_EPS).then_inc(ready("pool_const"), 1)
            g.memset(rw2[:, E0:PADW], 0.0).then_inc(ready("pool_const"), 1)
            g.memset(wr[:, E1:PADW], 0.0).then_inc(ready("pool_const"), 1)
            for dst, pattern, start, by_partition in (
                    (iota_node[:], [[2 * P, NT]], 0, 2), (iota_part[:], [[1, 1]], 0, 1),
                    (iota_region[:], [[CAP, E1]], 0, 0), (place[:, 0, :], [[2 * P, NT]], 0, 2),
                    (place[:, 1, :], [[2 * P, NT]], 1, 2), (base[:], [[CAP, E1]], 0, 0),
                    (iota_tile[:], [[1, TILES]], 0, 0)):
                g.iota(dst, pattern=pattern, base=start, channel_multiplier=by_partition,
                       allow_small_or_imprecise_dtypes=True).then_inc(ready("pool_const"), 1)
            pool.wait_ge(ready("ident0"), 2)
            g.affine_select(out=tri[:], in_=tri[:], compare_op=ALU.is_gt, fill=0.0, base=0,
                            pattern=[[1, P]], channel_multiplier=-1).then_inc(ready("pool_const"), 1)
            g.affine_select(out=ident[:], in_=ident[:], compare_op=ALU.not_equal, fill=1.0, base=0,
                            pattern=[[-1, P]], channel_multiplier=1).then_inc(ready("ident"), 1)
            pool.wait_ge(ready("pool_const"), POOL_CONSTANTS)
            pool.wait_ge(weights_loaded, WEIGHTS)

            def inverse_std(s, t):
                wait(pool, f"stats_{s}", t)
                g.tensor_tensor(var_eps[s][:], mv[s][:, :, 1], eps_tile[:], ALU.add).then_inc(
                    ready(f"var_eps_{s}"), 1)
                wait(pool, f"var_eps_{s}", t)
                g.tensor_tensor(rstd[s][:], var_eps[s][:], minus_half[:], ALU.pow).then_inc(
                    ready(f"rstd_{s}"), 1)

            def step(tA, tB, tC, par):
                if tA is not None:
                    inverse_std("A", tA)
                if tC is not None:
                    OB.wait_read(pool, tC, "e5")
                    HC.wait_free(pool, tC, "agg")
                    for j in range(NT):
                        last = g.tensor_tensor(x2b[:, j, :], x2[par][:, j, :], mb2_bc[:], ALU.add)
                    last.then_inc(ready("x2b"), 1)
                if tA is not None:
                    wait(pool, "pen", tA)
                    wait(pool, "aj02", tA)
                    for j in range(NT):
                        g.tensor_tensor(pen[:, j, :], pen[:, j, :], aj02[:], ALU.add).then_inc(
                            ready("pen_aj"), 1)
                if tC is not None:
                    inverse_std("D", tC)
                    inverse_std("E", tC)
                if tB is not None:
                    inverse_std("C", tB)
                if tA is not None:
                    inverse_std("B", tA)
                if tC is not None:
                    wait(pool, "slot", tC)
                    wait(pool, "rows_ready", tC)
                    apart(pool)
                    for k in range(2):
                        for j in range(NT):
                            g.indirect_dma_start(sent, bass.IndirectOffsetOnAxis(slot[:, k, j:j + 1], 0),
                                                 rows[k][:, j, :], None).then_inc(rows_sent, 16)

            iterations(pool, step)

            HB[1].wait_full(pool, G - 1, "adjT3")
            for n, buffer in enumerate((spare_rows, idle_rows)):
                g.memset(buffer, 0.0).then_inc(ready("filling0"), 1)
                pool.wait_ge(ready("filling0"), n + 1)
                g.iota(buffer[:, :, PLACE].bitcast(U32), pattern=[[P, E1]],
                       base=2 * NODES + n * E1 * P, channel_multiplier=1).then_inc(ready("filling"), 1)
            pool.wait_ge(ready("filling"), 2)
            g.dma_start(sent[SPARE:SPARE + IDLE * P, :].rearrange("(i p) r -> p i r", p=P),
                        idle_rows).then_inc(spare_sent, 16)
            pool.wait_ge(ready("spare"), 1)
            for e in range(E1):
                g.indirect_dma_start(sent, bass.IndirectOffsetOnAxis(spare[:, e:e + 1], 0),
                                     spare_rows[:, e, :], None).then_inc(spare_sent, 16)

            def send_slot(s, u):
                i = tile_at(s, LAG)
                if i is None:
                    return
                q = (u - LAG) % UNROLL
                wait(pool, "tile_yw", i)
                apart(pool)
                g.indirect_dma_start(
                    result2, bass.IndirectOffsetOnAxis(tile_rows[q][:, PLACE:PLACE + 1].bitcast(U32), 0),
                    yw[q], None).then_inc(result_sent[q], 16)

            slots(pool, send_slot)

        @block.scalar
        def _(act):
            s = nc.scalar
            act.wait_ge(weights_loaded, WEIGHTS)

            def drain(bk, t, use, dst, func=ACT.Copy, src=None, **kw):
                bk.wait_full(act, t, use)
                s.activation(dst, bk.tensor[:] if src is None else src, func, **kw).then_inc(
                    bk.drained, 1)

            def hidden1(t, e):
                drain(HB[0], t, f"h1_{e}", h1[e % 2][:], ACT.Relu, bias=eb1[:, e:e + 1])

            def hidden2(t, e):
                drain(HB[1], t, f"h2_{e}", h2[e % 2][:], ACT.Relu, bias=eb2[:, e:e + 1])

            def step(tA, tB, tC, par):
                if tB is not None:
                    for k in range(NT):
                        drain(HB[k % 2], tB, f"adjT{k}", adjT[1 - par][:, k, :])
                if tC is not None:
                    drain(HC, tC, "agg", hT[:])
                if tB is not None:
                    drain(HB[1], tB, "x1T", x1nT[:])
                    drain(HB[0], tB, "route_h", rh[:], ACT.Relu, src=HB[0].tensor[0:RH, :], bias=rb1[:])
                if tA is not None:
                    drain(TA[0], tA, "xT", xnT[:])
                if tB is not None:
                    hidden1(tB, 0)
                if tA is not None:
                    AJ.wait_full(act, tA, "aj")
                    wait_before(act, "pen_aj", tA, NT)
                    s.activation(aj02[:], AJ.tensor[:], ACT.Copy, scale=SLOPE).then_inc(ready("aj02"), 1)
                    wait(act, "relu_bias", tA)
                    for j in range(NT):
                        s.activation(att[:, j, :], AJ.tensor[:], ACT.Relu, bias=relu_bias[:, j:j + 1],
                                     scale=1.0 - SLOPE).then_inc(ready("relu"), 1)
                if tC is not None:
                    drain(HC, tC, "m0", m1[:, 0, :], ACT.Relu, bias=mb1[:, 0:1])
                if tB is not None:
                    wait(act, "lg_centred", tB)
                    s.activation(prob[:, :, 0:E0], lg[:], ACT.Exp).then_inc(ready("lg_exp"), 1)
                    hidden1(tB, 1)
                    hidden2(tB, 0)
                if tC is not None:
                    drain(HC, tC, "m1", m1[:, 1, :], ACT.Relu, bias=mb1[:, 1:2])
                if tB is not None:
                    hidden1(tB, 2)
                    hidden2(tB, 1)
                    wait(act, "wgap_B", tB)
                    s.activation(wexp["B"][:], wgap["B"][:], ACT.Exp).then_inc(ready("wexp_B"), 1)
                    hidden1(tB, 3)
                    hidden2(tB, 2)
                if tA is not None:
                    wait(act, "sink_arg", tA)
                    s.activation(sink_exp[:], sink_arg[:], ACT.Exp).then_inc(ready("sink_exp"), 1)
                    for j in range(NT):
                        s.activation(att[:, j, :], att[:, j, :], ACT.Exp, bias=neg_max[:, j:j + 1],
                                     accum_out=row_sum[:, j:j + 1]).then_inc(ready("edge_exp"), 1)
                if tB is not None:
                    hidden1(tB, 4)
                    hidden2(tB, 3)
                    hidden1(tB, 5)
                    hidden2(tB, 4)
                if tA is not None:
                    drain(TA[1], tA, "pT1", pT[:, 1, :])
                    drain(TA[1], tA, "pT3", pT[:, 3, :])
                if tC is not None:
                    drain(HC, tC, "x3T", x3T[:], ACT.Identity, bias=beta[:], scale=gamma[:])
                    wait(act, "x3n", tC)
                    if not (isinstance(tC, int) and tC == 0):
                        act.wait_ge(rows_sent, 16 * 2 * NT * tC)
                    s.activation(rows[1][:, :, 0:D], rows[0][:, :, 0:D], ACT.Copy).then_inc(
                        ready("row1_features"), 1)
                if tB is not None:
                    hidden2(tB, 5)
                if tA is not None:
                    drain(ZB, tA, "o", oT[:])
                if tC is not None:
                    wait(act, "wgap_D", tC)
                    s.activation(wexp["D"][:], wgap["D"][:], ACT.Exp).then_inc(ready("wexp_D"), 1)

            iterations(act, step)

            def tile_slot(s_, u):
                i = tile_at(s_, 0)
                if i is not None:
                    q = u % 2
                    wait(act, "tile_xT", i)
                    if not (isinstance(i, int) and i < 2):
                        wait(act, "tile_h", i - 2)
                    s.activation(xg[q], XT[q][:, 0:P], ACT.Identity, bias=beta[:],
                                 scale=gamma[:]).then_inc(ready("tile_xg"), 1)
                i = tile_at(s_, 2)
                if i is not None:
                    q = u % 2
                    wait(act, "tile_hb", i)
                    if not (isinstance(i, int) and i < 2):
                        wait(act, "tile_hT", i - 2)
                    s.activation(hg[q], hb[q], ACT.Gelu).then_inc(ready("tile_hg"), 1)
                i = tile_at(s_, 5)
                if i is not None:
                    q = (u - 5) % UNROLL
                    wait(act, "tile_yb", i)
                    if not (isinstance(i, int) and i < UNROLL):
                        act.wait_ge(result_sent[q], 16 * (i // UNROLL) if isinstance(i, int)
                                    else 16 // UNROLL * (i - q))
                    s.activation(yw[q], yb[q % 2], ACT.Copy,
                                 scale=tile_rows[q][:, WEIGHT:WEIGHT + 1]).then_inc(ready("tile_yw"), 1)

            slots(act, tile_slot)

        @block.tensor
        def _(pe):
            m = nc.tensor

            pe.wait_ge(ready("ident"), 1)
            pe.wait_ge(ready("pool_const"), POOL_CONSTANTS)
            pe.wait_ge(weights_loaded, WEIGHTS)
            m.transpose(HC.tensor[:, 0:D], gW[:], ident[:])
            m.matmul(HC.tensor[:, D:D + 2], gW[:], wa_col[:], start=True, stop=True).then_inc(
                ready("setup1"), 1)
            pe.wait_ge(ready("bwa"), 1)
            m.matmul(AJ.tensor[:, 0:2], ones[:], bwa[:], start=True, stop=True).then_inc(
                ready("setup2"), 1)
            pe.wait_ge(ready("setup_done"), 1)

            def transposes(bk, t, use, blocks):
                bk.wait_free(pe, t, use)
                for j, src in enumerate(blocks):
                    last = m.transpose(bk.tensor[:, j * P:(j + 1) * P], src, ident[:])
                last.then_inc(bk.filled, 1)

            def product(bk, t, use, lhsT, rhs):
                bk.wait_free(pe, t, use)
                m.matmul(bk.tensor[0:lhsT.shape[1], :], lhsT, rhs, start=True, stop=True).then_inc(
                    bk.filled, 1)

            def layer1(t, e):
                product(HB[0], t, f"h1_{e}", ew[0][:, e, :], x1nT[:])

            def layer2(t, e):
                HB[0].wait_read(pe, t, f"h1_{e}")
                product(HB[1], t, f"h2_{e}", ew[1][:, e, :], h1[e % 2][:])

            def layer3(t, e):
                OB.wait_free(pe, t, f"e{e}")
                HB[1].wait_read(pe, t, f"h2_{e}")
                for j in range(NT):
                    last = m.matmul(OB.tensor[:, j * P:(j + 1) * P], h2[e % 2][:, j * P:(j + 1) * P],
                                    ew[2][:, e, :], start=True, stop=True)
                last.then_inc(OB.filled, 1)

            def probT(t, k):
                if k == 0:
                    wait(pe, "edge_exp", t, NT, NT - 1)
                transposes(TA[k % 2], t, f"pT{k}", [att[:, j, k * P:(k + 1) * P] for j in range(NT)])

            def step(tA, tB, tC, par):
                if tB is not None:
                    for k in range(NT):
                        transposes(HB[k % 2], tB, f"adjT{k}",
                                   [adj[1 - par][:, j, k * P:(k + 1) * P] for j in range(NT)])
                if tC is not None:
                    HC.wait_free(pe, tC, "agg")
                    wait(pe, "x2n", tC)
                    HB[0].wait_read(pe, tC, "adjT2")
                    HB[1].wait_read(pe, tC, "adjT3")
                    for k in range(NT):
                        m.matmul(HC.tensor[:], x2n[par][:, k, :], adjT[par][:, k, :],
                                 start=(k == 0), stop=False)
                        last = m.matmul(HC.tensor[:, k * P:(k + 1) * P], x2n[par][:, k, :],
                                        eps_ident[:], start=False, stop=(k == NT - 1))
                    last.then_inc(HC.filled, 1)
                if tB is not None:
                    wait(pe, "x1n", tB)
                    transposes(HB[1], tB, "x1T", [x1n[:, j, :] for j in range(NT)])
                if tA is not None:
                    wait(pe, "xn", tA)
                    transposes(TA[0], tA, "xT", [xn[:, j, :] for j in range(NT)])
                if tB is not None:
                    HB[1].wait_read(pe, tB, "x1T")
                    product(HB[0], tB, "route_h", rw1[:], x1nT[:])
                    layer1(tB, 0)
                if tA is not None:
                    TA[0].wait_read(pe, tA, "xT")
                    wait_before(pe, "relu", tA, NT)
                    m.matmul(AJ.tensor[:], uj_bc[:], xnT[:], start=True, stop=True).then_inc(
                        AJ.filled, 1)
                    TA[1].wait_free(pe, tA, "ai")
                    for j in range(NT):
                        last = m.matmul(TA[1].tensor[:, j:j + 1], xnT[:, j * P:(j + 1) * P],
                                        u_col[:, 0:1], start=True, stop=True)
                    last.then_inc(TA[1].filled, 1)
                if tB is not None:
                    HB[0].wait_read(pe, tB, "route_h")
                    HB[1].wait_free(pe, tB, "logits")
                    for j in range(NT):
                        last = m.matmul(HB[1].tensor[:, j * PADW:(j + 1) * PADW], rh[:, j * P:(j + 1) * P],
                                        rw2[:], start=True, stop=True)
                    last.then_inc(HB[1].filled, 1)
                if tA is not None:
                    ZB.wait_free(pe, tA, "z")
                    for j in range(NT):
                        last = m.matmul(ZB.tensor[:, j * P:(j + 1) * P], xnT[:, j * P:(j + 1) * P],
                                        gWT[:], start=True, stop=True)
                    last.then_inc(ZB.filled, 1)
                if tC is not None:
                    HC.wait_read(pe, tC, "agg")
                    product(HC, tC, "m0", mw1[:, 0:P], hT[:])
                if tB is not None:
                    layer1(tB, 1)
                    layer2(tB, 0)
                if tC is not None:
                    product(HC, tC, "m1", mw1[:, P:DH], hT[:])
                if tB is not None:
                    layer1(tB, 2)
                    layer2(tB, 1)
                    layer3(tB, 0)
                    layer1(tB, 3)
                    layer2(tB, 2)
                    layer3(tB, 1)
                if tC is not None:
                    HC.wait_free(pe, tC, "out")
                    for j in range(NT):
                        for c in range(2):
                            last = m.matmul(HC.tensor[:, j * P:(j + 1) * P],
                                            m1[:, c, j * P:(j + 1) * P], mw2[:, c, :],
                                            start=(c == 0), stop=(c == 1))
                    last.then_inc(HC.filled, 1)
                if tB is not None:
                    layer1(tB, 4)
                    layer2(tB, 3)
                    OB.wait_free(pe, tB, "gateT")
                    wait(pe, "gate", tB)
                    for j in range(NT):
                        last = m.transpose(OB.tensor[0:8, j * P:(j + 1) * P], gate[:, j, :], ident[:])
                    last.then_inc(OB.filled, 1)
                    layer1(tB, 5)
                    layer3(tB, 2)
                    layer2(tB, 4)
                if tA is not None:
                    probT(tA, 0)
                    probT(tA, 1)
                if tB is not None:
                    OB.wait_free(pe, tB, "b3")
                    for j in range(NT):
                        last = m.matmul(OB.tensor[:, j * P:(j + 1) * P], gateT[0:E0, j * P:(j + 1) * P],
                                        eb3[:], start=True, stop=True)
                    last.then_inc(OB.filled, 1)
                    layer3(tB, 3)
                    layer2(tB, 5)
                if tA is not None:
                    probT(tA, 2)
                    probT(tA, 3)
                if tC is not None:
                    wait(pe, "x3n", tC)
                    transposes(HC, tC, "x3T", [rows[0][:, j, 0:D] for j in range(NT)])
                if tB is not None:
                    layer3(tB, 4)
                if tC is not None:
                    HC.wait_read(pe, tC, "x3T")
                    HC.wait_free(pe, tC, "logits1")
                    for j in range(NT):
                        last = m.matmul(HC.tensor[:, j * PADW:(j + 1) * PADW], x3T[:, j * P:(j + 1) * P],
                                        wr[:], start=True, stop=True)
                    last.then_inc(HC.filled, 1)
                if tA is not None:
                    ZB.wait_read(pe, tA, "z")
                    ZB.wait_free(pe, tA, "o")
                    for k in range(NT):
                        TA[k % 2].wait_read(pe, tA, f"pT{k}")
                        last = m.matmul(ZB.tensor[:], z[:, k, :], pT[:, k, :],
                                        start=(k == 0), stop=(k == NT - 1))
                    last.then_inc(ZB.filled, 1)
                if tB is not None:
                    layer3(tB, 5)
                if tA is not None:
                    ZB.wait_read(pe, tA, "o")
                    transposes(TA[0], tA, "oT", [oT[:, j * P:(j + 1) * P] for j in range(NT)])
                if tC is not None:
                    HC.wait_free(pe, tC, "ranks")
                    wait(pe, "earlier", tC)
                    m.matmul(HC.tensor[:, 0:8 * (NT + 1)], ones_b[:],
                             earlier[:].rearrange("p j e -> p (j e)"), start=True, stop=False)
                    m.matmul(HC.tensor[:, 0:8 * NT], tri[:], chosen_b[:].rearrange("p j e -> p (j e)"),
                             start=False, stop=True).then_inc(HC.filled, 1)

            iterations(pe, step)

            def tile_slot(s, u):
                i = tile_at(s, 0)
                if i is not None:
                    pe.wait_ge(tile_loaded[u], 16 * (i // UNROLL + 1) if isinstance(i, int)
                               else 16 // UNROLL * (i - u) + 16)
                    if not (isinstance(i, int) and i < 2):
                        wait(pe, "tile_xg", i - 2)
                    m.transpose(XT[u % 2][:, 0:P], tile_rows[u][:, 0:D], ident[:]).then_inc(
                        ready("tile_xT"), 1)
                i = tile_at(s, 1)
                if i is not None:
                    q = (u - 1) % 2
                    e = pe.value_load(expert_of[0:1, bass.ds(i, 1)], min_val=0, max_val=E1 - 1)
                    wait(pe, "tile_xg", i)
                    if not (isinstance(i, int) and i < 2):
                        wait(pe, "tile_hb", i - 2)
                    m.matmul(HX[q][:, 0:HE], xg[q], fw1[:, bass.ds(e * HE, HE)],
                             start=True, stop=True).then_inc(ready("tile_h"), 1)
                i = tile_at(s, 3)
                if i is not None:
                    q = (u - 3) % 2
                    wait(pe, "tile_hg", i)
                    if not (isinstance(i, int) and i < 2):
                        wait(pe, "tile_hgT", i - 2)
                    m.transpose(HTX[q][:, 0:P], hg[q][:, 0:P], ident[:])
                    m.transpose(HTX[q][:, P:HE], hg[q][:, P:HE], ident[:]).then_inc(
                        ready("tile_hT"), 1)
                i = tile_at(s, 4)
                if i is not None:
                    q = (u - 4) % 2
                    e = pe.value_load(expert_of[0:1, bass.ds(i, 1)], min_val=0, max_val=E1 - 1)
                    wait(pe, "tile_hgT", i)
                    if not (isinstance(i, int) and i < 2):
                        wait(pe, "tile_yb", i - 2)
                    m.matmul(YX[q][:, 0:D], hgT[q][:, 0:P], fw2[:, bass.ds(e * HE, D)],
                             start=True, stop=False)
                    m.matmul(YX[q][:, 0:D], hgT[q][:, P:HE], fw2[:, bass.ds(e * HE + D, D)],
                             start=False, stop=True).then_inc(ready("tile_y"), 1)

            pe.wait_ge(ready("table"), 1)
            HC.wait_read(pe, G - 1, "ranks")
            slots(pe, tile_slot)

        @block.vector
        def _(dve):
            v = nc.vector

            dve.wait_ge(weights_loaded, WEIGHTS)
            dve.wait_ge(ready("ident"), 1)
            dve.wait_ge(ready("pool_const"), POOL_CONSTANTS)
            v.tensor_scalar(bwa[:], wa_col[:], bW_col[:], None, ALU.mult).then_inc(ready("bwa"), 1)
            v.tensor_scalar(eps_ident[:], ident[:], eps_bc[:], None, ALU.mult).then_inc(
                ready("eps_ident0"), 1)
            dve.wait_ge(ready("eps_ident0"), 1)
            v.tensor_tensor(eps_ident[:], eps_ident[:], ident[:], ALU.add)
            dve.wait_ge(ready("setup1"), 1)
            v.tensor_copy(gWT[:], HC.tensor[:, 0:D])
            v.tensor_copy(u_col[:], HC.tensor[:, D:D + 2]).then_inc(ready("u_col"), 1)
            dve.wait_ge(ready("u_col"), 1)
            v.tensor_scalar(uj_bc[:], ones[:], u_col[:, 1:2], None, ALU.mult)
            dve.wait_ge(ready("setup2"), 1)
            v.tensor_tensor(c_pair[:], AJ.tensor[:, 0:2], ba_bc[:], ALU.add).then_inc(ready("c_pair"), 1)
            dve.wait_ge(ready("c_pair"), 1)
            v.tensor_tensor(c_sum[:], c_pair[:, 0:1], c_pair[:, 1:2], ALU.add).then_inc(ready("c_sum"), 1)
            dve.wait_ge(ready("c_sum"), 1)
            v.tensor_scalar(c_relu[:], c_sum[:], 1.0 - SLOPE, None, ALU.mult)
            v.tensor_scalar(c_sink[:], c_sum[:], -SLOPE, SINK, ALU.mult, ALU.add).then_inc(
                ready("setup_done"), 1)
            dve.wait_ge(ready("setup_done"), 1)

            def x3_of(g):
                return x3[:, g, :, :] if isinstance(g, int) else x3[:, bass.ds(g, 1), :, :].squeeze(1)

            v.memset(earlier_f[:, 0, :], 0.0)

            def stats(s, t, x):
                for j in range(NT):
                    last = v.bn_stats(bn[s][:, j, :], x[:, j, :])
                last.then_inc(ready(f"bn_{s}"), 1)
                wait(dve, f"bn_{s}", t)
                apart(dve)
                for j in range(NT):
                    last = v.bn_aggr(mv[s][:, j, :], bn[s][:, j, :])
                last.then_inc(ready(f"stats_{s}"), 1)

            def normalise(s, t, x, dst, name):
                wait(dve, f"rstd_{s}", t)
                for j in range(NT):
                    last = v.tensor_scalar(dst[:, j, 0:D], x[:, j, :], mv[s][:, j, 0:1],
                                           rstd[s][:, j:j + 1], ALU.subtract, ALU.mult)
                last.then_inc(ready(name), 1)

            def best_two(r, t, values, name):
                wait(dve, name, t)
                apart(dve)
                for j in range(NT):
                    last = v.max(best[r][:, j, :], values[:, j, :])
                last.then_inc(ready(f"best_{r}"), 1)
                wait(dve, f"best_{r}", t)
                v.tensor_tensor(wgap[r][:], best[r][:, :, 1], best[r][:, :, 0], ALU.subtract).then_inc(
                    ready(f"wgap_{r}"), 1)
                for j in range(NT):
                    last = v.max_index(best_i[r][:, j, :], best[r][:, j, :], values[:, j, :])
                last.then_inc(ready(f"best_i_{r}"), 1)
                wait(dve, f"best_i_{r}", t)
                v.tensor_copy(best_f[r][:], best_i[r][:, :, 0:2].rearrange("p j k -> p k j")).then_inc(
                    ready(f"best_f_{r}"), 1)
                wait(dve, f"best_f_{r}", t)
                for c in range(2):
                    last = v.tensor_tensor(hot[r][:, c, :, :], bc(iota8[:], 1, NT),
                                           bc(best_f[r][:, c, :], 2, 8), ALU.is_equal)
                last.then_inc(ready(f"hot_{r}"), 1)
                wait(dve, f"wexp_{r}", t)
                v.tensor_scalar(wden[r][:], wexp[r][:], 1.0, None, ALU.add).then_inc(
                    ready(f"wden_{r}"), 1)
                wait(dve, f"wden_{r}", t)
                v.reciprocal(w01[r][:, 0, :], wden[r][:]).then_inc(ready(f"w0_{r}"), 1)
                wait(dve, f"w0_{r}", t)
                v.tensor_tensor(w01[r][:, 1, :], wexp[r][:], w01[r][:, 0, :], ALU.mult).then_inc(
                    ready(f"w1_{r}"), 1)
                wait(dve, f"w1_{r}", t)
                wait(dve, f"hot_{r}", t)

            def add_expert(t, e, pb):
                OB.wait_full(dve, t, f"e{e}")
                if e == 0:
                    wait(dve, "gate", t)
                else:
                    OB.wait_read(dve, t, OB.uses[OB.uses.index(f"e{e}") - 1])
                for j in range(NT):
                    last = v.scalar_tensor_tensor(
                        out=x2[pb][:, j, :], in0=OB.tensor[:, j * P:(j + 1) * P],
                        scalar=gate[:, j, e:e + 1], in1=(x1 if e == 0 else x2)[pb][:, j, :],
                        op0=ALU.mult, op1=ALU.add)
                last.then_inc(OB.drained, 1)

            def step(tA, tB, tC, par):
                pb = 1 - par
                if tA is not None:
                    dve.wait_ge(x0_loaded[par], 16 * (tA // 2 + 1) if isinstance(tA, int)
                                else 8 * (tA - par) + 16)
                    stats("A", tA, x0[par])
                    dve.wait_ge(adj_loaded[par], 16 * (tA // 2 + 1) if isinstance(tA, int)
                                else 8 * (tA - par) + 16)
                    v.tensor_scalar(pen[:], adj[par][:], 0.0, MASKED, ALU.is_le, ALU.mult).then_inc(
                        ready("pen"), 1)
                    normalise("A", tA, x0[par], xn, "xn")
                    TA[1].wait_full(dve, tA, "ai")
                    v.tensor_scalar(relu_bias[:], TA[1].tensor[:, 0:NT], 1.0 - SLOPE, c_relu[:],
                                    ALU.mult, ALU.add).then_inc(ready("relu_bias"), 1)
                    v.tensor_scalar(sink[:], TA[1].tensor[:, 0:NT], -SLOPE, c_sink[:],
                                    ALU.mult, ALU.add).then_inc(TA[1].drained, 1)
                if tB is not None:
                    HB[1].wait_full(dve, tB, "logits")
                    v.tensor_tensor(lg[:], HB[1].tensor[:, 0:NT * PADW].rearrange("p (j e) -> p j e", e=PADW)[:, :, 0:E0],
                                    bc(rb2_bc[:], 1, NT), ALU.add).then_inc(HB[1].drained, 1)
                    HB[1].wait_read(dve, tB, "logits")
                    v.tensor_reduce(lg_max[:], lg[:], AX.X, ALU.max).then_inc(ready("lg_max"), 1)
                    wait(dve, "lg_max", tB)
                    v.tensor_tensor(lg[:], lg[:], bc(lg_max[:], 2, E0), ALU.subtract).then_inc(
                        ready("lg_centred"), 1)
                if tA is not None:
                    ZB.wait_full(dve, tA, "z")
                    v.tensor_tensor(z[:], ZB.tensor[:].rearrange("p (j d) -> p j d", d=D),
                                    bc(bW_bc[:], 1, NT), ALU.add).then_inc(ZB.drained, 1)
                if tB is not None:
                    wait(dve, "lg_exp", tB)
                    v.tensor_reduce(lg_sum[:], prob[:, :, 0:E0], AX.X, ALU.add).then_inc(ready("lg_sum"), 1)
                    wait(dve, "lg_sum", tB)
                    v.reciprocal(lg_rsum[:], lg_sum[:]).then_inc(ready("lg_rsum"), 1)
                    wait(dve, "lg_rsum", tB)
                    v.tensor_tensor(prob[:, :, 0:E0], prob[:, :, 0:E0], bc(lg_rsum[:], 2, E0),
                                    ALU.mult).then_inc(ready("prob"), 1)
                    best_two("B", tB, prob, "prob")
                    for c in range(2):
                        last = v.tensor_tensor(hotw[:, c, :, :], hot["B"][:, c, :, :],
                                               bc(w01["B"][:, c, :], 2, 8), ALU.mult)
                    last.then_inc(ready("hotw"), 1)
                    wait(dve, "hotw", tB)
                    v.tensor_tensor(gate[:], hotw[:, 0, :, :], hotw[:, 1, :, :], ALU.add).then_inc(
                        ready("gate"), 1)
                if tA is not None:
                    for j in range(NT):
                        wait(dve, "relu", tA, NT, j)
                        wait(dve, "pen_aj", tA, NT, j)
                        apart(dve)
                        last = v.tensor_tensor_reduce(att[:, j, :], att[:, j, :], pen[:, j, :], 1.0, MASKED,
                                                      ALU.add, ALU.max, row_max[:, j:j + 1])
                    last.then_inc(ready("row_max"), 1)
                    wait(dve, "row_max", tA)
                    v.tensor_tensor(top[:], row_max[:], sink[:], ALU.max).then_inc(ready("top"), 1)
                    wait(dve, "top", tA)
                    v.tensor_scalar(neg_max[:], top[:], -1.0, None, ALU.mult).then_inc(ready("neg_max"), 1)
                    wait(dve, "neg_max", tA)
                    v.tensor_tensor(sink_arg[:], sink[:], neg_max[:], ALU.add).then_inc(
                        ready("sink_arg"), 1)
                if tB is not None:
                    add_expert(tB, 0, pb)
                    add_expert(tB, 1, pb)
                if tC is not None:
                    HC.wait_full(dve, tC, "out")
                    wait(dve, "x2b", tC)
                    v.tensor_tensor(x3_of(tC), HC.tensor[:].rearrange("p (j d) -> p j d", d=D), x2b[:],
                                    ALU.add).then_inc(HC.drained, 1)
                    HC.wait_read(dve, tC, "out")
                    apart(dve)
                    stats("D", tC, x3_of(tC))
                if tB is not None:
                    OB.wait_full(dve, tB, "gateT")
                    v.tensor_copy(gateT[:], OB.tensor[0:8, :]).then_inc(OB.drained, 1)
                    add_expert(tB, 2, pb)
                if tC is not None:
                    normalise("D", tC, x3_of(tC), x3n, "x3_outer")
                    wait(dve, "x3_outer", tC)
                    stats("E", tC, x3n)
                if tA is not None:
                    TA[0].wait_full(dve, tA, "pT0")
                    v.tensor_copy(pT[:, 0, :], TA[0].tensor[:]).then_inc(TA[0].drained, 1)
                if tB is not None:
                    OB.wait_full(dve, tB, "b3")
                    OB.wait_read(dve, tB, "e2")
                    v.tensor_tensor(x2[pb][:], OB.tensor[:].rearrange("p (j d) -> p j d", d=D),
                                    x2[pb][:], ALU.add).then_inc(OB.drained, 1)
                    add_expert(tB, 3, pb)
                if tC is not None:
                    if not (isinstance(tC, int) and tC == 0):
                        dve.wait_ge(rows_sent, 16 * 2 * NT * tC)
                    normalise("E", tC, x3n, rows[0], "x3n")
                if tA is not None:
                    TA[0].wait_full(dve, tA, "pT2")
                    v.tensor_copy(pT[:, 2, :], TA[0].tensor[:]).then_inc(TA[0].drained, 1)
                    wait(dve, "edge_exp", tA, NT, NT - 1)
                    wait(dve, "sink_exp", tA)
                    v.tensor_tensor(den[:], row_sum[:], sink_exp[:], ALU.add).then_inc(ready("den"), 1)
                if tB is not None:
                    add_expert(tB, 4, pb)
                if tA is not None:
                    wait(dve, "den", tA)
                    v.reciprocal(rden[:], den[:]).then_inc(ready("rden"), 1)
                if tB is not None:
                    add_expert(tB, 5, pb)
                    OB.wait_read(dve, tB, "e5")
                    stats("C", tB, x2[pb])
                if tA is not None:
                    TA[0].wait_full(dve, tA, "oT")
                    wait(dve, "rden", tA)
                    for j in range(NT):
                        last = v.scalar_tensor_tensor(
                            out=x1[par][:, j, :], in0=TA[0].tensor[:, j * P:(j + 1) * P],
                            scalar=rden[:, j:j + 1], in1=x0[par][:, j, :], op0=ALU.mult, op1=ALU.add)
                    last.then_inc(TA[0].drained, 1)
                if tB is not None:
                    normalise("C", tB, x2[pb], x2n[pb], "x2n")
                if tC is not None:
                    HC.wait_full(dve, tC, "logits1")
                    v.tensor_tensor(logits1[:], HC.tensor[:, 0:NT * PADW].rearrange(
                        "p (j e) -> p j e", e=PADW)[:, :, 0:E1], bc(br_bc[:], 1, NT), ALU.add).then_inc(
                        HC.drained, 1)
                    HC.wait_read(dve, tC, "logits1")
                    best_two("D", tC, logits1, "x3n")
                    v.tensor_tensor(chosen[:], hot["D"][:, 0, :, :], hot["D"][:, 1, :, :],
                                    ALU.add).then_inc(ready("chosen"), 1)
                    wait(dve, "chosen", tC)
                    v.tensor_copy(chosen_b[:], chosen[:])
                    for j in range(NT):
                        v.tensor_tensor(earlier_f[:, j + 1, :], earlier_f[:, j, :], chosen[:, j, :],
                                        ALU.add).then_inc(ready("earlier_f"), 1)
                        wait(dve, "earlier_f", tC, NT, j)
                    v.tensor_copy(earlier[:], earlier_f[:]).then_inc(ready("earlier"), 1)
                    wait(dve, "row1_features", tC)
                    for k in range(2):
                        v.tensor_copy(rows[k][:, :, PLACE].bitcast(U32), place[:, k, :])
                        last = v.tensor_copy(rows[k][:, :, WEIGHT], w01["D"][:, k, :])
                    last.then_inc(ready("rows_ready"), 1)
                    wait(dve, "rows_ready", tC)
                    v.tensor_scalar(place[:], place[:], float(2 * N), None, ALU.add).then_inc(
                        ready("place"), 1)
                    HC.wait_full(dve, tC, "ranks")
                    v.tensor_tensor(slot_of[:], HC.tensor[:, 0:8 * NT].rearrange("p (j e) -> p j e", e=8),
                                    bc(base[:], 1, NT), ALU.add).then_inc(ready("slot_of"), 1)
                    wait(dve, "slot_of", tC)
                    v.tensor_tensor(base[:], HC.tensor[:, 8 * NT:8 * (NT + 1)], base[:], ALU.add).then_inc(
                        HC.drained, 1)
                    for k in range(2):
                        last = v.tensor_tensor(slot_hot[:, k, :, :], slot_of[:], hot["D"][:, k, :, :],
                                               ALU.mult)
                    last.then_inc(ready("slot_hot"), 1)
                    wait(dve, "slot_hot", tC)
                    v.tensor_reduce(slot_f[:], slot_hot[:], AX.X, ALU.add).then_inc(ready("slot_f"), 1)
                    wait(dve, "slot_f", tC)
                    v.tensor_copy(slot[:], slot_f[:]).then_inc(ready("slot"), 1)
                if tA is not None:
                    TA[0].wait_read(dve, tA, "oT")
                    stats("B", tA, x1[par])
                    normalise("B", tA, x1[par], x1n, "x1n")

            iterations(dve, step)

            def then(step, instruction):
                instruction.then_inc(ready("table_step"), 1)
                dve.wait_ge(ready("table_step"), step)

            HC.wait_read(dve, G - 1, "ranks")
            then(1, v.tensor_scalar(spare_f[:], base[:], iota_part[:], None, ALU.add))
            v.tensor_copy(spare[:], spare_f[:]).then_inc(ready("spare"), 1)
            then(2, v.tensor_tensor(count[:], base[0:1, :], iota_region[0:1, :], ALU.subtract))
            then(3, v.tensor_scalar(count[:], count[:], float(P - 1), None, ALU.add))
            then(4, v.tensor_copy(count_i[:], count[:]))
            then(5, v.tensor_scalar(tiles_i[:], count_i[:], P.bit_length() - 1, None,
                                            ALU.arith_shift_right))
            then(6, v.tensor_copy(tiles[:], tiles_i[:]))
            then(7, v.tensor_copy(ends[0][:], tiles[:]))
            for n, by in enumerate((1, 2, 4)):
                v.tensor_copy(ends[n + 1][:, 0:by], ends[n][:, 0:by])
                then(8 + n, v.tensor_tensor(ends[n + 1][:, by:E1], ends[n][:, by:E1],
                                                     ends[n][:, 0:E1 - by], ALU.add))
            then(11, v.tensor_tensor(passed[:], bc(iota_tile[:], 2, E1), bc(ends[3][:], 1, TILES),
                                           ALU.is_ge))
            then(12, v.tensor_tensor(behind[:], passed[:], bc(tiles[:], 1, TILES), ALU.mult))
            then(13, v.tensor_reduce(expert_f[:], passed[:], AX.X, ALU.add))
            then(14, v.tensor_reduce(first[:], behind[:], AX.X, ALU.add))
            then(15, v.tensor_tensor(inside[:], iota_tile[:], first[:], ALU.subtract))
            then(16, v.tensor_scalar(inside[:], inside[:], float(P), None, ALU.mult))
            then(17, v.scalar_tensor_tensor(out=row0_f[:], in0=expert_f[:], scalar=float(CAP),
                                                in1=inside[:], op0=ALU.mult, op1=ALU.add))
            then(18, v.tensor_scalar(expert_m[:], expert_f[:], float(E1 - 1), None, ALU.min))
            v.tensor_copy(row0_of[:], row0_f[:])
            v.tensor_copy(expert_of[:], expert_m[:]).then_inc(ready("table"), 1)
            dve.wait_ge(ready("table"), 1)

            def tile_slot(s, u):
                i = tile_at(s, 1)
                if i is not None:
                    q = (u - 1) % 2
                    e = dve.value_load(expert_of[0:1, bass.ds(i, 1)], min_val=0, max_val=E1 - 1)
                    wait(dve, "tile_h", i)
                    if not (isinstance(i, int) and i < 2):
                        wait(dve, "tile_hg", i - 2)
                    v.tensor_tensor(hb[q], HX[q][:, 0:HE], fb1_bc[:, bass.ds(e * HE, HE)],
                                    ALU.add).then_inc(ready("tile_hb"), 1)
                i = tile_at(s, 3)
                if i is not None:
                    q = (u - 3) % 2
                    wait(dve, "tile_hT", i)
                    if not (isinstance(i, int) and i < 2):
                        wait(dve, "tile_y", i - 2)
                    v.tensor_copy(hgT[q], HTX[q][:, 0:HE]).then_inc(ready("tile_hgT"), 1)
                i = tile_at(s, 4)
                if i is not None:
                    q = (u - 4) % 2
                    e = dve.value_load(expert_of[0:1, bass.ds(i, 1)], min_val=0, max_val=E1 - 1)
                    wait(dve, "tile_y", i)
                    if not (isinstance(i, int) and i < 2):
                        wait(dve, "tile_yw", i - 2)
                    v.tensor_tensor(yb[q], YX[q][:, 0:D], fb2_bc[:, bass.ds(e * D, D)],
                                    ALU.add).then_inc(ready("tile_yb"), 1)

            slots(dve, tile_slot)

            def add_pair(g, par):
                dve.wait_ge(pair_loaded[par], 16 * (g // 2 + 1) if isinstance(g, int)
                            else 8 * (g - par) + 16)
                if not (isinstance(g, int) and g < 2):
                    dve.wait_ge(out_stored[par], 16 * (g // 2) if isinstance(g, int)
                                else 8 * (g - par))
                v.tensor_tensor(fin[par], pair[par][:, :, 0:D], x3_of(g), ALU.add).then_inc(
                    ready("fin_part"), 1)
                wait(dve, "fin_part", g)
                v.tensor_tensor(fin[par], fin[par], pair[par][:, :, D:2 * D], ALU.add).then_inc(
                    ready("fin"), 1)

            add_pair(0, 0)
            add_pair(1, 1)
            with dve.Fori(1, G // 2) as i:
                for par in range(2):
                    add_pair(2 * i + par, par)


_INS = ['x', 'adj', 'L0_gnn_W', 'L0_gnn_bW', 'L0_gnn_wai', 'L0_gnn_bai', 'L0_gnn_waj', 'L0_gnn_baj',
        'L0_ffn_router_w1', 'L0_ffn_router_b1', 'L0_ffn_router_w2', 'L0_ffn_router_b2',
        'L0_ffn_expert_w1', 'L0_ffn_expert_b1', 'L0_ffn_expert_w2', 'L0_ffn_expert_b2',
        'L0_ffn_expert_w3', 'L0_ffn_expert_b3', 'L1_gnn_eps', 'L1_gnn_W1', 'L1_gnn_b1', 'L1_gnn_W2',
        'L1_gnn_b2', 'L1_ffn_gamma', 'L1_ffn_beta', 'L1_ffn_Wr', 'L1_ffn_br', 'L1_ffn_W1',
        'L1_ffn_b1', 'L1_ffn_W2', 'L1_ffn_b2']


def kernel(**inputs):
    import numpy as _np
    import concourse.bacc as _bacc
    from concourse import mybir as _mybir
    from concourse.bass_utils import run_bass_kernel_spmd as _run

    nc = _bacc.Bacc("TRN2", target_bir_lowering=False, num_devices=1)
    arrays, args = {}, {}
    for name in _INS:
        a = _np.ascontiguousarray(inputs[name])
        arrays[f"in_{name}"] = a
        args[name] = nc.dram_tensor(f"in_{name}", a.shape, _mybir.dt.from_np(a.dtype),
                                    kind="ExternalInput").ap()
    out = nc.dram_tensor("result", (G, N, D), _mybir.dt.float32, kind="ExternalOutput").ap()
    build(nc, args, out)
    r = _run(nc, [arrays], core_ids=[0])
    return r.results[0]["result"]
```

```python
from contextlib import ExitStack

import concourse.bass as bass
from concourse import mybir

F32 = mybir.dt.float32
U32 = mybir.dt.uint32
I32 = mybir.dt.int32
BF16 = mybir.dt.bfloat16
ALU = mybir.AluOpType
ACT = mybir.ActivationFunctionType
AX = mybir.AxisListType

P = 128
G, N, D = 16, 512, 128
NT = N // P
E0 = 6
RH = 64
DH = 256
E1 = 8
SLOPE = 0.2
MASKED = -9.0e15
SINK = -1.0e9
LN_EPS = 1e-5
HE = 256
NODES = G * N
TILE = 2 * P
CAP = NODES + TILE
SPARE = E1 * CAP
ROW = D + 2
PLACE, WEIGHT = D, D + 1
TILES = 2 * NODES // TILE + E1
IDLE = E1
LAG = 3
UNROLL = 6
PADW = 96


class Bank:

    def __init__(self, tensor, filled, drained, uses):
        self.tensor, self.filled, self.drained, self.uses = tensor, filled, drained, uses

    def wait_free(self, eng, t, use):
        k = self.uses.index(use)
        n = t * len(self.uses) + k
        if isinstance(n, int) and n == 0:
            return
        eng.wait_ge(self.drained, n)

    def wait_read(self, eng, t, use):
        eng.wait_ge(self.drained, t * len(self.uses) + self.uses.index(use) + 1)

    def wait_full(self, eng, t, use):
        eng.wait_ge(self.filled, t * len(self.uses) + self.uses.index(use) + 1)


def build(nc, a, out):
    with ExitStack() as ctx:
        def sb(name, shape, dt=F32):
            return ctx.enter_context(nc.sbuf_tensor(name, shape, dt))

        def sem(name):
            return ctx.enter_context(nc.semaphore(name))

        def bank(name, uses):
            t = ctx.enter_context(nc.psum_tensor(name + "_bank", [P, 512], F32))
            return Bank(t, sem(name + "_filled"), sem(name + "_drained"), uses)

        TA = [bank("ta0", ["xT", "pT0", "pT2", "oT"]), bank("ta1", ["ai", "pT1", "pT3"])]
        AJ = bank("aj", ["aj"])
        ZB = bank("zb", ["z", "o"])
        HB = [bank("hb0", ["adjT0", "adjT2", "route_h"] + [f"h1_{e}" for e in range(E0)]),
              bank("hb1", ["adjT1", "x1T", "adjT3", "logits"] + [f"h2_{e}" for e in range(E0)])]
        OB = bank("ob", ["e0", "gateT", "e1", "b3", "e2", "e3", "e4", "e5"])
        HC = bank("hc", ["agg", "m0", "m1", "out", "x3T", "logits1"])
        RK = Bank(AJ.tensor, sem("rk_filled"), sem("rk_drained"), ["ranks"])

        XT = [TA[0].tensor, TA[1].tensor]
        HX = [AJ.tensor, ZB.tensor]
        YX = [OB.tensor, HC.tensor]

        tri = sb("tri", [P, P], BF16)
        ones_b = sb("ones_b", [P, P], BF16)
        iota_node = sb("iota_node", [P, NT])
        iota_part = sb("iota_part", [P, 1])
        iota_region = sb("iota_region", [P, E1])
        iota_tile = sb("iota_tile", [1, TILES])
        gamma = sb("gamma", [P, 1])
        beta = sb("beta", [P, 1])
        wr = sb("wr", [P, PADW])
        br_bc = sb("br_bc", [P, E1])
        fw1 = sb("fw1", [P, E1 * HE])
        fw2 = sb("fw2", [P, E1 * HE])
        fb1 = sb("fb1", [P, E1 * HE // P])
        fb2_bc = sb("fb2_bc", [P, E1 * D])
        ident = sb("ident", [P, P])
        eps_ident = sb("eps_ident", [P, P])
        eps_tile = sb("eps_tile", [P, NT])
        minus_half = sb("minus_half", [P, NT])
        iota8 = sb("iota8", [P, 8])
        gW = sb("gW", [P, D])
        gWT = sb("gWT", [P, D])
        bW_bc = sb("bW_bc", [P, D])
        bW_col = sb("bW_col", [P, 1])
        wa_col = sb("wa_col", [P, 2])
        ba_bc = sb("ba_bc", [P, 2])
        u_col = sb("u_col", [P, 2])
        uj_bc = sb("uj_bc", [P, P])
        bwa = sb("bwa", [P, 2])
        c_pair = sb("c_pair", [P, 2])
        c_sum = sb("c_sum", [P, 1])
        c_relu = sb("c_relu", [P, 1])
        c_sink = sb("c_sink", [P, 1])
        ones = sb("ones", [P, P])
        rw1 = sb("rw1", [P, RH])
        rb1 = sb("rb1", [RH, 1])
        rw2 = sb("rw2", [RH, PADW])
        rb2_bc = sb("rb2_bc", [P, E0])
        ew = [sb(f"ew{i}", [P, E0, D]) for i in (1, 2, 3)]
        eb1 = sb("eb1", [P, E0])
        eb2 = sb("eb2", [P, E0])
        eb3 = sb("eb3", [E0, D])
        eps_bc = sb("eps_bc", [P, 1])
        mw1 = sb("mw1", [P, DH])
        mb1 = sb("mb1", [P, 2])
        mw2 = sb("mw2", [P, 2, D])
        mb2_bc = sb("mb2_bc", [P, D])

        adj = [sb(f"adj{i}", [P, NT, N]) for i in range(2)]
        x0 = [sb(f"x0_{i}", [P, NT, D]) for i in range(2)]
        bn = {s: sb(f"bn_{s}", [P, NT, 6]) for s in "ABCDE"}
        mv = {s: sb(f"mv_{s}", [P, NT, 2]) for s in "ABCDE"}
        var_eps = {s: sb(f"ve_{s}", [P, NT]) for s in "ABCDE"}
        rstd = {s: sb(f"rstd_{s}", [P, NT]) for s in "ABCDE"}
        xn = sb("xn", [P, NT, D])
        xnT = sb("xnT", [P, N])
        z = sb("z", [P, NT, D])
        relu_bias = sb("relu_bias", [P, NT])
        sink = sb("sink", [P, NT])
        aj02 = sb("aj02", [P, N])
        pen = sb("pen", [P, NT, N])
        att = sb("att", [P, NT, N])
        row_max = sb("row_max", [P, NT])
        top = sb("top", [P, NT])
        neg_max = sb("neg_max", [P, NT])
        sink_arg = sb("sink_arg", [P, NT])
        sink_exp = sb("sink_exp", [P, NT])
        row_sum = sb("row_sum", [P, NT])
        den = sb("den", [P, NT])
        rden = sb("rden", [P, NT])
        pT = sb("pT", [P, NT, N])
        oT = sb("oT", [P, N])
        x1 = [sb(f"x1_{i}", [P, NT, D]) for i in range(2)]
        x1n = sb("x1n", [P, NT, D])
        x1nT = sb("x1nT", [P, N])
        adjT = [sb(f"adjT{i}", [P, NT, N]) for i in range(2)]
        rh = sb("rh", [RH, N])
        lg = sb("lg", [P, NT, E0])
        lg_max = sb("lg_max", [P, NT])
        lg_sum = sb("lg_sum", [P, NT])
        lg_rsum = sb("lg_rsum", [P, NT])
        prob = sb("prob", [P, NT, 8])
        best, best_i, best_f, wgap, wexp, wden, w01, hot = ({} for _ in range(8))
        for r in "BD":
            best[r] = sb(f"best_{r}", [P, NT, 8])
            best_i[r] = sb(f"best_i_{r}", [P, NT, 8], U32)
            best_f[r] = sb(f"best_f_{r}", [P, 2, NT])
            wgap[r] = sb(f"wgap_{r}", [P, NT])
            wexp[r] = sb(f"wexp_{r}", [P, NT])
            wden[r] = sb(f"wden_{r}", [P, NT])
            w01[r] = sb(f"w01_{r}", [P, 2, NT])
            hot[r] = sb(f"hot_{r}", [P, 2, NT, 8])
        hotw = sb("hotw", [P, 2, NT, 8])
        gate = sb("gate", [P, NT, 8])
        gateT = sb("gateT", [8, N])
        h1 = [sb(f"h1_{i}", [P, N]) for i in range(2)]
        h2 = [sb(f"h2_{i}", [P, N]) for i in range(2)]
        x2 = [sb(f"x2_{i}", [P, NT, D]) for i in range(2)]
        x2n = [sb(f"x2n_{i}", [P, NT, D]) for i in range(2)]
        x2b = sb("x2b", [P, NT, D])
        hT = sb("hT", [P, N])
        m1 = sb("m1", [P, 2, N])
        x3 = sb("x3", [P, G, NT, D])
        x3n = sb("x3n", [P, NT, D])
        rows = [sb(f"rows{k}", [P, NT, ROW]) for k in range(2)]
        x3T = sb("x3T", [P, N])
        logits1 = sb("logits1", [P, NT, 8])
        chosen = sb("chosen", [P, NT, 8])
        earlier = sb("earlier", [P, NT + 1, 8], BF16)
        chosen_b = sb("chosen_b", [P, NT, 8], BF16)
        earlier_f = sb("earlier_f", [P, NT + 1, 8])
        base = sb("base", [P, E1])
        slot_of = sb("slot_of", [P, NT, 8])
        slot_hot = sb("slot_hot", [P, 2, NT, 8])
        slot_f = sb("slot_f", [P, 2, NT])
        slot = sb("slot", [P, 2, NT], U32)
        place = sb("place", [P, 2, NT])
        filling = [b[:].rearrange("p j m -> p (j m)")[:, 0:4 * 2 * ROW].rearrange(
            "p (e b r) -> p e b r", b=2, r=ROW) for b in (adj[0], adj[1], pen, att)]
        filled_to = sb("filled_to", [1, E1], I32)
        count = sb("count", [1, E1])
        count_i = sb("count_i", [1, E1], I32)
        tiles_i = sb("tiles_i", [1, E1], I32)
        tiles = sb("tiles", [1, E1])
        ends = [sb(f"ends{i}", [1, E1]) for i in range(4)]
        passed, behind = (pT[0:1, k:k + 2, :].rearrange("p j m -> p (j m)")[:, 0:TILES * E1].rearrange(
            "p (t e) -> p t e", e=E1) for k in (0, 2))
        expert_f = sb("expert_f", [1, TILES])
        first = sb("first", [1, TILES])
        inside = sb("inside", [1, TILES])
        row0_f = sb("row0_f", [1, TILES])
        column_f = sb("column_f", [1, TILES])
        column_of = sb("column_of", [1, TILES], I32)
        row0_of = sb("row0_of", [1, TILES], I32)
        tile_rows = [sb(f"tile_rows{i}", [P, 2, ROW]) for i in range(UNROLL)]
        xg, yb = ([pT[:, k, i * TILE:(i + 1) * TILE] for i in range(2)] for k in (0, 1))
        hg = [pT[:, 2 + i, :].rearrange("p (c r) -> p c r", c=2) for i in range(2)]
        w1 = [adjT[1][:, 0, i * HE:(i + 1) * HE] for i in range(2)]
        adjT_flat = adjT[0][:].rearrange("p j m -> p (j m)")
        yw = [adjT_flat[:, i * 2 * D:(i + 1) * 2 * D].rearrange("p (b d) -> p b d", b=2)
              for i in range(UNROLL)]
        pair = [b[:, 0:2, :].rearrange("p a (b d) -> p (a b) d", d=2 * D) for b in adj]
        fin = [b[:, 0, :].rearrange("p (j d) -> p j d", d=D) for b in adjT]
        sent = nc.dram_tensor("sent", (E1 * CAP + IDLE * TILE, ROW), F32, kind="Internal").ap()
        result2 = nc.dram_tensor("result2", (2 * NODES + (E1 + IDLE) * TILE, D), F32, kind="Internal").ap()

        S = {}

        def ready(name):
            if name not in S:
                S[name] = sem(name)
            return S[name]

        adj_loaded = [sem(f"adj_loaded{i}") for i in range(2)]
        x0_loaded = [sem(f"x0_loaded{i}") for i in range(2)]
        weights_loaded = sem("weights_loaded")
        rows_sent = sem("rows_sent")
        spare_sent = sem("spare_sent")
        idle_sent = sem("idle_sent")
        tile_loaded = [sem(f"tile_loaded{i}") for i in range(UNROLL)]
        result_sent = [sem(f"result_sent{i}") for i in range(UNROLL)]
        pair_loaded = [sem(f"pair_loaded{i}") for i in range(2)]
        out_stored = [sem(f"out_stored{i}") for i in range(2)]

        x_d = a["x"].rearrange("g (j p) d -> g p j d", p=P)
        adj_d = a["adj"].rearrange("g (j p) m -> g p j m", p=P)
        out_d = out.rearrange("g (j p) d -> g p j d", p=P)

        def col(ap):
            return ap.rearrange("(p a) -> p a", a=1)

        loads = [
            (gW[:], a["L0_gnn_W"]),
            (bW_bc[:], a["L0_gnn_bW"].partition_broadcast(P)),
            (bW_col[:], col(a["L0_gnn_bW"])),
            (wa_col[:, 0:1], a["L0_gnn_wai"].rearrange("a p -> p a")),
            (wa_col[:, 1:2], a["L0_gnn_waj"].rearrange("a p -> p a")),
            (ba_bc[:, 0:1], a["L0_gnn_bai"].partition_broadcast(P)),
            (ba_bc[:, 1:2], a["L0_gnn_baj"].partition_broadcast(P)),
            (rw1[:], a["L0_ffn_router_w1"]),
            (rb1[:], col(a["L0_ffn_router_b1"])),
            (rw2[:, 0:E0], a["L0_ffn_router_w2"]),
            (rb2_bc[:], a["L0_ffn_router_b2"].partition_broadcast(P)),
            (ew[0][:], a["L0_ffn_expert_w1"].rearrange("e d h -> d e h")),
            (ew[1][:], a["L0_ffn_expert_w2"].rearrange("e d h -> d e h")),
            (ew[2][:], a["L0_ffn_expert_w3"].rearrange("e d h -> d e h")),
            (eb1[:], a["L0_ffn_expert_b1"].rearrange("e h -> h e")),
            (eb2[:], a["L0_ffn_expert_b2"].rearrange("e h -> h e")),
            (eb3[:], a["L0_ffn_expert_b3"]),
            (eps_bc[:], a["L1_gnn_eps"].partition_broadcast(P)),
            (mw1[:], a["L1_gnn_W1"]),
            (mb1[:], a["L1_gnn_b1"].rearrange("(c p) -> p c", p=P)),
            (mw2[:], a["L1_gnn_W2"].rearrange("(c p) d -> p c d", p=P)),
            (mb2_bc[:], a["L1_gnn_b2"].partition_broadcast(P)),
            (gamma[:], col(a["L1_ffn_gamma"])),
            (beta[:], col(a["L1_ffn_beta"])),
            (wr[:, 0:E1], a["L1_ffn_Wr"]),
            (br_bc[:], a["L1_ffn_br"].partition_broadcast(P)),
            (fw1[:].rearrange("p (e h) -> p e h", e=E1), a["L1_ffn_W1"].rearrange("e d h -> d e h")),
            (fw2[:].rearrange("p (e c d) -> p e c d", e=E1, c=2),
             a["L1_ffn_W2"].rearrange("e (c p) d -> p e c d", p=P)),
            (fb1[:].rearrange("p (e c) -> p e c", c=2), a["L1_ffn_b1"].rearrange("e (c p) -> p e c", p=P)),
            (fb2_bc[:], a["L1_ffn_b2"].rearrange("e h -> (e h)").partition_broadcast(P)),
        ]
        WEIGHTS = 16 * len(loads)
        POOL_CONSTANTS = 16

        def iterations(eng, step):
            step(0, None, None, None, 0)
            step(1, 0, None, None, 1)
            step(2, 1, 0, None, 0)
            step(3, 2, 1, 0, 1)
            with eng.Fori(2, G // 2) as i:
                step(2 * i, 2 * i - 1, 2 * i - 2, 2 * i - 3, 0)
                step(2 * i + 1, 2 * i, 2 * i - 1, 2 * i - 2, 1)
            step(None, G - 1, G - 2, G - 3, 0)
            step(None, None, G - 1, G - 2, 1)
            step(None, None, None, G - 1, 0)

        def wait(eng, name, t, per=1, k=0):
            eng.wait_ge(ready(name), t * per + k + 1)

        def wait_before(eng, name, t, per=1):
            if not (isinstance(t, int) and t == 0):
                eng.wait_ge(ready(name), t * per)

        def bc(ap, axis, n):
            shape = list(ap.shape)
            shape.insert(axis, n)
            return ap.unsqueeze(axis).broadcast_to(shape)

        def apart(eng):
            eng.nop(nofuse=True)

        def slots(eng, slot):
            for s in range(2 * UNROLL):
                slot(s, s % UNROLL, s // UNROLL)
            with eng.Fori(2, TILES // UNROLL) as r:
                for u in range(UNROLL):
                    slot(UNROLL * r + u, u, r)
            for s in range(TILES, TILES + LAG):
                slot(s, s % UNROLL, s // UNROLL)

        def turn_at(u, r, back):
            return r if u >= back else r - 1

        def tile_at(s, back):
            if isinstance(s, int) and not 0 <= s - back < TILES:
                return None
            return s - back

        block = ctx.enter_context(nc.Block())

        @block.sync
        def _(sp):
            def load(t, par):
                sp.dma_start(x0[par][:], x_d[t]).then_inc(x0_loaded[par], 16)
                sp.dma_start(adj[par][:], adj_d[t]).then_inc(adj_loaded[par], 16)

            load(0, 0)
            for dst, src in loads:
                sp.dma_start(dst, src, allow_slow_non_contiguous=True).then_inc(weights_loaded, 16)
            load(1, 1)
            with sp.Fori(0, (G - 2) // 2) as i:
                for par in range(2):
                    t = 2 * i + 2 + par
                    TA[0].wait_read(sp, t - 2, "oT")
                    HB[1].wait_full(sp, t - 2, "adjT3")
                    load(t, par)

            sp.wait_ge(ready("filling"), 4)
            sp.wait_ge(ready("table"), 1)
            for e in range(E1):
                end = sp.value_load(filled_to[0:1, e:e + 1], min_val=e * CAP, max_val=e * CAP + NODES)
                sp.dma_start(sent[bass.ds(end, TILE), :].rearrange("(p b) r -> p b r", b=2),
                             filling[e // 4][:, e % 4, :, :]).then_inc(spare_sent, 16)
            sp.wait_ge(rows_sent, 16 * 2 * NT * G)
            sp.wait_ge(spare_sent, 16 * E1)
            sp.wait_ge(idle_sent, 16 * 2)

            def tile(i, q, r):
                row0 = sp.value_load(row0_of[0:1, bass.ds(i, 1)], min_val=0,
                                     max_val=SPARE + (IDLE - 1) * TILE)
                if not (isinstance(r, int) and r == 0):
                    sp.wait_ge(result_sent[q], 32 * r)
                sp.dma_start(tile_rows[q][:], sent[bass.ds(row0, TILE), :].rearrange(
                    "(p b) r -> p b r", b=2)).then_inc(tile_loaded[q], 16)

            for q in range(UNROLL):
                tile(q, q, 0)
            with sp.Fori(1, TILES // UNROLL) as r:
                for q in range(UNROLL):
                    tile(UNROLL * r + q, q, r)

            for q in range(UNROLL):
                sp.wait_ge(result_sent[q], 32 * (TILES // UNROLL))
            pairs = result2[0:2 * NODES, :].rearrange("(g j p k) d -> g p j (k d)", j=NT, p=P, k=2)

            def load_pair(g, par):
                sp.dma_start(pair[par], pairs[g]).then_inc(pair_loaded[par], 16)

            def store(g, par):
                wait(sp, "fin", g)
                sp.dma_start(out_d[g], fin[par]).then_inc(out_stored[par], 16)

            load_pair(0, 0)
            load_pair(1, 1)
            with sp.Fori(0, G // 2 - 1) as i:
                for par in range(2):
                    store(2 * i + par, par)
                    load_pair(2 * i + par + 2, par)
            for par in range(2):
                store(G - 2 + par, par)
            for par in range(2):
                sp.wait_ge(out_stored[par], 16 * G // 2)

        @block.gpsimd
        def _(pool):
            g = nc.gpsimd
            g.memset(ident[:], 0.0).then_inc(ready("ident0"), 1)
            g.memset(minus_half[:], -0.5).then_inc(ready("pool_const"), 1)
            g.memset(ones[:], 1.0).then_inc(ready("pool_const"), 1)
            g.memset(prob[:], -1.0).then_inc(ready("pool_const"), 1)
            g.iota(iota8[:], pattern=[[1, 8]], base=0, channel_multiplier=0,
                   allow_small_or_imprecise_dtypes=True).then_inc(ready("pool_const"), 1)
            g.memset(tri[:], 1.0).then_inc(ready("ident0"), 1)
            g.memset(ones_b[:], 1.0).then_inc(ready("pool_const"), 1)
            g.memset(eps_tile[:], LN_EPS).then_inc(ready("pool_const"), 1)
            g.memset(rw2[:, E0:PADW], 0.0).then_inc(ready("pool_const"), 1)
            g.memset(wr[:, E1:PADW], 0.0).then_inc(ready("pool_const"), 1)
            for dst, pattern, start, by_partition in (
                    (iota_node[:], [[2 * P, NT]], 0, 2), (iota_part[:], [[1, 1]], 0, 1),
                    (iota_region[:], [[CAP, E1]], 0, 0), (place[:, 0, :], [[2 * P, NT]], 0, 2),
                    (place[:, 1, :], [[2 * P, NT]], 1, 2), (base[:], [[CAP, E1]], 0, 0),
                    (iota_tile[:], [[1, TILES]], 0, 0)):
                g.iota(dst, pattern=pattern, base=start, channel_multiplier=by_partition,
                       allow_small_or_imprecise_dtypes=True).then_inc(ready("pool_const"), 1)
            pool.wait_ge(ready("ident0"), 2)
            g.affine_select(out=tri[:], in_=tri[:], compare_op=ALU.is_gt, fill=0.0, base=0,
                            pattern=[[1, P]], channel_multiplier=-1).then_inc(ready("pool_const"), 1)
            g.affine_select(out=ident[:], in_=ident[:], compare_op=ALU.not_equal, fill=1.0, base=0,
                            pattern=[[-1, P]], channel_multiplier=1).then_inc(ready("ident"), 1)
            pool.wait_ge(ready("pool_const"), POOL_CONSTANTS)
            pool.wait_ge(weights_loaded, WEIGHTS)

            def inverse_std(s, t):
                wait(pool, f"stats_{s}", t)
                g.tensor_tensor(var_eps[s][:], mv[s][:, :, 1], eps_tile[:], ALU.add).then_inc(
                    ready(f"var_eps_{s}"), 1)
                wait(pool, f"var_eps_{s}", t)
                g.tensor_tensor(rstd[s][:], var_eps[s][:], minus_half[:], ALU.pow).then_inc(
                    ready(f"rstd_{s}"), 1)

            def dispatch(t, moves):
                for k, j in moves:
                    g.indirect_dma_start(sent, bass.IndirectOffsetOnAxis(slot[:, k, j:j + 1], 0),
                                         rows[k][:, j, :], None).then_inc(rows_sent, 16)

            moves = [(k, j) for k in range(2) for j in range(NT)]

            def step(tA, tB, tC, tD, par):
                if tA is not None:
                    inverse_std("A", tA)
                if tC is not None:
                    OB.wait_read(pool, tC, "e5")
                    HC.wait_free(pool, tC, "agg")
                    for j in range(NT):
                        last = g.tensor_tensor(x2b[:, j, :], x2[par][:, j, :], mb2_bc[:], ALU.add)
                    last.then_inc(ready("x2b"), 1)
                if tA is not None:
                    wait(pool, "pen", tA)
                    wait(pool, "aj02", tA)
                    for j in range(NT):
                        g.tensor_tensor(pen[:, j, :], pen[:, j, :], aj02[:], ALU.add).then_inc(
                            ready("pen_aj"), 1)
                if tD is not None:
                    wait(pool, "slot", tD)
                    wait(pool, "rows_ready", tD)
                    apart(pool)
                    dispatch(tD, moves[:5])
                if tC is not None:
                    inverse_std("D", tC)
                if tD is not None:
                    dispatch(tD, moves[5:])
                if tC is not None:
                    inverse_std("E", tC)
                if tA is not None:
                    inverse_std("B", tA)
                if tB is not None:
                    inverse_std("C", tB)

            iterations(pool, step)

            HB[1].wait_full(pool, G - 1, "adjT3")
            TA[0].wait_read(pool, G - 1, "oT")
            for n, buffer in enumerate(filling):
                g.memset(buffer, 0.0).then_inc(ready("filling0"), 1)
                pool.wait_ge(ready("filling0"), n + 1)
                g.iota(buffer[:, :, :, PLACE].bitcast(U32), pattern=[[TILE, 4], [1, 2]],
                       base=2 * NODES + n * 4 * TILE, channel_multiplier=2).then_inc(ready("filling"), 1)
            pool.wait_ge(ready("filling"), 4)
            for n in range(2):
                g.dma_start(sent[SPARE + n * 4 * TILE:SPARE + (n + 1) * 4 * TILE, :].rearrange(
                    "(e p b) r -> p e b r", p=P, b=2), filling[2 + n]).then_inc(idle_sent, 16)

            def send_slot(s, u, r):
                i = tile_at(s, 3)
                if i is None:
                    return
                q = (u - 3) % UNROLL
                wait(pool, "tile_yw", i)
                apart(pool)
                for b in range(2):
                    g.indirect_dma_start(
                        result2, bass.IndirectOffsetOnAxis(
                            tile_rows[q][:, b, PLACE:PLACE + 1].bitcast(U32), 0),
                        yw[q][:, b, :], None).then_inc(result_sent[q], 16)

            slots(pool, send_slot)

        @block.scalar
        def _(act):
            s = nc.scalar
            act.wait_ge(weights_loaded, WEIGHTS)

            def drain(bk, t, use, dst, func=ACT.Copy, src=None, **kw):
                bk.wait_full(act, t, use)
                s.activation(dst, bk.tensor[:] if src is None else src, func, **kw).then_inc(
                    bk.drained, 1)

            def hidden1(t, e):
                drain(HB[0], t, f"h1_{e}", h1[e % 2][:], ACT.Relu, bias=eb1[:, e:e + 1])

            def edge_exp(j):
                s.activation(att[:, j, :], att[:, j, :], ACT.Exp, bias=neg_max[:, j:j + 1],
                             accum_out=row_sum[:, j:j + 1]).then_inc(ready("edge_exp"), 1)

            def hidden2(t, e):
                drain(HB[1], t, f"h2_{e}", h2[e % 2][:], ACT.Relu, bias=eb2[:, e:e + 1])

            def step(tA, tB, tC, tD, par):
                if tB is not None:
                    for k in (0, 1):
                        drain(HB[k % 2], tB, f"adjT{k}", adjT[1 - par][:, k, :])
                    drain(HB[1], tB, "x1T", x1nT[:])
                    for k in (2, 3):
                        drain(HB[k % 2], tB, f"adjT{k}", adjT[1 - par][:, k, :])
                    drain(HB[0], tB, "route_h", rh[:], ACT.Relu, src=HB[0].tensor[0:RH, :], bias=rb1[:])
                    hidden1(tB, 0)
                if tA is not None:
                    drain(TA[0], tA, "xT", xnT[:])
                if tD is not None:
                    wait(act, "wgap_D", tD)
                    s.activation(wexp["D"][:], wgap["D"][:], ACT.Exp).then_inc(ready("wexp_D"), 1)
                if tB is not None:
                    wait(act, "lg_centred", tB)
                    s.activation(prob[:, :, 0:E0], lg[:], ACT.Exp).then_inc(ready("lg_exp"), 1)
                if tA is not None:
                    AJ.wait_full(act, tA, "aj")
                    wait_before(act, "pen_aj", tA, NT)
                    s.activation(aj02[:], AJ.tensor[:], ACT.Copy, scale=SLOPE).then_inc(ready("aj02"), 1)
                    wait(act, "relu_bias", tA)
                    for j in range(NT):
                        s.activation(att[:, j, :], AJ.tensor[:], ACT.Relu, bias=relu_bias[:, j:j + 1],
                                     scale=1.0 - SLOPE).then_inc(ready("relu"), 1)
                if tB is not None:
                    wait(act, "wgap_B", tB)
                    s.activation(wexp["B"][:], wgap["B"][:], ACT.Exp).then_inc(ready("wexp_B"), 1)
                if tC is not None:
                    drain(HC, tC, "agg", hT[:])
                if tB is not None:
                    hidden2(tB, 0)
                if tC is not None:
                    drain(HC, tC, "m0", m1[:, 0, :], ACT.Relu, bias=mb1[:, 0:1])
                if tB is not None:
                    hidden1(tB, 1)
                if tC is not None:
                    drain(HC, tC, "m1", m1[:, 1, :], ACT.Relu, bias=mb1[:, 1:2])
                if tA is not None:
                    wait(act, "sink_arg", tA)
                    s.activation(sink_exp[:], sink_arg[:], ACT.Exp).then_inc(ready("sink_exp"), 1)
                    for j in (0, 1):
                        edge_exp(j)
                if tB is not None:
                    hidden2(tB, 1)
                if tA is not None:
                    for j in (2, 3):
                        edge_exp(j)
                if tB is not None:
                    hidden1(tB, 2)
                    OB.wait_full(act, tB, "gateT")
                    s.activation(gateT[:], OB.tensor[0:8, :], ACT.Copy).then_inc(OB.drained, 1)
                    hidden2(tB, 2)
                if tA is not None:
                    drain(TA[0], tA, "pT0", pT[:, 0, :])
                    drain(TA[1], tA, "pT1", pT[:, 1, :])
                if tB is not None:
                    hidden1(tB, 3)
                    hidden2(tB, 3)
                if tA is not None:
                    drain(TA[0], tA, "pT2", pT[:, 2, :])
                    drain(TA[1], tA, "pT3", pT[:, 3, :])
                if tC is not None:
                    wait(act, "x3n", tC)
                    if not (isinstance(tC, int) and tC == 0):
                        act.wait_ge(rows_sent, 16 * 2 * NT * tC)
                    s.activation(rows[1][:, :, 0:D], rows[0][:, :, 0:D], ACT.Copy).then_inc(
                        ready("row1_features"), 1)
                if tB is not None:
                    hidden1(tB, 4)
                if tA is not None:
                    drain(ZB, tA, "o", oT[:])
                if tB is not None:
                    hidden2(tB, 4)
                    hidden1(tB, 5)
                if tC is not None:
                    drain(HC, tC, "x3T", x3T[:], ACT.Identity, bias=beta[:], scale=gamma[:])
                if tB is not None:
                    hidden2(tB, 5)

            iterations(act, step)

            def tile_slot(s_, u, r):
                i = tile_at(s_, 3)
                if i is not None:
                    q = (u - 3) % UNROLL
                    wait(act, "tile_yb", i)
                    if not (isinstance(i, int) and i < UNROLL):
                        act.wait_ge(result_sent[q], 32 * turn_at(u, r, 3))
                    for b in range(2):
                        last = s.activation(yw[q][:, b, :], yb[(u - 3) % 2][:, b * D:(b + 1) * D], ACT.Copy,
                                            scale=tile_rows[q][:, b, WEIGHT:WEIGHT + 1])
                    last.then_inc(ready("tile_yw"), 1)
                i = tile_at(s_, 1)
                if i is not None:
                    q = (u - 1) % 2
                    column = act.value_load(column_of[0:1, bass.ds(i, 1)], min_val=0,
                                            max_val=2 * (E1 - 1))
                    wait(act, "tile_h", i)
                    if not (isinstance(i, int) and i < 2):
                        wait(act, "tile_y", i - 2)
                    apart(act)
                    for c in range(2):
                        last = s.activation(hg[q][:, c, :], HX[q][:, c * TILE:(c + 1) * TILE], ACT.Gelu,
                                            bias=fb1[:, bass.ds(column + c, 1)])
                    last.then_inc(ready("tile_hg"), 1)

            act.wait_ge(ready("table"), 1)
            slots(act, tile_slot)

        @block.tensor
        def _(pe):
            m = nc.tensor

            pe.wait_ge(ready("ident"), 1)
            pe.wait_ge(ready("pool_const"), POOL_CONSTANTS)
            pe.wait_ge(weights_loaded, WEIGHTS)
            m.transpose(HC.tensor[:, 0:D], gW[:], ident[:])
            m.matmul(HC.tensor[:, D:D + 2], gW[:], wa_col[:], start=True, stop=True).then_inc(
                ready("setup1"), 1)
            pe.wait_ge(ready("bwa"), 1)
            m.matmul(AJ.tensor[:, 0:2], ones[:], bwa[:], start=True, stop=True).then_inc(
                ready("setup2"), 1)
            pe.wait_ge(ready("setup_done"), 1)

            def transposes(bk, t, use, blocks):
                bk.wait_free(pe, t, use)
                for j, src in enumerate(blocks):
                    last = m.transpose(bk.tensor[:, j * P:(j + 1) * P], src, ident[:])
                last.then_inc(bk.filled, 1)

            def product(bk, t, use, lhsT, rhs):
                bk.wait_free(pe, t, use)
                m.matmul(bk.tensor[0:lhsT.shape[1], :], lhsT, rhs, start=True, stop=True).then_inc(
                    bk.filled, 1)

            def layer1(t, e):
                product(HB[0], t, f"h1_{e}", ew[0][:, e, :], x1nT[:])

            def layer2(t, e):
                HB[0].wait_read(pe, t, f"h1_{e}")
                product(HB[1], t, f"h2_{e}", ew[1][:, e, :], h1[e % 2][:])

            def layer3(t, e):
                OB.wait_free(pe, t, f"e{e}")
                HB[1].wait_read(pe, t, f"h2_{e}")
                for j in range(NT):
                    last = m.matmul(OB.tensor[:, j * P:(j + 1) * P], h2[e % 2][:, j * P:(j + 1) * P],
                                    ew[2][:, e, :], start=True, stop=True)
                last.then_inc(OB.filled, 1)

            def probT(t, k):
                if k == 0:
                    wait(pe, "edge_exp", t, NT, NT - 1)
                transposes(TA[k % 2], t, f"pT{k}", [att[:, j, k * P:(k + 1) * P] for j in range(NT)])

            def adj_transposed(t, k, par):
                transposes(HB[k % 2], t, f"adjT{k}", [adj[par][:, j, k * P:(k + 1) * P] for j in range(NT)])

            def step(tA, tB, tC, tD, par):
                if tB is not None:
                    adj_transposed(tB, 0, 1 - par)
                    adj_transposed(tB, 1, 1 - par)
                    wait(pe, "x1n", tB)
                    transposes(HB[1], tB, "x1T", [x1n[:, j, :] for j in range(NT)])
                    adj_transposed(tB, 2, 1 - par)
                    adj_transposed(tB, 3, 1 - par)
                    HB[1].wait_read(pe, tB, "x1T")
                    product(HB[0], tB, "route_h", rw1[:], x1nT[:])
                    layer1(tB, 0)
                if tA is not None:
                    wait(pe, "xn", tA)
                    transposes(TA[0], tA, "xT", [xn[:, j, :] for j in range(NT)])
                if tB is not None:
                    HB[0].wait_read(pe, tB, "route_h")
                    HB[1].wait_free(pe, tB, "logits")
                    for j in range(NT):
                        last = m.matmul(HB[1].tensor[:, j * PADW:(j + 1) * PADW], rh[:, j * P:(j + 1) * P],
                                        rw2[:], start=True, stop=True)
                    last.then_inc(HB[1].filled, 1)
                if tA is not None:
                    TA[0].wait_read(pe, tA, "xT")
                    wait_before(pe, "relu", tA, NT)
                    if tD is not None and not (isinstance(tD, int) and tD == 0):
                        RK.wait_read(pe, tD - 1, "ranks")
                    m.matmul(AJ.tensor[:], uj_bc[:], xnT[:], start=True, stop=True).then_inc(
                        AJ.filled, 1)
                    TA[1].wait_free(pe, tA, "ai")
                    for j in range(NT):
                        last = m.matmul(TA[1].tensor[:, j:j + 1], xnT[:, j * P:(j + 1) * P],
                                        u_col[:, 0:1], start=True, stop=True)
                    last.then_inc(TA[1].filled, 1)
                    ZB.wait_free(pe, tA, "z")
                    for j in range(NT):
                        last = m.matmul(ZB.tensor[:, j * P:(j + 1) * P], xnT[:, j * P:(j + 1) * P],
                                        gWT[:], start=True, stop=True)
                    last.then_inc(ZB.filled, 1)
                if tC is not None:
                    HC.wait_free(pe, tC, "agg")
                    wait(pe, "x2n", tC)
                    for k in range(NT):
                        m.matmul(HC.tensor[:], x2n[par][:, k, :], adjT[par][:, k, :],
                                 start=(k == 0), stop=False)
                        last = m.matmul(HC.tensor[:, k * P:(k + 1) * P], x2n[par][:, k, :],
                                        eps_ident[:], start=False, stop=(k == NT - 1))
                    last.then_inc(HC.filled, 1)
                if tB is not None:
                    layer2(tB, 0)
                if tC is not None:
                    HC.wait_read(pe, tC, "agg")
                    product(HC, tC, "m0", mw1[:, 0:P], hT[:])
                if tB is not None:
                    layer1(tB, 1)
                if tC is not None:
                    product(HC, tC, "m1", mw1[:, P:DH], hT[:])
                if tB is not None:
                    layer3(tB, 0)
                    layer2(tB, 1)
                if tD is not None:
                    RK.wait_free(pe, tD, "ranks")
                    if tA is not None:
                        wait(pe, "relu", tA, NT, NT - 1)
                    else:
                        wait(pe, "relu", G - 1, NT, NT - 1)
                    wait(pe, "earlier", tD)
                    m.matmul(RK.tensor[:, 0:8 * (NT + 1)], ones_b[:],
                             earlier[:].rearrange("p j e -> p (j e)"), start=True, stop=False)
                    m.matmul(RK.tensor[:, 0:8 * NT], tri[:], chosen_b[:].rearrange("p j e -> p (j e)"),
                             start=False, stop=True).then_inc(RK.filled, 1)
                if tC is not None:
                    HC.wait_free(pe, tC, "out")
                    for j in range(NT):
                        for c in range(2):
                            last = m.matmul(HC.tensor[:, j * P:(j + 1) * P],
                                            m1[:, c, j * P:(j + 1) * P], mw2[:, c, :],
                                            start=(c == 0), stop=(c == 1))
                    last.then_inc(HC.filled, 1)
                if tB is not None:
                    layer1(tB, 2)
                    OB.wait_free(pe, tB, "gateT")
                    wait(pe, "gate", tB)
                    for j in range(NT):
                        last = m.transpose(OB.tensor[0:8, j * P:(j + 1) * P], gate[:, j, :], ident[:])
                    last.then_inc(OB.filled, 1)
                    layer3(tB, 1)
                    layer2(tB, 2)
                if tA is not None:
                    probT(tA, 0)
                    probT(tA, 1)
                if tB is not None:
                    layer1(tB, 3)
                    OB.wait_read(pe, tB, "gateT")
                    OB.wait_free(pe, tB, "b3")
                    for j in range(NT):
                        last = m.matmul(OB.tensor[:, j * P:(j + 1) * P], gateT[0:E0, j * P:(j + 1) * P],
                                        eb3[:], start=True, stop=True)
                    last.then_inc(OB.filled, 1)
                    layer2(tB, 3)
                    layer3(tB, 2)
                if tA is not None:
                    probT(tA, 2)
                    probT(tA, 3)
                if tB is not None:
                    layer1(tB, 4)
                    layer3(tB, 3)
                if tA is not None:
                    ZB.wait_read(pe, tA, "z")
                    ZB.wait_free(pe, tA, "o")
                    for k in range(NT):
                        TA[k % 2].wait_read(pe, tA, f"pT{k}")
                        last = m.matmul(ZB.tensor[:], z[:, k, :], pT[:, k, :],
                                        start=(k == 0), stop=(k == NT - 1))
                    last.then_inc(ZB.filled, 1)
                if tB is not None:
                    layer2(tB, 4)
                    layer1(tB, 5)
                if tA is not None:
                    ZB.wait_read(pe, tA, "o")
                    transposes(TA[0], tA, "oT", [oT[:, j * P:(j + 1) * P] for j in range(NT)])
                if tC is not None:
                    wait(pe, "x3n", tC)
                    transposes(HC, tC, "x3T", [rows[0][:, j, 0:D] for j in range(NT)])
                if tB is not None:
                    layer3(tB, 4)
                    layer2(tB, 5)
                if tC is not None:
                    HC.wait_read(pe, tC, "x3T")
                    for j in range(NT):
                        last = m.matmul(HC.tensor[:, j * PADW:(j + 1) * PADW], x3T[:, j * P:(j + 1) * P],
                                        wr[:], start=True, stop=True)
                    last.then_inc(HC.filled, 1)
                if tB is not None:
                    layer3(tB, 5)

            iterations(pe, step)

            def tile_slot(s, u, r):
                i = tile_at(s, 0)
                if i is not None:
                    pe.wait_ge(tile_loaded[u], 16 * (r + 1))
                    if not (isinstance(i, int) and i < 2):
                        wait(pe, "tile_xg", i - 2)
                    for b in range(2):
                        last = m.transpose(XT[u % 2][:, b * P:(b + 1) * P], tile_rows[u][:, b, 0:D],
                                           ident[:])
                    last.then_inc(ready("tile_xT"), 1)
                i = tile_at(s, 2)
                if i is not None:
                    q = (u - 2) % 2
                    column = pe.value_load(column_of[0:1, bass.ds(i, 1)], min_val=0,
                                           max_val=2 * (E1 - 1))
                    wait(pe, "tile_hg", i)
                    if not (isinstance(i, int) and i < 2):
                        wait(pe, "tile_yb", i - 2)
                    for b in range(2):
                        for c in range(2):
                            last = m.matmul(YX[q][:, b * D:(b + 1) * D], hg[q][:, c, b * P:(b + 1) * P],
                                            fw2[:, bass.ds(column * P + c * D, D)],
                                            start=(c == 0), stop=(c == 1))
                    last.then_inc(ready("tile_y"), 1)
                i = tile_at(s, 1)
                if i is not None:
                    q = (u - 1) % 2
                    wait(pe, "tile_xg", i)
                    if not (isinstance(i, int) and i < 2):
                        wait(pe, "tile_hg", i - 2)
                    for c in range(2):
                        last = m.matmul(HX[q][:, c * TILE:(c + 1) * TILE],
                                        w1[q][:, c * P:(c + 1) * P], xg[q],
                                        start=True, stop=True)
                    last.then_inc(ready("tile_h"), 1)

            pe.wait_ge(ready("table"), 1)
            RK.wait_read(pe, G - 1, "ranks")
            slots(pe, tile_slot)

        @block.vector
        def _(dve):
            v = nc.vector

            dve.wait_ge(weights_loaded, WEIGHTS)
            dve.wait_ge(ready("ident"), 1)
            dve.wait_ge(ready("pool_const"), POOL_CONSTANTS)
            v.tensor_scalar(bwa[:], wa_col[:], bW_col[:], None, ALU.mult).then_inc(ready("bwa"), 1)
            v.tensor_scalar(eps_ident[:], ident[:], eps_bc[:], None, ALU.mult).then_inc(
                ready("eps_ident0"), 1)
            dve.wait_ge(ready("eps_ident0"), 1)
            v.tensor_tensor(eps_ident[:], eps_ident[:], ident[:], ALU.add)
            dve.wait_ge(ready("setup1"), 1)
            v.tensor_copy(gWT[:], HC.tensor[:, 0:D])
            v.tensor_copy(u_col[:], HC.tensor[:, D:D + 2]).then_inc(ready("u_col"), 1)
            dve.wait_ge(ready("u_col"), 1)
            v.tensor_scalar(uj_bc[:], ones[:], u_col[:, 1:2], None, ALU.mult)
            dve.wait_ge(ready("setup2"), 1)
            v.tensor_tensor(c_pair[:], AJ.tensor[:, 0:2], ba_bc[:], ALU.add).then_inc(ready("c_pair"), 1)
            dve.wait_ge(ready("c_pair"), 1)
            v.tensor_tensor(c_sum[:], c_pair[:, 0:1], c_pair[:, 1:2], ALU.add).then_inc(ready("c_sum"), 1)
            dve.wait_ge(ready("c_sum"), 1)
            v.tensor_scalar(c_relu[:], c_sum[:], 1.0 - SLOPE, None, ALU.mult)
            v.tensor_scalar(c_sink[:], c_sum[:], -SLOPE, SINK, ALU.mult, ALU.add).then_inc(
                ready("setup_done"), 1)
            dve.wait_ge(ready("setup_done"), 1)

            def x3_of(g):
                return x3[:, g, :, :] if isinstance(g, int) else x3[:, bass.ds(g, 1), :, :].squeeze(1)

            v.memset(earlier_f[:, 0, :], 0.0)

            def stats(s, t, x):
                for j in range(NT):
                    last = v.bn_stats(bn[s][:, j, :], x[:, j, :])
                last.then_inc(ready(f"bn_{s}"), 1)
                wait(dve, f"bn_{s}", t)
                apart(dve)
                for j in range(NT):
                    last = v.bn_aggr(mv[s][:, j, :], bn[s][:, j, :])
                last.then_inc(ready(f"stats_{s}"), 1)

            def normalise(s, t, x, dst, name):
                wait(dve, f"rstd_{s}", t)
                for j in range(NT):
                    last = v.tensor_scalar(dst[:, j, 0:D], x[:, j, :], mv[s][:, j, 0:1],
                                           rstd[s][:, j:j + 1], ALU.subtract, ALU.mult)
                last.then_inc(ready(name), 1)

            def choose_two(r, t, values):
                apart(dve)
                for j in range(NT):
                    last = v.max(best[r][:, j, :], values[:, j, :])
                last.then_inc(ready(f"best_{r}"), 1)
                wait(dve, f"best_{r}", t)
                v.tensor_tensor(wgap[r][:], best[r][:, :, 1], best[r][:, :, 0], ALU.subtract).then_inc(
                    ready(f"wgap_{r}"), 1)
                for j in range(NT):
                    last = v.max_index(best_i[r][:, j, :], best[r][:, j, :], values[:, j, :])
                last.then_inc(ready(f"best_i_{r}"), 1)
                wait(dve, f"best_i_{r}", t)
                v.tensor_copy(best_f[r][:], best_i[r][:, :, 0:2].rearrange("p j k -> p k j")).then_inc(
                    ready(f"best_f_{r}"), 1)
                wait(dve, f"best_f_{r}", t)
                for c in range(2):
                    last = v.tensor_tensor(hot[r][:, c, :, :], bc(iota8[:], 1, NT),
                                           bc(best_f[r][:, c, :], 2, 8), ALU.is_equal)
                last.then_inc(ready(f"hot_{r}"), 1)

            def weigh_two(r, t):
                wait(dve, f"wexp_{r}", t)
                v.tensor_scalar(wden[r][:], wexp[r][:], 1.0, None, ALU.add).then_inc(
                    ready(f"wden_{r}"), 1)
                wait(dve, f"wden_{r}", t)
                v.reciprocal(w01[r][:, 0, :], wden[r][:]).then_inc(ready(f"w0_{r}"), 1)
                wait(dve, f"w0_{r}", t)
                v.tensor_tensor(w01[r][:, 1, :], wexp[r][:], w01[r][:, 0, :], ALU.mult).then_inc(
                    ready(f"w1_{r}"), 1)
                wait(dve, f"w1_{r}", t)
                wait(dve, f"hot_{r}", t)

            def add_expert(t, e, pb):
                OB.wait_full(dve, t, f"e{e}")
                if e == 0:
                    wait(dve, "gate", t)
                else:
                    OB.wait_read(dve, t, OB.uses[OB.uses.index(f"e{e}") - 1])
                for j in range(NT):
                    last = v.scalar_tensor_tensor(
                        out=x2[pb][:, j, :], in0=OB.tensor[:, j * P:(j + 1) * P],
                        scalar=gate[:, j, e:e + 1], in1=(x1 if e == 0 else x2)[pb][:, j, :],
                        op0=ALU.mult, op1=ALU.add)
                last.then_inc(OB.drained, 1)

            def step(tA, tB, tC, tD, par):
                pb = 1 - par
                if tA is not None:
                    dve.wait_ge(x0_loaded[par], 16 * (tA // 2 + 1) if isinstance(tA, int)
                                else 8 * (tA - par) + 16)
                    stats("A", tA, x0[par])
                if tC is not None:
                    normalise("C", tC, x2[par], x2n[par], "x2n")
                if tA is not None:
                    dve.wait_ge(adj_loaded[par], 16 * (tA // 2 + 1) if isinstance(tA, int)
                                else 8 * (tA - par) + 16)
                    v.tensor_scalar(pen[:], adj[par][:], 0.0, MASKED, ALU.is_le, ALU.mult).then_inc(
                        ready("pen"), 1)
                    normalise("A", tA, x0[par], xn, "xn")
                if tD is not None:
                    HC.wait_read(dve, tD, "logits1")
                    choose_two("D", tD, logits1)
                if tB is not None:
                    HB[1].wait_full(dve, tB, "logits")
                    v.tensor_tensor(lg[:], HB[1].tensor[:, 0:NT * PADW].rearrange(
                        "p (j e) -> p j e", e=PADW)[:, :, 0:E0], bc(rb2_bc[:], 1, NT), ALU.add).then_inc(
                        HB[1].drained, 1)
                    HB[1].wait_read(dve, tB, "logits")
                    v.tensor_reduce(lg_max[:], lg[:], AX.X, ALU.max).then_inc(ready("lg_max"), 1)
                    wait(dve, "lg_max", tB)
                    v.tensor_tensor(lg[:], lg[:], bc(lg_max[:], 2, E0), ALU.subtract).then_inc(
                        ready("lg_centred"), 1)
                if tA is not None:
                    TA[1].wait_full(dve, tA, "ai")
                    v.tensor_scalar(relu_bias[:], TA[1].tensor[:, 0:NT], 1.0 - SLOPE, c_relu[:],
                                    ALU.mult, ALU.add).then_inc(ready("relu_bias"), 1)
                    v.tensor_scalar(sink[:], TA[1].tensor[:, 0:NT], -SLOPE, c_sink[:],
                                    ALU.mult, ALU.add).then_inc(TA[1].drained, 1)
                    ZB.wait_full(dve, tA, "z")
                    v.tensor_tensor(z[:], ZB.tensor[:].rearrange("p (j d) -> p j d", d=D),
                                    bc(bW_bc[:], 1, NT), ALU.add).then_inc(ZB.drained, 1)
                if tB is not None:
                    wait(dve, "lg_exp", tB)
                    v.tensor_reduce(lg_sum[:], prob[:, :, 0:E0], AX.X, ALU.add).then_inc(ready("lg_sum"), 1)
                    wait(dve, "lg_sum", tB)
                    v.reciprocal(lg_rsum[:], lg_sum[:]).then_inc(ready("lg_rsum"), 1)
                    wait(dve, "lg_rsum", tB)
                    v.tensor_tensor(prob[:, :, 0:E0], prob[:, :, 0:E0], bc(lg_rsum[:], 2, E0),
                                    ALU.mult).then_inc(ready("prob"), 1)
                    wait(dve, "prob", tB)
                    choose_two("B", tB, prob)
                if tD is not None:
                    weigh_two("D", tD)
                    v.tensor_tensor(chosen[:], hot["D"][:, 0, :, :], hot["D"][:, 1, :, :],
                                    ALU.add).then_inc(ready("chosen"), 1)
                    wait(dve, "chosen", tD)
                    v.tensor_copy(chosen_b[:], chosen[:])
                    for j in range(NT):
                        v.tensor_tensor(earlier_f[:, j + 1, :], earlier_f[:, j, :], chosen[:, j, :],
                                        ALU.add).then_inc(ready("earlier_f"), 1)
                        wait(dve, "earlier_f", tD, NT, j)
                    v.tensor_copy(earlier[:], earlier_f[:]).then_inc(ready("earlier"), 1)
                    wait(dve, "row1_features", tD)
                    for k in range(2):
                        v.tensor_copy(rows[k][:, :, PLACE].bitcast(U32), place[:, k, :])
                        last = v.tensor_copy(rows[k][:, :, WEIGHT], w01["D"][:, k, :])
                    last.then_inc(ready("rows_ready"), 1)
                    wait(dve, "rows_ready", tD)
                    v.tensor_scalar(place[:], place[:], float(2 * N), None, ALU.add).then_inc(
                        ready("place"), 1)
                if tA is not None:
                    for j in range(NT):
                        wait(dve, "relu", tA, NT, j)
                        wait(dve, "pen_aj", tA, NT, j)
                        apart(dve)
                        last = v.tensor_tensor_reduce(att[:, j, :], att[:, j, :], pen[:, j, :], 1.0, MASKED,
                                                      ALU.add, ALU.max, row_max[:, j:j + 1])
                    last.then_inc(ready("row_max"), 1)
                if tB is not None:
                    weigh_two("B", tB)
                    for c in range(2):
                        last = v.tensor_tensor(hotw[:, c, :, :], hot["B"][:, c, :, :],
                                               bc(w01["B"][:, c, :], 2, 8), ALU.mult)
                    last.then_inc(ready("hotw"), 1)
                if tA is not None:
                    wait(dve, "row_max", tA)
                    v.tensor_tensor(top[:], row_max[:], sink[:], ALU.max).then_inc(ready("top"), 1)
                if tB is not None:
                    wait(dve, "hotw", tB)
                    v.tensor_tensor(gate[:], hotw[:, 0, :, :], hotw[:, 1, :, :], ALU.add).then_inc(
                        ready("gate"), 1)
                if tA is not None:
                    wait(dve, "top", tA)
                    v.tensor_scalar(neg_max[:], top[:], -1.0, None, ALU.mult).then_inc(ready("neg_max"), 1)
                    wait(dve, "neg_max", tA)
                    v.tensor_tensor(sink_arg[:], sink[:], neg_max[:], ALU.add).then_inc(
                        ready("sink_arg"), 1)
                if tB is not None:
                    add_expert(tB, 0, pb)
                if tD is not None:
                    RK.wait_full(dve, tD, "ranks")
                    v.tensor_tensor(slot_of[:], RK.tensor[:, 0:8 * NT].rearrange("p (j e) -> p j e", e=8),
                                    bc(base[:], 1, NT), ALU.add).then_inc(ready("slot_of"), 1)
                    wait(dve, "slot_of", tD)
                    v.tensor_tensor(base[:], RK.tensor[:, 8 * NT:8 * (NT + 1)], base[:], ALU.add).then_inc(
                        RK.drained, 1)
                    for k in range(2):
                        last = v.tensor_tensor(slot_hot[:, k, :, :], slot_of[:], hot["D"][:, k, :, :],
                                               ALU.mult)
                    last.then_inc(ready("slot_hot"), 1)
                    wait(dve, "slot_hot", tD)
                    v.tensor_reduce(slot_f[:], slot_hot[:], AX.X, ALU.add).then_inc(ready("slot_f"), 1)
                    wait(dve, "slot_f", tD)
                    v.tensor_copy(slot[:], slot_f[:]).then_inc(ready("slot"), 1)
                if tC is not None:
                    HC.wait_full(dve, tC, "out")
                    wait(dve, "x2b", tC)
                    v.tensor_tensor(x3_of(tC), HC.tensor[:].rearrange("p (j d) -> p j d", d=D), x2b[:],
                                    ALU.add).then_inc(HC.drained, 1)
                    HC.wait_read(dve, tC, "out")
                    apart(dve)
                    stats("D", tC, x3_of(tC))
                if tB is not None:
                    add_expert(tB, 1, pb)
                if tC is not None:
                    normalise("D", tC, x3_of(tC), x3n, "x3_outer")
                    wait(dve, "x3_outer", tC)
                    stats("E", tC, x3n)
                if tB is not None:
                    OB.wait_full(dve, tB, "b3")
                    OB.wait_read(dve, tB, "e1")
                    v.tensor_tensor(x2[pb][:], OB.tensor[:].rearrange("p (j d) -> p j d", d=D),
                                    x2[pb][:], ALU.add).then_inc(OB.drained, 1)
                    add_expert(tB, 2, pb)
                if tC is not None:
                    if not (isinstance(tC, int) and tC == 0):
                        dve.wait_ge(rows_sent, 16 * 2 * NT * tC)
                    normalise("E", tC, x3n, rows[0], "x3n")
                if tA is not None:
                    wait(dve, "edge_exp", tA, NT, NT - 1)
                    wait(dve, "sink_exp", tA)
                    v.tensor_tensor(den[:], row_sum[:], sink_exp[:], ALU.add).then_inc(ready("den"), 1)
                    wait(dve, "den", tA)
                    v.reciprocal(rden[:], den[:]).then_inc(ready("rden"), 1)
                if tB is not None:
                    add_expert(tB, 3, pb)
                if tA is not None:
                    TA[0].wait_full(dve, tA, "oT")
                    wait(dve, "rden", tA)
                    for j in range(NT):
                        last = v.scalar_tensor_tensor(
                            out=x1[par][:, j, :], in0=TA[0].tensor[:, j * P:(j + 1) * P],
                            scalar=rden[:, j:j + 1], in1=x0[par][:, j, :], op0=ALU.mult, op1=ALU.add)
                    last.then_inc(TA[0].drained, 1)
                    TA[0].wait_read(dve, tA, "oT")
                    stats("B", tA, x1[par])
                if tB is not None:
                    add_expert(tB, 4, pb)
                if tA is not None:
                    normalise("B", tA, x1[par], x1n, "x1n")
                if tC is not None:
                    HC.wait_full(dve, tC, "logits1")
                    v.tensor_tensor(logits1[:], HC.tensor[:, 0:NT * PADW].rearrange(
                        "p (j e) -> p j e", e=PADW)[:, :, 0:E1], bc(br_bc[:], 1, NT), ALU.add).then_inc(
                        HC.drained, 1)
                if tB is not None:
                    add_expert(tB, 5, pb)
                    OB.wait_read(dve, tB, "e5")
                    stats("C", tB, x2[pb])

            iterations(dve, step)

            def then(step, instruction):
                instruction.then_inc(ready("table_step"), 1)
                dve.wait_ge(ready("table_step"), step)

            RK.wait_read(dve, G - 1, "ranks")
            v.tensor_copy(filled_to[:], base[0:1, :])
            then(1, v.tensor_tensor(count[:], base[0:1, :], iota_region[0:1, :], ALU.subtract))
            then(2, v.tensor_scalar(count[:], count[:], float(TILE - 1), None, ALU.add))
            then(3, v.tensor_copy(count_i[:], count[:]))
            then(4, v.tensor_scalar(tiles_i[:], count_i[:], TILE.bit_length() - 1, None,
                                            ALU.arith_shift_right))
            then(5, v.tensor_copy(tiles[:], tiles_i[:]))
            then(6, v.tensor_copy(ends[0][:], tiles[:]))
            for n, by in enumerate((1, 2, 4)):
                v.tensor_copy(ends[n + 1][:, 0:by], ends[n][:, 0:by])
                then(7 + n, v.tensor_tensor(ends[n + 1][:, by:E1], ends[n][:, by:E1],
                                                     ends[n][:, 0:E1 - by], ALU.add))
            then(10, v.tensor_tensor(passed[:], bc(iota_tile[:], 2, E1), bc(ends[3][:], 1, TILES),
                                           ALU.is_ge))
            then(11, v.tensor_tensor(behind[:], passed[:], bc(tiles[:], 1, TILES), ALU.mult))
            then(12, v.tensor_reduce(expert_f[:], passed[:], AX.X, ALU.add))
            then(13, v.tensor_reduce(first[:], behind[:], AX.X, ALU.add))
            then(14, v.tensor_tensor(inside[:], iota_tile[:], first[:], ALU.subtract))
            then(15, v.tensor_scalar(inside[:], inside[:], float(TILE), None, ALU.mult))
            then(16, v.scalar_tensor_tensor(out=row0_f[:], in0=expert_f[:], scalar=float(CAP),
                                                in1=inside[:], op0=ALU.mult, op1=ALU.add))
            then(17, v.tensor_scalar(column_f[:], expert_f[:], float(E1 - 1), 2.0, ALU.min, ALU.mult))
            v.tensor_copy(row0_of[:], row0_f[:])
            v.tensor_copy(column_of[:], column_f[:]).then_inc(ready("table"), 1)
            dve.wait_ge(ready("table"), 1)

            def tile_slot(s, u, r):
                i = tile_at(s, 0)
                if i is not None:
                    column = dve.value_load(column_of[0:1, bass.ds(i, 1)], min_val=0,
                                            max_val=2 * (E1 - 1))
                    if not (isinstance(i, int) and i < 2):
                        wait(dve, "tile_h", i - 2)
                        apart(dve)
                    v.tensor_copy(w1[u % 2], fw1[:, bass.ds(column * P, HE)])
                    wait(dve, "tile_xT", i)
                    v.tensor_scalar(xg[u % 2], XT[u % 2][:, 0:TILE], gamma[:], beta[:], ALU.mult,
                                    ALU.add).then_inc(ready("tile_xg"), 1)
                i = tile_at(s, 2)
                if i is not None:
                    q = (u - 2) % 2
                    column = dve.value_load(column_of[0:1, bass.ds(i, 1)], min_val=0,
                                            max_val=2 * (E1 - 1))
                    wait(dve, "tile_y", i)
                    if not (isinstance(i, int) and i < 2):
                        wait(dve, "tile_yw", i - 2)
                    v.tensor_tensor(yb[q].rearrange("p (b d) -> p b d", b=2),
                                    YX[q][:, 0:2 * D].rearrange("p (b d) -> p b d", b=2),
                                    bc(fb2_bc[:, bass.ds(column * (D // 2), D)], 1, 2),
                                    ALU.add).then_inc(ready("tile_yb"), 1)

            slots(dve, tile_slot)

            def add_pair(g, par):
                dve.wait_ge(pair_loaded[par], 16 * (g // 2 + 1) if isinstance(g, int)
                            else 8 * (g - par) + 16)
                if not (isinstance(g, int) and g < 2):
                    dve.wait_ge(out_stored[par], 16 * (g // 2) if isinstance(g, int)
                                else 8 * (g - par))
                v.tensor_tensor(fin[par], pair[par][:, :, 0:D], x3_of(g), ALU.add).then_inc(
                    ready("fin_part"), 1)
                wait(dve, "fin_part", g)
                v.tensor_tensor(fin[par], fin[par], pair[par][:, :, D:2 * D], ALU.add).then_inc(
                    ready("fin"), 1)

            add_pair(0, 0)
            add_pair(1, 1)
            with dve.Fori(1, G // 2) as i:
                for par in range(2):
                    add_pair(2 * i + par, par)


_INS = ['x', 'adj', 'L0_gnn_W', 'L0_gnn_bW', 'L0_gnn_wai', 'L0_gnn_bai', 'L0_gnn_waj', 'L0_gnn_baj',
        'L0_ffn_router_w1', 'L0_ffn_router_b1', 'L0_ffn_router_w2', 'L0_ffn_router_b2',
        'L0_ffn_expert_w1', 'L0_ffn_expert_b1', 'L0_ffn_expert_w2', 'L0_ffn_expert_b2',
        'L0_ffn_expert_w3', 'L0_ffn_expert_b3', 'L1_gnn_eps', 'L1_gnn_W1', 'L1_gnn_b1', 'L1_gnn_W2',
        'L1_gnn_b2', 'L1_ffn_gamma', 'L1_ffn_beta', 'L1_ffn_Wr', 'L1_ffn_br', 'L1_ffn_W1',
        'L1_ffn_b1', 'L1_ffn_W2', 'L1_ffn_b2']


def kernel(**inputs):
    import numpy as _np
    import concourse.bacc as _bacc
    from concourse import mybir as _mybir
    from concourse.bass_utils import run_bass_kernel_spmd as _run

    nc = _bacc.Bacc("TRN2", target_bir_lowering=False, num_devices=1)
    arrays, args = {}, {}
    for name in _INS:
        a = _np.ascontiguousarray(inputs[name])
        arrays[f"in_{name}"] = a
        args[name] = nc.dram_tensor(f"in_{name}", a.shape, _mybir.dt.from_np(a.dtype),
                                    kind="ExternalInput").ap()
    out = nc.dram_tensor("result", (G, N, D), _mybir.dt.float32, kind="ExternalOutput").ap()
    build(nc, args, out)
    r = _run(nc, [arrays], core_ids=[0])
    return r.results[0]["result"]
```

```python
from contextlib import ExitStack

import concourse.bass as bass
from concourse import mybir

F32 = mybir.dt.float32
U32 = mybir.dt.uint32
I32 = mybir.dt.int32
BF16 = mybir.dt.bfloat16
ALU = mybir.AluOpType
ACT = mybir.ActivationFunctionType
AX = mybir.AxisListType

P = 128
G, N, D = 16, 512, 128
NT = N // P
E0 = 6
RH = 64
DH = 256
E1 = 8
SLOPE = 0.2
MASKED = -9.0e15
SINK = -1.0e9
LN_EPS = 1e-5
HE = 256
NODES = G * N
TILE = 2 * P
CAP = NODES + TILE
SPARE = E1 * CAP
ROW = D + 2
PLACE, WEIGHT = D, D + 1
TILES = 2 * NODES // TILE + E1
IDLE = E1
LAG = 3
UNROLL = 8
DEEP = 4
PADW = 96


class Bank:

    def __init__(self, tensor, filled, drained, uses):
        self.tensor, self.filled, self.drained, self.uses = tensor, filled, drained, uses

    def wait_free(self, eng, t, use):
        k = self.uses.index(use)
        n = t * len(self.uses) + k
        if isinstance(n, int) and n == 0:
            return
        eng.wait_ge(self.drained, n)

    def wait_read(self, eng, t, use):
        eng.wait_ge(self.drained, t * len(self.uses) + self.uses.index(use) + 1)

    def wait_full(self, eng, t, use):
        eng.wait_ge(self.filled, t * len(self.uses) + self.uses.index(use) + 1)


def build(nc, a, out):
    with ExitStack() as ctx:
        def sb(name, shape, dt=F32):
            return ctx.enter_context(nc.sbuf_tensor(name, shape, dt))

        def sem(name):
            return ctx.enter_context(nc.semaphore(name))

        def bank(name, uses):
            t = ctx.enter_context(nc.psum_tensor(name + "_bank", [P, 512], F32))
            return Bank(t, sem(name + "_filled"), sem(name + "_drained"), uses)

        TA = [bank("ta0", ["pT0", "pT2", "x1T"]), bank("ta1", ["xT", "z1", "pT1", "pT3"])]
        AJ = bank("aj", ["aj"])
        ZB = bank("zb", ["z0", "o"])
        HB = [bank("hb0", ["adjT0", "adjT2", "route_h"] + [f"h1_{e}" for e in range(E0)]),
              bank("hb1", ["adjT1", "adjT3", "logits"] + [f"h2_{e}" for e in range(E0)])]
        OB = bank("ob", [f"e{e}" for e in range(E0)])
        HC = bank("hc", ["agg", "m0", "m1", "out", "x3T", "logits1"])
        RK = Bank(AJ.tensor, sem("rk_filled"), sem("rk_drained"), ["ranks"])
        GT = Bank(AJ.tensor, sem("gt_filled"), sem("gt_drained"), ["gateT", "b3"])

        z_banks = [(ZB, "z0"), (TA[1], "z1")]

        XT = [TA[0].tensor, TA[1].tensor]
        HX = [AJ.tensor, ZB.tensor]
        YX = [OB.tensor, HC.tensor]

        tri = sb("tri", [P, P], BF16)
        ones_b = sb("ones_b", [P, P], BF16)
        iota_region = sb("iota_region", [P, E1])
        iota_tile = sb("iota_tile", [1, TILES])
        gamma = sb("gamma", [P, 1])
        beta = sb("beta", [P, 1])
        wr = sb("wr", [P, PADW])
        br_bc = sb("br_bc", [P, E1])
        fw1 = sb("fw1", [P, E1 * HE])
        fw2 = sb("fw2", [P, E1 * HE])
        fb1 = sb("fb1", [P, E1 * HE // P])
        fb2_bc = sb("fb2_bc", [P, E1 * D])
        ident = sb("ident", [P, P])
        eps_ident = sb("eps_ident", [P, P])
        eps_tile = sb("eps_tile", [P, NT])
        minus_half = sb("minus_half", [P, NT])
        iota8 = sb("iota8", [P, 8])
        gW = sb("gW", [P, D])
        gWTu = sb("gWTu", [P, D + 1])
        bW_bc = sb("bW_bc", [P, D])
        bW_col = sb("bW_col", [P, 1])
        wa_col = sb("wa_col", [P, 2])
        ba_bc = sb("ba_bc", [P, 2])
        u_col = sb("u_col", [P, 2])
        uj_bc = sb("uj_bc", [P, P])
        bwa = sb("bwa", [P, 2])
        c_pair = sb("c_pair", [P, 2])
        c_sum = sb("c_sum", [P, 1])
        c_relu = sb("c_relu", [P, 1])
        c_sink = sb("c_sink", [P, 1])
        ones = sb("ones", [P, P])
        rw1 = sb("rw1", [P, RH])
        rb1 = sb("rb1", [RH, 1])
        rw2 = sb("rw2", [RH, PADW])
        rb2_bc = sb("rb2_bc", [P, E0])
        ew = [sb(f"ew{i}", [P, E0, D]) for i in (1, 2, 3)]
        eb1 = sb("eb1", [P, E0])
        eb2 = sb("eb2", [P, E0])
        eb3 = sb("eb3", [E0, D])
        eps_bc = sb("eps_bc", [P, 1])
        mw1 = sb("mw1", [P, DH])
        mb1 = sb("mb1", [P, 2])
        mw2 = sb("mw2", [P, 2, D])
        mb2_bc = sb("mb2_bc", [P, D])

        adj = [sb(f"adj{i}", [P, NT, N]) for i in range(2)]
        x0 = [sb(f"x0_{i}", [P, NT, D]) for i in range(2)]
        bn = {s: sb(f"bn_{s}", [P, NT, 6]) for s in "ABCDE"}
        mv = {s: sb(f"mv_{s}", [P, NT, 2]) for s in "ABCDE"}
        var_eps = {s: sb(f"ve_{s}", [P, NT]) for s in "ABCDE"}
        rstd = {s: sb(f"rstd_{s}", [P, NT]) for s in "ABCDE"}
        xn = sb("xn", [P, NT, D])
        xnT = sb("xnT", [P, N])
        z = sb("z", [P, NT, D])
        relu_bias = sb("relu_bias", [P, NT])
        sink = sb("sink", [P, NT])
        aj02 = sb("aj02", [P, N])
        pen = sb("pen", [P, NT, N])
        att = sb("att", [P, NT, N])
        row_max = sb("row_max", [P, NT])
        top = sb("top", [P, NT])
        neg_max = sb("neg_max", [P, NT])
        sink_arg = sb("sink_arg", [P, NT])
        sink_exp = sb("sink_exp", [P, NT])
        row_sum = sb("row_sum", [P, NT])
        den = sb("den", [P, NT])
        rden = sb("rden", [P, NT])
        pT = sb("pT", [P, NT, N])
        x1 = [sb(f"x1_{i}", [P, NT, D]) for i in range(2)]
        x1n = sb("x1n", [P, NT, D])
        x1nT = sb("x1nT", [P, N])
        adjT = [sb(f"adjT{i}", [P, NT, N]) for i in range(2)]
        rh = sb("rh", [RH, N])
        lg = sb("lg", [P, NT, E0])
        lg_max = sb("lg_max", [P, NT])
        lg_sum = sb("lg_sum", [P, NT])
        lg_rsum = sb("lg_rsum", [P, NT])
        prob = sb("prob", [P, NT, 8])
        best, best_i, best_f, wgap, wexp, wden, w01, hot = ({} for _ in range(8))
        for r in "BD":
            best[r] = sb(f"best_{r}", [P, NT, 8])
            best_i[r] = sb(f"best_i_{r}", [P, NT, 8], U32)
            best_f[r] = sb(f"best_f_{r}", [P, 2, NT])
            wgap[r] = sb(f"wgap_{r}", [P, NT])
            wexp[r] = sb(f"wexp_{r}", [P, NT])
            wden[r] = sb(f"wden_{r}", [P, NT])
            w01[r] = sb(f"w01_{r}", [P, 2, NT])
            hot[r] = sb(f"hot_{r}", [P, 2, NT, 8])
        hotw = sb("hotw", [P, 2, NT, 8])
        gate = sb("gate", [P, NT, 8])
        gateT = sb("gateT", [8, N])
        h1 = [sb(f"h1_{i}", [P, N]) for i in range(2)]
        h2 = [sb(f"h2_{i}", [P, N]) for i in range(2)]
        x2 = [sb(f"x2_{i}", [P, NT, D]) for i in range(2)]
        x2n = [sb(f"x2n_{i}", [P, NT, D]) for i in range(2)]
        x2b = sb("x2b", [P, NT, D])
        hT = sb("hT", [P, N])
        m1 = sb("m1", [P, 2, N])
        x3 = sb("x3", [P, G, NT, D])
        x3n = sb("x3n", [P, NT, D])
        rows = [[sb(f"rows{k}_{i}", [P, NT, ROW]) for i in range(2)] for k in range(2)]
        x3T = sb("x3T", [P, N])
        logits1 = sb("logits1", [P, NT, 8])
        chosen = sb("chosen", [P, NT, 8])
        earlier = sb("earlier", [P, NT + 1, 8], BF16)
        chosen_b = sb("chosen_b", [P, NT, 8], BF16)
        earlier_f = sb("earlier_f", [P, NT + 1, 8])
        base = sb("base", [P, E1])
        slot_of = sb("slot_of", [P, NT, 8])
        slot_hot = sb("slot_hot", [P, 2, NT, 8])
        slot_f = sb("slot_f", [P, 2, NT])
        slot = sb("slot", [P, 2, NT], U32)
        place = sb("place", [P, 2, NT])
        filling = [b[:].rearrange("p j m -> p (j m)")[:, 0:4 * 2 * ROW].rearrange(
            "p (e b r) -> p e b r", b=2, r=ROW) for b in (adj[0], adj[1], pen, att)]
        filled_to = sb("filled_to", [1, E1], I32)
        count = sb("count", [1, E1])
        count_i = sb("count_i", [1, E1], I32)
        tiles_i = sb("tiles_i", [1, E1], I32)
        tiles = sb("tiles", [1, E1])
        ends = [sb(f"ends{i}", [1, E1]) for i in range(4)]
        passed, passed_tiles = (
            pT[0:1, k:k + 2, :].rearrange("p j m -> p (j m)")[:, 0:TILES * E1].rearrange(
                "p (t e) -> p t e", e=E1) for k in (0, 2))
        expert_f = sb("expert_f", [1, TILES])
        first = sb("first", [1, TILES])
        inside = sb("inside", [1, TILES])
        row0_f = sb("row0_f", [1, TILES])
        column_f = sb("column_f", [1, TILES])
        column_of = sb("column_of", [1, TILES], I32)
        row0_of = sb("row0_of", [1, TILES], I32)
        tile_rows = [sb(f"tile_rows{i}", [P, 2, ROW]) for i in range(UNROLL)]
        xg, yb = ([pT[:, k, i * TILE:(i + 1) * TILE] for i in range(2)] for k in (0, 1))
        hg = [pT[:, 2 + i, :].rearrange("p (c r) -> p c r", c=2) for i in range(2)]
        w1 = [adjT[1][:, 0, i * HE:(i + 1) * HE] for i in range(2)]
        adjT_flat = adjT[0][:].rearrange("p j m -> p (j m)")
        yw = [adjT_flat[:, i * 2 * D:(i + 1) * 2 * D].rearrange("p (b d) -> p b d", b=2)
              for i in range(UNROLL)]
        pair = [b[:, 2 * h:2 * h + 2, :].rearrange("p a (b d) -> p (a b) d", d=2 * D)
                for b in adj for h in range(2)]
        fin = [b[:, h, :].rearrange("p (j d) -> p j d", d=D) for b in adjT for h in range(2)]
        sent = nc.dram_tensor("sent", (E1 * CAP + IDLE * TILE, ROW), F32, kind="Internal").ap()
        result2 = nc.dram_tensor("result2", (2 * NODES + (E1 + IDLE) * TILE, D), F32, kind="Internal").ap()

        S = {}

        def ready(name):
            if name not in S:
                S[name] = sem(name)
            return S[name]

        adj_loaded = [sem(f"adj_loaded{i}") for i in range(2)]
        x0_loaded = [sem(f"x0_loaded{i}") for i in range(2)]
        attention_loaded = sem("attention_loaded")
        weights_loaded = sem("weights_loaded")
        rows_sent = sem("rows_sent")
        spare_sent = sem("spare_sent")
        idle_sent = sem("idle_sent")
        tile_loaded = [sem(f"tile_loaded{i}") for i in range(UNROLL)]
        result_sent = [sem(f"result_sent{i}") for i in range(UNROLL)]
        pair_loaded = [sem(f"pair_loaded{i}") for i in range(DEEP)]
        out_stored = [sem(f"out_stored{i}") for i in range(DEEP)]

        x_d = a["x"].rearrange("g (j p) d -> g p j d", p=P)
        adj_d = a["adj"].rearrange("g (j p) m -> g p j m", p=P)
        out_d = out.rearrange("g (j p) d -> g p j d", p=P)

        def col(ap):
            return ap.rearrange("(p a) -> p a", a=1)

        attention_loads = [
            (gW[:], a["L0_gnn_W"]),
            (bW_bc[:], a["L0_gnn_bW"].partition_broadcast(P)),
            (bW_col[:], col(a["L0_gnn_bW"])),
            (wa_col[:, 0:1], a["L0_gnn_wai"].rearrange("a p -> p a")),
            (wa_col[:, 1:2], a["L0_gnn_waj"].rearrange("a p -> p a")),
            (ba_bc[:, 0:1], a["L0_gnn_bai"].partition_broadcast(P)),
            (ba_bc[:, 1:2], a["L0_gnn_baj"].partition_broadcast(P)),
            (eps_bc[:], a["L1_gnn_eps"].partition_broadcast(P)),
        ]
        loads = [
            (rw1[:], a["L0_ffn_router_w1"]),
            (rb1[:], col(a["L0_ffn_router_b1"])),
            (rw2[:, 0:E0], a["L0_ffn_router_w2"]),
            (rb2_bc[:], a["L0_ffn_router_b2"].partition_broadcast(P)),
            (ew[0][:], a["L0_ffn_expert_w1"].rearrange("e d h -> d e h")),
            (ew[1][:], a["L0_ffn_expert_w2"].rearrange("e d h -> d e h")),
            (ew[2][:], a["L0_ffn_expert_w3"].rearrange("e d h -> d e h")),
            (eb1[:], a["L0_ffn_expert_b1"].rearrange("e h -> h e")),
            (eb2[:], a["L0_ffn_expert_b2"].rearrange("e h -> h e")),
            (eb3[:], a["L0_ffn_expert_b3"]),
            (mw1[:], a["L1_gnn_W1"]),
            (mb1[:], a["L1_gnn_b1"].rearrange("(c p) -> p c", p=P)),
            (mw2[:], a["L1_gnn_W2"].rearrange("(c p) d -> p c d", p=P)),
            (mb2_bc[:], a["L1_gnn_b2"].partition_broadcast(P)),
            (gamma[:], col(a["L1_ffn_gamma"])),
            (beta[:], col(a["L1_ffn_beta"])),
            (wr[:, 0:E1], a["L1_ffn_Wr"]),
            (br_bc[:], a["L1_ffn_br"].partition_broadcast(P)),
            (fw1[:].rearrange("p (e h) -> p e h", e=E1), a["L1_ffn_W1"].rearrange("e d h -> d e h")),
            (fw2[:].rearrange("p (e c d) -> p e c d", e=E1, c=2),
             a["L1_ffn_W2"].rearrange("e (c p) d -> p e c d", p=P)),
            (fb1[:].rearrange("p (e c) -> p e c", c=2), a["L1_ffn_b1"].rearrange("e (c p) -> p e c", p=P)),
            (fb2_bc[:], a["L1_ffn_b2"].rearrange("e h -> (e h)").partition_broadcast(P)),
        ]
        ATTENTION_WEIGHTS = 16 * len(attention_loads)
        WEIGHTS = 16 * len(loads)
        POOL_CONSTANTS = 14

        def iterations(eng, step):
            step(0, None, None, None, None, 1)
            step(1, 0, None, None, None, 0)
            step(2, 1, 0, None, None, 1)
            step(3, 2, 1, 0, None, 0)
            step(4, 3, 2, 1, 0, 1)
            with eng.Fori(2, G // 2 - 1) as i:
                step(2 * i + 1, 2 * i, 2 * i - 1, 2 * i - 2, 2 * i - 3, 0)
                step(2 * i + 2, 2 * i + 1, 2 * i, 2 * i - 1, 2 * i - 2, 1)
            step(G - 1, G - 2, G - 3, G - 4, G - 5, 0)
            step(None, G - 1, G - 2, G - 3, G - 4, 1)
            step(None, None, G - 1, G - 2, G - 3, 0)
            step(None, None, None, G - 1, G - 2, 1)
            step(None, None, None, None, G - 1, 0)

        def wait(eng, name, t, per=1, k=0):
            eng.wait_ge(ready(name), t * per + k + 1)

        def wait_before(eng, name, t, per=1):
            if not (isinstance(t, int) and t == 0):
                eng.wait_ge(ready(name), t * per)

        def bc(ap, axis, n):
            shape = list(ap.shape)
            shape.insert(axis, n)
            return ap.unsqueeze(axis).broadcast_to(shape)

        def apart(eng):
            eng.nop(nofuse=True)

        def slots(eng, slot):
            for s in range(2 * UNROLL):
                slot(s, s % UNROLL, s // UNROLL)
            with eng.Fori(2, TILES // UNROLL) as r:
                for u in range(UNROLL):
                    slot(UNROLL * r + u, u, r)
            for s in range(TILES, TILES + LAG):
                slot(s, s % UNROLL, s // UNROLL)

        def turn_at(u, r, back):
            return r if u >= back else r - 1

        def tile_at(s, back):
            if isinstance(s, int) and not 0 <= s - back < TILES:
                return None
            return s - back

        block = ctx.enter_context(nc.Block())

        @block.sync
        def _(sp):
            def load(t, par):
                sp.dma_start(x0[par][:], x_d[t]).then_inc(x0_loaded[par], 16)
                sp.dma_start(adj[par][:], adj_d[t]).then_inc(adj_loaded[par], 16)

            for dst, src in attention_loads:
                sp.dma_start(dst, src, allow_slow_non_contiguous=True).then_inc(attention_loaded, 16)
            load(0, 0)
            load(1, 1)
            for dst, src in loads:
                sp.dma_start(dst, src, allow_slow_non_contiguous=True).then_inc(weights_loaded, 16)
            with sp.Fori(0, (G - 2) // 2) as i:
                for par in range(2):
                    t = 2 * i + 2 + par
                    ZB.wait_read(sp, t - 2, "o")
                    HB[1].wait_full(sp, t - 2, "adjT3")
                    load(t, par)

            sp.wait_ge(ready("filling"), 4)
            sp.wait_ge(ready("filled_to"), 1)
            for e in range(E1):
                end = sp.value_load(filled_to[0:1, e:e + 1], min_val=e * CAP, max_val=e * CAP + NODES)
                sp.dma_start(sent[bass.ds(end, TILE), :].rearrange("(p b) r -> p b r", b=2),
                             filling[e // 4][:, e % 4, :, :]).then_inc(spare_sent, 16)
            sp.wait_ge(ready("table"), 1)
            sp.wait_ge(rows_sent, 16 * 2 * NT * G)
            sp.wait_ge(spare_sent, 16 * E1)
            sp.wait_ge(idle_sent, 16 * 2)

            def tile(i, q, r):
                row0 = sp.value_load(row0_of[0:1, bass.ds(i, 1)], min_val=0,
                                     max_val=SPARE + (IDLE - 1) * TILE)
                if not (isinstance(r, int) and r == 0):
                    sp.wait_ge(result_sent[q], 32 * r)
                sp.dma_start(tile_rows[q][:], sent[bass.ds(row0, TILE), :].rearrange(
                    "(p b) r -> p b r", b=2)).then_inc(tile_loaded[q], 16)

            for q in range(UNROLL):
                tile(q, q, 0)
            with sp.Fori(1, TILES // UNROLL) as r:
                for q in range(UNROLL):
                    tile(UNROLL * r + q, q, r)

            for q in range(UNROLL):
                sp.wait_ge(result_sent[q], 32 * (TILES // UNROLL))
            pairs = result2[0:2 * NODES, :].rearrange("(g j p k) d -> g p j (k d)", j=NT, p=P, k=2)

            def load_pair(g, n):
                sp.dma_start(pair[n], pairs[g]).then_inc(pair_loaded[n], 16)

            def store(g, n):
                wait(sp, "fin", g)
                sp.dma_start(out_d[g], fin[n]).then_inc(out_stored[n], 16)

            for n in range(DEEP):
                load_pair(n, n)
            with sp.Fori(0, G // DEEP - 1) as i:
                for n in range(DEEP):
                    store(DEEP * i + n, n)
                    load_pair(DEEP * i + n + DEEP, n)
            for n in range(DEEP):
                store(G - DEEP + n, n)
            for n in range(DEEP):
                sp.wait_ge(out_stored[n], 16 * (G // DEEP))

        @block.gpsimd
        def _(pool):
            g = nc.gpsimd
            g.memset(ident[:], 0.0).then_inc(ready("ident0"), 1)
            g.memset(minus_half[:], -0.5).then_inc(ready("pool_const"), 1)
            g.memset(ones[:], 1.0).then_inc(ready("pool_const"), 1)
            g.memset(prob[:], -1.0).then_inc(ready("pool_const"), 1)
            g.iota(iota8[:], pattern=[[1, 8]], base=0, channel_multiplier=0,
                   allow_small_or_imprecise_dtypes=True).then_inc(ready("pool_const"), 1)
            g.memset(tri[:], 1.0).then_inc(ready("ident0"), 1)
            g.memset(ones_b[:], 1.0).then_inc(ready("pool_const"), 1)
            g.memset(eps_tile[:], LN_EPS).then_inc(ready("pool_const"), 1)
            g.memset(rw2[:, E0:PADW], 0.0).then_inc(ready("pool_const"), 1)
            g.memset(wr[:, E1:PADW], 0.0).then_inc(ready("pool_const"), 1)
            for dst, pattern, start, by_partition in (
                    (iota_region[:], [[CAP, E1]], 0, 0), (place[:, 0, :], [[2 * P, NT]], 0, 2),
                    (place[:, 1, :], [[2 * P, NT]], 1, 2), (base[:], [[CAP, E1]], 0, 0),
                    (iota_tile[:], [[1, TILES]], 0, 0)):
                g.iota(dst, pattern=pattern, base=start, channel_multiplier=by_partition,
                       allow_small_or_imprecise_dtypes=True).then_inc(ready("pool_const"), 1)
            pool.wait_ge(ready("ident0"), 2)
            g.affine_select(out=tri[:], in_=tri[:], compare_op=ALU.is_gt, fill=0.0, base=0,
                            pattern=[[1, P]], channel_multiplier=-1).then_inc(ready("pool_const"), 1)
            g.affine_select(out=ident[:], in_=ident[:], compare_op=ALU.not_equal, fill=1.0, base=0,
                            pattern=[[-1, P]], channel_multiplier=1).then_inc(ready("ident"), 1)
            pool.wait_ge(ready("pool_const"), POOL_CONSTANTS)

            def inverse_std(s, t):
                wait(pool, f"stats_{s}", t)
                g.tensor_tensor(var_eps[s][:], mv[s][:, :, 1], eps_tile[:], ALU.add).then_inc(
                    ready(f"var_eps_{s}"), 1)
                wait(pool, f"var_eps_{s}", t)
                g.tensor_tensor(rstd[s][:], var_eps[s][:], minus_half[:], ALU.pow).then_inc(
                    ready(f"rstd_{s}"), 1)

            def make_filling():
                HB[1].wait_full(pool, G - 1, "adjT3")
                ZB.wait_read(pool, G - 1, "o")
                for n, buffer in enumerate(filling):
                    g.memset(buffer, 0.0).then_inc(ready("filling0"), 1)
                    pool.wait_ge(ready("filling0"), n + 1)
                    g.iota(buffer[:, :, :, PLACE].bitcast(U32), pattern=[[TILE, 4], [1, 2]],
                           base=2 * NODES + n * 4 * TILE, channel_multiplier=2).then_inc(ready("filling"), 1)
                pool.wait_ge(ready("filling"), 4)
                for n in range(2):
                    g.dma_start(sent[SPARE + n * 4 * TILE:SPARE + (n + 1) * 4 * TILE, :].rearrange(
                        "(e p b) r -> p e b r", p=P, b=2), filling[2 + n]).then_inc(idle_sent, 16)

            moves = [(k, j) for k in range(2) for j in range(NT)]

            def dispatch(par, moves):
                for k, j in moves:
                    g.indirect_dma_start(sent, bass.IndirectOffsetOnAxis(slot[:, k, j:j + 1], 0),
                                         rows[k][par][:, j, :], None).then_inc(rows_sent, 16)

            def step(tN, tA, tB, tC, tD, par):
                if isinstance(tB, int) and tB == 0:
                    pool.wait_ge(weights_loaded, WEIGHTS)
                if isinstance(tC, int) and tC == G - 1:
                    make_filling()
                if tA is not None:
                    wait(pool, "pen", tA)
                    wait(pool, "aj02", tA)
                    for j in range(NT):
                        g.tensor_tensor(pen[:, j, :], pen[:, j, :], aj02[:], ALU.add).then_inc(
                            ready("pen_aj"), 1)
                if tB is not None:
                    HB[0].wait_read(pool, tB, "adjT2")
                    HB[1].wait_read(pool, tB, "adjT3")
                    for k in range(NT):
                        block_kk = adjT[1 - par][:, k, k * P:(k + 1) * P]
                        last = g.tensor_tensor(block_kk, block_kk, eps_ident[:], ALU.add)
                    last.then_inc(ready("diagonal"), 1)
                if tC is not None:
                    OB.wait_read(pool, tC, "e5")
                    HC.wait_free(pool, tC, "agg")
                    for j in range(NT):
                        last = g.tensor_tensor(x2b[:, j, :], x2[par][:, j, :], mb2_bc[:], ALU.add)
                    last.then_inc(ready("x2b"), 1)
                if tD is not None:
                    wait(pool, "slot", tD)
                    wait(pool, "rows_ready", tD)
                    apart(pool)
                    dispatch(1 - par, moves[:3])
                if tC is not None:
                    inverse_std("D", tC)
                if tN is not None:
                    inverse_std("A", tN)
                if tD is not None:
                    dispatch(1 - par, moves[3:4])
                if tC is not None:
                    inverse_std("E", tC)
                if tD is not None:
                    dispatch(1 - par, moves[4:])
                if tA is not None:
                    inverse_std("B", tA)
                if tB is not None:
                    inverse_std("C", tB)

            iterations(pool, step)

            def send_slot(s, u, r):
                i = tile_at(s, 3)
                if i is None:
                    return
                q = (u - 3) % UNROLL
                wait(pool, "tile_yw", i)
                apart(pool)
                for b in range(2):
                    g.indirect_dma_start(
                        result2, bass.IndirectOffsetOnAxis(
                            tile_rows[q][:, b, PLACE:PLACE + 1].bitcast(U32), 0),
                        yw[q][:, b, :], None).then_inc(result_sent[q], 16)

            slots(pool, send_slot)

        @block.scalar
        def _(act):
            s = nc.scalar
            act.wait_ge(attention_loaded, ATTENTION_WEIGHTS)

            def drain(bk, t, use, dst, func=ACT.Copy, src=None, **kw):
                bk.wait_full(act, t, use)
                s.activation(dst, bk.tensor[:] if src is None else src, func, **kw).then_inc(
                    bk.drained, 1)

            def hidden1(t, e):
                drain(HB[0], t, f"h1_{e}", h1[e % 2][:], ACT.Relu, bias=eb1[:, e:e + 1])

            def edge_relu(j):
                s.activation(att[:, j, :], AJ.tensor[:], ACT.Relu, bias=relu_bias[:, j:j + 1],
                             scale=1.0 - SLOPE).then_inc(ready("relu"), 1)

            def edge_exp(j):
                s.activation(att[:, j, :], att[:, j, :], ACT.Exp, bias=neg_max[:, j:j + 1],
                             accum_out=row_sum[:, j:j + 1]).then_inc(ready("edge_exp"), 1)

            def hidden2(t, e):
                drain(HB[1], t, f"h2_{e}", h2[e % 2][:], ACT.Relu, bias=eb2[:, e:e + 1])

            def step(tN, tA, tB, tC, tD, par):
                if isinstance(tB, int) and tB == 0:
                    act.wait_ge(weights_loaded, WEIGHTS)
                if tB is not None:
                    for k in (0, 1):
                        drain(HB[k % 2], tB, f"adjT{k}", adjT[1 - par][:, k, :])
                if tA is not None:
                    drain(TA[1], tA, "xT", xnT[:])
                if tB is not None:
                    drain(HB[0], tB, "adjT2", adjT[1 - par][:, 2, :])
                    drain(TA[0], tB, "x1T", x1nT[:])
                if tA is not None:
                    AJ.wait_full(act, tA, "aj")
                    wait_before(act, "pen_aj", tA, NT)
                    s.activation(aj02[:], AJ.tensor[:], ACT.Copy, scale=SLOPE).then_inc(ready("aj02"), 1)
                    wait(act, "relu_bias", tA)
                    edge_relu(0)
                if tB is not None:
                    drain(HB[0], tB, "route_h", rh[:], ACT.Relu, src=HB[0].tensor[0:RH, :], bias=rb1[:])
                    drain(HB[1], tB, "adjT3", adjT[1 - par][:, 3, :])
                if tA is not None:
                    for j in (1, 2, 3):
                        edge_relu(j)
                if tD is not None:
                    wait(act, "wgap_D", tD)
                    s.activation(wexp["D"][:], wgap["D"][:], ACT.Exp).then_inc(ready("wexp_D"), 1)
                if tB is not None:
                    hidden1(tB, 0)
                if tB is not None:
                    wait(act, "lg_centred", tB)
                    s.activation(prob[:, :, 0:E0], lg[:], ACT.Exp).then_inc(ready("lg_exp"), 1)
                if tC is not None:
                    drain(HC, tC, "agg", hT[:])
                if tB is not None:
                    wait(act, "wgap_B", tB)
                    s.activation(wexp["B"][:], wgap["B"][:], ACT.Exp).then_inc(ready("wexp_B"), 1)
                    hidden2(tB, 0)
                if tC is not None:
                    drain(HC, tC, "m0", m1[:, 0, :], ACT.Relu, bias=mb1[:, 0:1])
                if tB is not None:
                    hidden1(tB, 1)
                if tC is not None:
                    drain(HC, tC, "m1", m1[:, 1, :], ACT.Relu, bias=mb1[:, 1:2])
                if tA is not None:
                    wait(act, "sink_arg", tA)
                    s.activation(sink_exp[:], sink_arg[:], ACT.Exp).then_inc(ready("sink_exp"), 1)
                    for j in (0, 1):
                        edge_exp(j)
                if tB is not None:
                    hidden2(tB, 1)
                if tA is not None:
                    for j in (2, 3):
                        edge_exp(j)
                if tB is not None:
                    hidden1(tB, 2)
                    drain(GT, tB, "gateT", gateT[:], src=GT.tensor[0:8, :])
                    hidden2(tB, 2)
                if tA is not None:
                    drain(TA[0], tA, "pT0", pT[:, 0, :])
                    drain(TA[1], tA, "pT1", pT[:, 1, :])
                if tB is not None:
                    hidden1(tB, 3)
                    hidden2(tB, 3)
                if tA is not None:
                    drain(TA[0], tA, "pT2", pT[:, 2, :])
                    drain(TA[1], tA, "pT3", pT[:, 3, :])
                if tB is not None:
                    hidden1(tB, 4)
                    hidden2(tB, 4)
                if tC is not None:
                    wait(act, "x3n", tC)
                    if not (isinstance(tC, int) and tC < 2):
                        act.wait_ge(rows_sent, 16 * 2 * NT * (tC - 1))
                    s.activation(rows[1][par][:, :, 0:D], rows[0][par][:, :, 0:D], ACT.Copy).then_inc(
                        ready("row1_features"), 1)
                if tB is not None:
                    hidden1(tB, 5)
                if tC is not None:
                    drain(HC, tC, "x3T", x3T[:], ACT.Identity, bias=beta[:], scale=gamma[:])
                if tB is not None:
                    hidden2(tB, 5)

            iterations(act, step)

            def tile_slot(s_, u, r):
                i = tile_at(s_, 3)
                if i is not None:
                    q = (u - 3) % UNROLL
                    wait(act, "tile_yb", i)
                    if not (isinstance(i, int) and i < UNROLL):
                        act.wait_ge(result_sent[q], 32 * turn_at(u, r, 3))
                    for b in range(2):
                        last = s.activation(yw[q][:, b, :], yb[(u - 3) % 2][:, b * D:(b + 1) * D], ACT.Copy,
                                            scale=tile_rows[q][:, b, WEIGHT:WEIGHT + 1])
                    last.then_inc(ready("tile_yw"), 1)
                i = tile_at(s_, 1)
                if i is not None:
                    q = (u - 1) % 2
                    column = act.value_load(column_of[0:1, bass.ds(i, 1)], min_val=0,
                                            max_val=2 * (E1 - 1))
                    wait(act, "tile_h", i)
                    if not (isinstance(i, int) and i < 2):
                        wait(act, "tile_y", i - 2)
                    apart(act)
                    for c in range(2):
                        last = s.activation(hg[q][:, c, :], HX[q][:, c * TILE:(c + 1) * TILE], ACT.Gelu,
                                            bias=fb1[:, bass.ds(column + c, 1)])
                    last.then_inc(ready("tile_hg"), 1)

            act.wait_ge(ready("table"), 1)
            slots(act, tile_slot)

        @block.tensor
        def _(pe):
            m = nc.tensor

            pe.wait_ge(ready("ident"), 1)
            pe.wait_ge(ready("pool_const"), POOL_CONSTANTS)
            pe.wait_ge(attention_loaded, ATTENTION_WEIGHTS)
            m.transpose(HC.tensor[:, 0:D], gW[:], ident[:])
            m.matmul(HC.tensor[:, D:D + 2], gW[:], wa_col[:], start=True, stop=True).then_inc(
                ready("setup1"), 1)
            pe.wait_ge(ready("bwa"), 1)
            m.matmul(AJ.tensor[:, 0:2], ones[:], bwa[:], start=True, stop=True).then_inc(
                ready("setup2"), 1)
            pe.wait_ge(ready("setup_done"), 1)

            def transposes(bk, t, use, blocks):
                bk.wait_free(pe, t, use)
                for j, src in enumerate(blocks):
                    last = m.transpose(bk.tensor[:, j * P:(j + 1) * P], src, ident[:])
                last.then_inc(bk.filled, 1)

            def product(bk, t, use, lhsT, rhs):
                bk.wait_free(pe, t, use)
                m.matmul(bk.tensor[0:lhsT.shape[1], :], lhsT, rhs, start=True, stop=True).then_inc(
                    bk.filled, 1)

            def layer1(t, e):
                product(HB[0], t, f"h1_{e}", ew[0][:, e, :], x1nT[:])

            def layer2(t, e):
                HB[0].wait_read(pe, t, f"h1_{e}")
                product(HB[1], t, f"h2_{e}", ew[1][:, e, :], h1[e % 2][:])

            def layer3(t, e):
                OB.wait_free(pe, t, f"e{e}")
                HB[1].wait_read(pe, t, f"h2_{e}")
                for j in range(NT):
                    last = m.matmul(OB.tensor[:, j * P:(j + 1) * P], h2[e % 2][:, j * P:(j + 1) * P],
                                    ew[2][:, e, :], start=True, stop=True)
                last.then_inc(OB.filled, 1)

            def probT(t, k):
                if k == 0:
                    wait(pe, "edge_exp", t, NT, NT - 1)
                transposes(TA[k % 2], t, f"pT{k}", [att[:, j, k * P:(k + 1) * P] for j in range(NT)])

            def adj_transposed(t, k, par):
                transposes(HB[k % 2], t, f"adjT{k}", [adj[par][:, j, k * P:(k + 1) * P] for j in range(NT)])

            def step(tN, tA, tB, tC, tD, par):
                if isinstance(tB, int) and tB == 0:
                    pe.wait_ge(weights_loaded, WEIGHTS)
                if tB is not None:
                    adj_transposed(tB, 0, 1 - par)
                    adj_transposed(tB, 1, 1 - par)
                if tA is not None:
                    wait(pe, "xn", tA)
                    transposes(TA[1], tA, "xT", [xn[:, j, :] for j in range(NT)])
                if tB is not None:
                    adj_transposed(tB, 2, 1 - par)
                    wait(pe, "x1n", tB)
                    transposes(TA[0], tB, "x1T", [x1n[:, j, :] for j in range(NT)])
                if tA is not None:
                    TA[1].wait_read(pe, tA, "xT")
                    wait_before(pe, "relu", tA, NT)
                    if tD is not None and not (isinstance(tD, int) and tD == 0):
                        RK.wait_read(pe, tD - 1, "ranks")
                    if tB is not None and not (isinstance(tB, int) and tB == 0):
                        GT.wait_read(pe, tB - 1, "b3")
                    m.matmul(AJ.tensor[:], uj_bc[:], xnT[:], start=True, stop=True).then_inc(
                        AJ.filled, 1)
                    for h, (bk, use) in enumerate(z_banks):
                        bk.wait_free(pe, tA, use)
                        for j in range(2):
                            last = m.matmul(bk.tensor[:, j * (D + 1):(j + 1) * (D + 1)],
                                            xnT[:, (2 * h + j) * P:(2 * h + j + 1) * P], gWTu[:],
                                            start=True, stop=True)
                        last.then_inc(bk.filled, 1)
                if tB is not None:
                    TA[0].wait_read(pe, tB, "x1T")
                    product(HB[0], tB, "route_h", rw1[:], x1nT[:])
                    adj_transposed(tB, 3, 1 - par)
                    layer1(tB, 0)
                    HB[0].wait_read(pe, tB, "route_h")
                    HB[1].wait_free(pe, tB, "logits")
                    for j in range(NT):
                        last = m.matmul(HB[1].tensor[:, j * PADW:(j + 1) * PADW], rh[:, j * P:(j + 1) * P],
                                        rw2[:], start=True, stop=True)
                    last.then_inc(HB[1].filled, 1)
                if tC is not None:
                    HC.wait_free(pe, tC, "agg")
                    wait(pe, "diagonal", tC)
                    wait(pe, "x2n", tC)
                    for k in range(NT):
                        last = m.matmul(HC.tensor[:], x2n[par][:, k, :], adjT[par][:, k, :],
                                        start=(k == 0), stop=(k == NT - 1))
                    last.then_inc(HC.filled, 1)
                if tD is not None:
                    RK.wait_free(pe, tD, "ranks")
                    if tA is not None:
                        wait(pe, "relu", tA, NT, NT - 1)
                    else:
                        wait(pe, "relu", G - 1, NT, NT - 1)
                    wait(pe, "earlier", tD)
                    m.matmul(RK.tensor[:, 0:8 * (NT + 1)], ones_b[:],
                             earlier[:].rearrange("p j e -> p (j e)"), start=True, stop=False)
                    m.matmul(RK.tensor[:, 0:8 * NT], tri[:], chosen_b[:].rearrange("p j e -> p (j e)"),
                             start=False, stop=True).then_inc(RK.filled, 1)
                if tB is not None:
                    layer2(tB, 0)
                if tC is not None:
                    HC.wait_read(pe, tC, "agg")
                    product(HC, tC, "m0", mw1[:, 0:P], hT[:])
                if tB is not None:
                    layer1(tB, 1)
                if tC is not None:
                    product(HC, tC, "m1", mw1[:, P:DH], hT[:])
                if tB is not None:
                    layer3(tB, 0)
                    layer2(tB, 1)
                if tC is not None:
                    HC.wait_free(pe, tC, "out")
                    for j in range(NT):
                        for c in range(2):
                            last = m.matmul(HC.tensor[:, j * P:(j + 1) * P],
                                            m1[:, c, j * P:(j + 1) * P], mw2[:, c, :],
                                            start=(c == 0), stop=(c == 1))
                    last.then_inc(HC.filled, 1)
                if tB is not None:
                    layer1(tB, 2)
                    if tD is not None:
                        RK.wait_read(pe, tD, "ranks")
                    elif tA is not None:
                        wait(pe, "relu", tA, NT, NT - 1)
                    wait(pe, "gate", tB)
                    for j in range(NT):
                        last = m.transpose(GT.tensor[0:8, j * P:(j + 1) * P], gate[:, j, :], ident[:])
                    last.then_inc(GT.filled, 1)
                    layer3(tB, 1)
                    layer2(tB, 2)
                if tA is not None:
                    probT(tA, 0)
                    probT(tA, 1)
                if tB is not None:
                    layer1(tB, 3)
                    GT.wait_free(pe, tB, "b3")
                    for j in range(NT):
                        last = m.matmul(GT.tensor[:, j * P:(j + 1) * P], gateT[0:E0, j * P:(j + 1) * P],
                                        eb3[:], start=True, stop=True)
                    last.then_inc(GT.filled, 1)
                    layer2(tB, 3)
                    layer3(tB, 2)
                if tA is not None:
                    probT(tA, 2)
                    probT(tA, 3)
                if tB is not None:
                    layer1(tB, 4)
                    layer3(tB, 3)
                    layer2(tB, 4)
                if tA is not None:
                    ZB.wait_read(pe, tA, "z0")
                    TA[1].wait_read(pe, tA, "z1")
                    ZB.wait_free(pe, tA, "o")
                    for k in (2, 3):
                        TA[k % 2].wait_read(pe, tA, f"pT{k}")
                    for j in range(NT):
                        for k in range(NT):
                            last = m.matmul(ZB.tensor[:, j * P:(j + 1) * P], pT[:, k, j * P:(j + 1) * P],
                                            z[:, k, :], start=(k == 0), stop=(k == NT - 1))
                    last.then_inc(ZB.filled, 1)
                if tB is not None:
                    layer1(tB, 5)
                    layer3(tB, 4)
                if tC is not None:
                    wait(pe, "x3n", tC)
                    transposes(HC, tC, "x3T", [rows[0][par][:, j, 0:D] for j in range(NT)])
                if tB is not None:
                    layer2(tB, 5)
                if tC is not None:
                    HC.wait_read(pe, tC, "x3T")
                    for j in range(NT):
                        last = m.matmul(HC.tensor[:, j * PADW:(j + 1) * PADW], x3T[:, j * P:(j + 1) * P],
                                        wr[:], start=True, stop=True)
                    last.then_inc(HC.filled, 1)
                if tB is not None:
                    layer3(tB, 5)

            iterations(pe, step)

            def tile_slot(s, u, r):
                i = tile_at(s, 0)
                if i is not None:
                    pe.wait_ge(tile_loaded[u], 16 * (r + 1))
                    if not (isinstance(i, int) and i < 2):
                        wait(pe, "tile_xg", i - 2)
                    for b in range(2):
                        last = m.transpose(XT[u % 2][:, b * P:(b + 1) * P], tile_rows[u][:, b, 0:D],
                                           ident[:])
                    last.then_inc(ready("tile_xT"), 1)
                i = tile_at(s, 1)
                if i is not None:
                    q = (u - 1) % 2
                    wait(pe, "tile_xg", i)
                    if not (isinstance(i, int) and i < 2):
                        wait(pe, "tile_hg", i - 2)
                    for c in range(2):
                        last = m.matmul(HX[q][:, c * TILE:(c + 1) * TILE],
                                        w1[q][:, c * P:(c + 1) * P], xg[q],
                                        start=True, stop=True)
                    last.then_inc(ready("tile_h"), 1)
                i = tile_at(s, 2)
                if i is not None:
                    q = (u - 2) % 2
                    column = pe.value_load(column_of[0:1, bass.ds(i, 1)], min_val=0,
                                           max_val=2 * (E1 - 1))
                    wait(pe, "tile_hg", i)
                    if not (isinstance(i, int) and i < 2):
                        wait(pe, "tile_yb", i - 2)
                    for b in range(2):
                        for c in range(2):
                            last = m.matmul(YX[q][:, b * D:(b + 1) * D], hg[q][:, c, b * P:(b + 1) * P],
                                            fw2[:, bass.ds(column * P + c * D, D)],
                                            start=(c == 0), stop=(c == 1))
                    last.then_inc(ready("tile_y"), 1)

            pe.wait_ge(ready("table"), 1)
            RK.wait_read(pe, G - 1, "ranks")
            slots(pe, tile_slot)

        @block.vector
        def _(dve):
            v = nc.vector

            dve.wait_ge(attention_loaded, ATTENTION_WEIGHTS)
            dve.wait_ge(ready("ident"), 1)
            dve.wait_ge(ready("pool_const"), POOL_CONSTANTS)
            v.tensor_scalar(bwa[:], wa_col[:], bW_col[:], None, ALU.mult).then_inc(ready("bwa"), 1)
            v.tensor_scalar(eps_ident[:], ident[:], eps_bc[:], None, ALU.mult).then_inc(
                ready("eps_ident0"), 1)
            dve.wait_ge(ready("eps_ident0"), 1)
            v.tensor_tensor(eps_ident[:], eps_ident[:], ident[:], ALU.add)
            dve.wait_ge(ready("setup1"), 1)
            v.tensor_copy(gWTu[:], HC.tensor[:, 0:D + 1])
            v.tensor_copy(u_col[:], HC.tensor[:, D:D + 2]).then_inc(ready("u_col"), 1)
            dve.wait_ge(ready("u_col"), 1)
            v.tensor_scalar(uj_bc[:], ones[:], u_col[:, 1:2], None, ALU.mult)
            dve.wait_ge(ready("setup2"), 1)
            v.tensor_tensor(c_pair[:], AJ.tensor[:, 0:2], ba_bc[:], ALU.add).then_inc(ready("c_pair"), 1)
            dve.wait_ge(ready("c_pair"), 1)
            v.tensor_tensor(c_sum[:], c_pair[:, 0:1], c_pair[:, 1:2], ALU.add).then_inc(ready("c_sum"), 1)
            dve.wait_ge(ready("c_sum"), 1)
            v.tensor_scalar(c_relu[:], c_sum[:], 1.0 - SLOPE, None, ALU.mult)
            v.tensor_scalar(c_sink[:], c_sum[:], -SLOPE, SINK, ALU.mult, ALU.add).then_inc(
                ready("setup_done"), 1)
            dve.wait_ge(ready("setup_done"), 1)

            def x3_of(g):
                return x3[:, g, :, :] if isinstance(g, int) else x3[:, bass.ds(g, 1), :, :].squeeze(1)

            v.memset(earlier_f[:, 0, :], 0.0)

            def stats(s, t, x):
                for j in range(NT):
                    last = v.bn_stats(bn[s][:, j, :], x[:, j, :])
                last.then_inc(ready(f"bn_{s}"), 1)
                wait(dve, f"bn_{s}", t)
                apart(dve)
                for j in range(NT):
                    last = v.bn_aggr(mv[s][:, j, :], bn[s][:, j, :])
                last.then_inc(ready(f"stats_{s}"), 1)

            def normalise(s, t, x, dst, name):
                wait(dve, f"rstd_{s}", t)
                for j in range(NT):
                    last = v.tensor_scalar(dst[:, j, 0:D], x[:, j, :], mv[s][:, j, 0:1],
                                           rstd[s][:, j:j + 1], ALU.subtract, ALU.mult)
                last.then_inc(ready(name), 1)

            def choose_two(r, t, values):
                apart(dve)
                for j in range(NT):
                    last = v.max(best[r][:, j, :], values[:, j, :])
                last.then_inc(ready(f"best_{r}"), 1)
                wait(dve, f"best_{r}", t)
                v.tensor_tensor(wgap[r][:], best[r][:, :, 1], best[r][:, :, 0], ALU.subtract).then_inc(
                    ready(f"wgap_{r}"), 1)
                for j in range(NT):
                    last = v.max_index(best_i[r][:, j, :], best[r][:, j, :], values[:, j, :])
                last.then_inc(ready(f"best_i_{r}"), 1)
                wait(dve, f"best_i_{r}", t)
                v.tensor_copy(best_f[r][:], best_i[r][:, :, 0:2].rearrange("p j k -> p k j")).then_inc(
                    ready(f"best_f_{r}"), 1)
                wait(dve, f"best_f_{r}", t)
                for c in range(2):
                    last = v.tensor_tensor(hot[r][:, c, :, :], bc(iota8[:], 1, NT),
                                           bc(best_f[r][:, c, :], 2, 8), ALU.is_equal)
                last.then_inc(ready(f"hot_{r}"), 1)

            def weigh_two(r, t):
                wait(dve, f"wexp_{r}", t)
                v.tensor_scalar(wden[r][:], wexp[r][:], 1.0, None, ALU.add).then_inc(
                    ready(f"wden_{r}"), 1)
                wait(dve, f"wden_{r}", t)
                v.reciprocal(w01[r][:, 0, :], wden[r][:]).then_inc(ready(f"w0_{r}"), 1)
                wait(dve, f"w0_{r}", t)
                v.tensor_tensor(w01[r][:, 1, :], wexp[r][:], w01[r][:, 0, :], ALU.mult).then_inc(
                    ready(f"w1_{r}"), 1)
                wait(dve, f"w1_{r}", t)
                wait(dve, f"hot_{r}", t)

            def add_expert(t, e, pb):
                OB.wait_full(dve, t, f"e{e}")
                if e == 0:
                    wait(dve, "gate", t)
                elif e == 3:
                    GT.wait_read(dve, t, "b3")
                else:
                    OB.wait_read(dve, t, OB.uses[OB.uses.index(f"e{e}") - 1])
                for j in range(NT):
                    last = v.scalar_tensor_tensor(
                        out=x2[pb][:, j, :], in0=OB.tensor[:, j * P:(j + 1) * P],
                        scalar=gate[:, j, e:e + 1], in1=(x1 if e == 0 else x2)[pb][:, j, :],
                        op0=ALU.mult, op1=ALU.add)
                last.then_inc(OB.drained, 1)

            def count_earlier(t, j):
                if j > 0:
                    wait(dve, "earlier_f", t, NT, j - 1)
                v.tensor_tensor(earlier_f[:, j + 1, :], earlier_f[:, j, :], chosen[:, j, :],
                                ALU.add).then_inc(ready("earlier_f"), 1)

            def z_and_ai(bk):
                return bk.tensor[:, 0:2 * (D + 1)].rearrange("p (j d) -> p j d", d=D + 1)

            def edge_max(t, j):
                wait(dve, "relu", t, NT, j)
                wait(dve, "pen_aj", t, NT, j)
                apart(dve)
                return v.tensor_tensor_reduce(att[:, j, :], att[:, j, :], pen[:, j, :], 1.0, MASKED,
                                              ALU.add, ALU.max, row_max[:, j:j + 1])

            def step(tN, tA, tB, tC, tD, par):
                if isinstance(tB, int) and tB == 0:
                    dve.wait_ge(weights_loaded, WEIGHTS)
                pb = 1 - par
                if tA is not None:
                    for h, (bk, use) in enumerate(z_banks):
                        bk.wait_full(dve, tA, use)
                        last = v.tensor_scalar(relu_bias[:, 2 * h:2 * h + 2], z_and_ai(bk)[:, :, D],
                                               1.0 - SLOPE, c_relu[:], ALU.mult, ALU.add)
                    last.then_inc(ready("relu_bias"), 1)
                    for h, (bk, use) in enumerate(z_banks):
                        v.tensor_scalar(sink[:, 2 * h:2 * h + 2], z_and_ai(bk)[:, :, D], -SLOPE,
                                        c_sink[:], ALU.mult, ALU.add)
                if tC is not None:
                    normalise("C", tC, x2[par], x2n[par], "x2n")
                if tD is not None:
                    HC.wait_read(dve, tD, "logits1")
                    choose_two("D", tD, logits1)
                if tA is not None:
                    for h, (bk, use) in enumerate(z_banks):
                        v.tensor_tensor(z[:, 2 * h:2 * h + 2, :], z_and_ai(bk)[:, :, 0:D],
                                        bc(bW_bc[:], 1, 2), ALU.add).then_inc(bk.drained, 1)
                if tD is not None:
                    wait(dve, "hot_D", tD)
                    v.tensor_tensor(chosen[:], hot["D"][:, 0, :, :], hot["D"][:, 1, :, :],
                                    ALU.add).then_inc(ready("chosen"), 1)
                if tB is not None:
                    HB[1].wait_full(dve, tB, "logits")
                    v.tensor_tensor(lg[:], HB[1].tensor[:, 0:NT * PADW].rearrange(
                        "p (j e) -> p j e", e=PADW)[:, :, 0:E0], bc(rb2_bc[:], 1, NT), ALU.add).then_inc(
                        HB[1].drained, 1)
                if tD is not None:
                    wait(dve, "chosen", tD)
                    v.tensor_copy(chosen_b[:], chosen[:])
                    count_earlier(tD, 0)
                if tB is not None:
                    HB[1].wait_read(dve, tB, "logits")
                    v.tensor_reduce(lg_max[:], lg[:], AX.X, ALU.max).then_inc(ready("lg_max"), 1)
                if tD is not None:
                    count_earlier(tD, 1)
                if tB is not None:
                    wait(dve, "lg_max", tB)
                    v.tensor_tensor(lg[:], lg[:], bc(lg_max[:], 2, E0), ALU.subtract).then_inc(
                        ready("lg_centred"), 1)
                if tD is not None:
                    count_earlier(tD, 2)
                if tA is not None:
                    edge_max(tA, 0)
                if tD is not None:
                    count_earlier(tD, 3)
                    wait(dve, "earlier_f", tD, NT, NT - 1)
                    v.tensor_copy(earlier[:], earlier_f[:]).then_inc(ready("earlier"), 1)
                if tB is not None:
                    wait(dve, "lg_exp", tB)
                    v.tensor_reduce(lg_sum[:], prob[:, :, 0:E0], AX.X, ALU.add).then_inc(ready("lg_sum"), 1)
                    wait(dve, "lg_sum", tB)
                    v.reciprocal(lg_rsum[:], lg_sum[:]).then_inc(ready("lg_rsum"), 1)
                if tA is not None:
                    edge_max(tA, 1)
                if tB is not None:
                    wait(dve, "lg_rsum", tB)
                    v.tensor_tensor(prob[:, :, 0:E0], prob[:, :, 0:E0], bc(lg_rsum[:], 2, E0),
                                    ALU.mult).then_inc(ready("prob"), 1)
                if tD is not None:
                    weigh_two("D", tD)
                if tB is not None:
                    wait(dve, "prob", tB)
                    choose_two("B", tB, prob)
                if tA is not None:
                    edge_max(tA, 2)
                if tD is not None:
                    wait(dve, "row1_features", tD)
                    for k in range(2):
                        v.tensor_copy(rows[k][pb][:, :, PLACE].bitcast(U32), place[:, k, :])
                        last = v.tensor_copy(rows[k][pb][:, :, WEIGHT], w01["D"][:, k, :])
                    last.then_inc(ready("rows_ready"), 1)
                if tB is not None:
                    weigh_two("B", tB)
                    for c in range(2):
                        last = v.tensor_tensor(hotw[:, c, :, :], hot["B"][:, c, :, :],
                                               bc(w01["B"][:, c, :], 2, 8), ALU.mult)
                    last.then_inc(ready("hotw"), 1)
                if tA is not None:
                    edge_max(tA, 3).then_inc(ready("row_max"), 1)
                if tB is not None:
                    wait(dve, "hotw", tB)
                    v.tensor_tensor(gate[:], hotw[:, 0, :, :], hotw[:, 1, :, :], ALU.add).then_inc(
                        ready("gate"), 1)
                if tA is not None:
                    wait(dve, "row_max", tA)
                    v.tensor_tensor(top[:], row_max[:], sink[:], ALU.max).then_inc(ready("top"), 1)
                if tD is not None:
                    wait(dve, "rows_ready", tD)
                    v.tensor_scalar(place[:], place[:], float(2 * N), None, ALU.add).then_inc(
                        ready("place"), 1)
                if tA is not None:
                    wait(dve, "top", tA)
                    v.tensor_scalar(neg_max[:], top[:], -1.0, None, ALU.mult).then_inc(ready("neg_max"), 1)
                if tD is not None:
                    RK.wait_full(dve, tD, "ranks")
                    v.tensor_tensor(slot_of[:], RK.tensor[:, 0:8 * NT].rearrange("p (j e) -> p j e", e=8),
                                    bc(base[:], 1, NT), ALU.add).then_inc(ready("slot_of"), 1)
                if tA is not None:
                    wait(dve, "neg_max", tA)
                    v.tensor_tensor(sink_arg[:], sink[:], neg_max[:], ALU.add).then_inc(
                        ready("sink_arg"), 1)
                if tD is not None:
                    wait(dve, "slot_of", tD)
                    v.tensor_tensor(base[:], RK.tensor[:, 8 * NT:8 * (NT + 1)], base[:], ALU.add).then_inc(
                        RK.drained, 1)
                    for k in range(2):
                        last = v.tensor_tensor(slot_hot[:, k, :, :], slot_of[:], hot["D"][:, k, :, :],
                                               ALU.mult)
                    last.then_inc(ready("slot_hot"), 1)
                    wait(dve, "slot_hot", tD)
                    v.tensor_reduce(slot_f[:], slot_hot[:], AX.X, ALU.add).then_inc(ready("slot_f"), 1)
                    wait(dve, "slot_f", tD)
                    if not (isinstance(tD, int) and tD == 0):
                        dve.wait_ge(rows_sent, 16 * 2 * NT * tD)
                    v.tensor_copy(slot[:], slot_f[:]).then_inc(ready("slot"), 1)
                if tB is not None:
                    add_expert(tB, 0, pb)
                if tC is not None:
                    HC.wait_full(dve, tC, "out")
                    wait(dve, "x2b", tC)
                    v.tensor_tensor(x3_of(tC), HC.tensor[:].rearrange("p (j d) -> p j d", d=D), x2b[:],
                                    ALU.add).then_inc(HC.drained, 1)
                    HC.wait_read(dve, tC, "out")
                    apart(dve)
                    stats("D", tC, x3_of(tC))
                if tB is not None:
                    add_expert(tB, 1, pb)
                if tN is not None:
                    dve.wait_ge(x0_loaded[pb], 16 * (tN // 2 + 1) if isinstance(tN, int)
                                else 8 * (tN - pb) + 16)
                    stats("A", tN, x0[pb])
                if tC is not None:
                    normalise("D", tC, x3_of(tC), x3n, "x3_outer")
                    wait(dve, "x3_outer", tC)
                    stats("E", tC, x3n)
                if tB is not None:
                    add_expert(tB, 2, pb)
                if tC is not None:
                    if not (isinstance(tC, int) and tC < 2):
                        dve.wait_ge(rows_sent, 16 * 2 * NT * (tC - 1))
                    normalise("E", tC, x3n, rows[0][par], "x3n")
                if tN is not None:
                    dve.wait_ge(adj_loaded[pb], 16 * (tN // 2 + 1) if isinstance(tN, int)
                                else 8 * (tN - pb) + 16)
                    v.tensor_scalar(pen[:], adj[pb][:], 0.0, MASKED, ALU.is_le, ALU.mult).then_inc(
                        ready("pen"), 1)
                    if tA is not None:
                        TA[1].wait_full(dve, tA, "xT")
                    normalise("A", tN, x0[pb], xn, "xn")
                if tA is not None:
                    wait(dve, "edge_exp", tA, NT, NT - 1)
                    wait(dve, "sink_exp", tA)
                    v.tensor_tensor(den[:], row_sum[:], sink_exp[:], ALU.add).then_inc(ready("den"), 1)
                    wait(dve, "den", tA)
                    v.reciprocal(rden[:], den[:]).then_inc(ready("rden"), 1)
                if tB is not None:
                    GT.wait_full(dve, tB, "b3")
                    OB.wait_read(dve, tB, "e2")
                    v.tensor_tensor(x2[pb][:], GT.tensor[:].rearrange("p (j d) -> p j d", d=D),
                                    x2[pb][:], ALU.add).then_inc(GT.drained, 1)
                    add_expert(tB, 3, pb)
                if tA is not None:
                    ZB.wait_full(dve, tA, "o")
                    wait(dve, "rden", tA)
                    for j in range(NT):
                        last = v.scalar_tensor_tensor(
                            out=x1[par][:, j, :], in0=ZB.tensor[:, j * P:(j + 1) * P],
                            scalar=rden[:, j:j + 1], in1=x0[par][:, j, :], op0=ALU.mult, op1=ALU.add)
                    last.then_inc(ZB.drained, 1)
                    ZB.wait_read(dve, tA, "o")
                    stats("B", tA, x1[par])
                if tB is not None:
                    add_expert(tB, 4, pb)
                if tC is not None:
                    HC.wait_full(dve, tC, "logits1")
                    v.tensor_tensor(logits1[:], HC.tensor[:, 0:NT * PADW].rearrange(
                        "p (j e) -> p j e", e=PADW)[:, :, 0:E1], bc(br_bc[:], 1, NT), ALU.add).then_inc(
                        HC.drained, 1)
                if tA is not None:
                    normalise("B", tA, x1[par], x1n, "x1n")
                if tB is not None:
                    add_expert(tB, 5, pb)
                    OB.wait_read(dve, tB, "e5")
                    stats("C", tB, x2[pb])

            iterations(dve, step)

            def then(step, instruction):
                instruction.then_inc(ready("table_step"), 1)
                dve.wait_ge(ready("table_step"), step)

            RK.wait_read(dve, G - 1, "ranks")
            v.tensor_copy(filled_to[:], base[0:1, :]).then_inc(ready("filled_to"), 1)
            then(1, v.tensor_tensor(count[:], base[0:1, :], iota_region[0:1, :], ALU.subtract))
            then(2, v.tensor_scalar(count[:], count[:], float(TILE - 1), None, ALU.add))
            then(3, v.tensor_copy(count_i[:], count[:]))
            then(4, v.tensor_scalar(tiles_i[:], count_i[:], TILE.bit_length() - 1, None,
                                            ALU.arith_shift_right))
            then(5, v.tensor_copy(tiles[:], tiles_i[:]))
            then(6, v.tensor_copy(ends[0][:], tiles[:]))
            for n, by in enumerate((1, 2, 4)):
                v.tensor_copy(ends[n + 1][:, 0:by], ends[n][:, 0:by])
                then(7 + n, v.tensor_tensor(ends[n + 1][:, by:E1], ends[n][:, by:E1],
                                                     ends[n][:, 0:E1 - by], ALU.add))
            then(10, v.tensor_tensor(passed[:], bc(iota_tile[:], 2, E1), bc(ends[3][:], 1, TILES),
                                           ALU.is_ge))
            then(11, v.tensor_tensor(passed_tiles[:], passed[:], bc(tiles[:], 1, TILES), ALU.mult))
            then(12, v.tensor_reduce(expert_f[:], passed[:], AX.X, ALU.add))
            then(13, v.tensor_reduce(first[:], passed_tiles[:], AX.X, ALU.add))
            then(14, v.tensor_tensor(inside[:], iota_tile[:], first[:], ALU.subtract))
            then(15, v.tensor_scalar(inside[:], inside[:], float(TILE), None, ALU.mult))
            then(16, v.scalar_tensor_tensor(out=row0_f[:], in0=expert_f[:], scalar=float(CAP),
                                                in1=inside[:], op0=ALU.mult, op1=ALU.add))
            then(17, v.tensor_scalar(column_f[:], expert_f[:], float(E1 - 1), 2.0, ALU.min, ALU.mult))
            v.tensor_copy(row0_of[:], row0_f[:])
            v.tensor_copy(column_of[:], column_f[:]).then_inc(ready("table"), 1)
            dve.wait_ge(ready("table"), 1)

            def tile_slot(s, u, r):
                i = tile_at(s, 0)
                if i is not None:
                    column = dve.value_load(column_of[0:1, bass.ds(i, 1)], min_val=0,
                                            max_val=2 * (E1 - 1))
                    if not (isinstance(i, int) and i < 2):
                        wait(dve, "tile_h", i - 2)
                        apart(dve)
                    v.tensor_copy(w1[u % 2], fw1[:, bass.ds(column * P, HE)])
                    wait(dve, "tile_xT", i)
                    v.tensor_scalar(xg[u % 2], XT[u % 2][:, 0:TILE], gamma[:], beta[:], ALU.mult,
                                    ALU.add).then_inc(ready("tile_xg"), 1)
                i = tile_at(s, 2)
                if i is not None:
                    q = (u - 2) % 2
                    column = dve.value_load(column_of[0:1, bass.ds(i, 1)], min_val=0,
                                            max_val=2 * (E1 - 1))
                    wait(dve, "tile_y", i)
                    if not (isinstance(i, int) and i < 2):
                        wait(dve, "tile_yw", i - 2)
                    v.tensor_tensor(yb[q].rearrange("p (b d) -> p b d", b=2),
                                    YX[q][:, 0:2 * D].rearrange("p (b d) -> p b d", b=2),
                                    bc(fb2_bc[:, bass.ds(column * (D // 2), D)], 1, 2),
                                    ALU.add).then_inc(ready("tile_yb"), 1)

            slots(dve, tile_slot)

            def add_pair(turn, n):
                g = DEEP * turn + n
                dve.wait_ge(pair_loaded[n], 16 * (turn + 1))
                if not (isinstance(turn, int) and turn == 0):
                    dve.wait_ge(out_stored[n], 16 * turn)
                v.tensor_tensor(fin[n], pair[n][:, :, 0:D], x3_of(g), ALU.add).then_inc(
                    ready("fin_part"), 1)
                wait(dve, "fin_part", g)
                v.tensor_tensor(fin[n], fin[n], pair[n][:, :, D:2 * D], ALU.add).then_inc(
                    ready("fin"), 1)

            for n in range(DEEP):
                add_pair(0, n)
            with dve.Fori(1, G // DEEP) as turn:
                for n in range(DEEP):
                    add_pair(turn, n)


_INS = ['x', 'adj', 'L0_gnn_W', 'L0_gnn_bW', 'L0_gnn_wai', 'L0_gnn_bai', 'L0_gnn_waj', 'L0_gnn_baj',
        'L0_ffn_router_w1', 'L0_ffn_router_b1', 'L0_ffn_router_w2', 'L0_ffn_router_b2',
        'L0_ffn_expert_w1', 'L0_ffn_expert_b1', 'L0_ffn_expert_w2', 'L0_ffn_expert_b2',
        'L0_ffn_expert_w3', 'L0_ffn_expert_b3', 'L1_gnn_eps', 'L1_gnn_W1', 'L1_gnn_b1', 'L1_gnn_W2',
        'L1_gnn_b2', 'L1_ffn_gamma', 'L1_ffn_beta', 'L1_ffn_Wr', 'L1_ffn_br', 'L1_ffn_W1',
        'L1_ffn_b1', 'L1_ffn_W2', 'L1_ffn_b2']


def kernel(**inputs):
    import numpy as _np
    import concourse.bacc as _bacc
    from concourse import mybir as _mybir
    from concourse.bass_utils import run_bass_kernel_spmd as _run

    nc = _bacc.Bacc("TRN2", target_bir_lowering=False, num_devices=1)
    arrays, args = {}, {}
    for name in _INS:
        a = _np.ascontiguousarray(inputs[name])
        arrays[f"in_{name}"] = a
        args[name] = nc.dram_tensor(f"in_{name}", a.shape, _mybir.dt.from_np(a.dtype),
                                    kind="ExternalInput").ap()
    out = nc.dram_tensor("result", (G, N, D), _mybir.dt.float32, kind="ExternalOutput").ap()
    build(nc, args, out)
    r = _run(nc, [arrays], core_ids=[0])
    return r.results[0]["result"]
```
